# Optimizing a Trainium2 kernel written in Bass

```python
import numpy as np
import jax
import jax.numpy as jnp

def _softmax(x, axis=-1):
    return jax.nn.softmax(x, axis=axis)

def _gelu(x):
    return jax.nn.gelu(x, approximate=True)

def _silu(x):
    return jax.nn.silu(x)

def _sigmoid(x):
    return jax.nn.sigmoid(x)

def _layernorm(x, axis=-1, eps=1e-05):
    m = jnp.mean(x, axis=axis, keepdims=True)
    v = jnp.var(x, axis=axis, keepdims=True)
    return (x - m) / jnp.sqrt(v + eps)

def _scatter_add(tgt, idx, src, axis=0):
    return tgt.at[idx].add(src)

def _segment_sum(src, seg, n):
    return jax.ops.segment_sum(src, seg, n)
kernel_name = 'mk_gnn_preln_d4_gnn_r64_8ecb8f'

def setup_inputs(seed: int=0):
    np.random.seed(seed)
    _w = jnp.asarray

    def _rec_inputs():
        import jax
        import jax.numpy as jnp
        _gk = jax.random.key(seed)
        x = -0.0001006 + 1 * jax.random.normal(jax.random.fold_in(_gk, 1), (100000, 96), jnp.float32)
        src = jax.random.randint(jax.random.fold_in(_gk, 2), (25000,), 0, 100000, jnp.int32)
        dst = jax.random.randint(jax.random.fold_in(_gk, 3), (25000,), 0, 100000, jnp.int32)
        _o = jnp.argsort(dst, stable=True)
        src = src[_o]
        dst = dst[_o]
        edge_attr_17 = jax.random.uniform(jax.random.fold_in(_gk, 11), (25000, 17), jnp.float32, 0.0, 1)
        edge_attr_4 = 0.000714719 + 1.00021 * jax.random.normal(jax.random.fold_in(_gk, 12), (25000, 4), jnp.float32)
        edge_attr_96 = 5.93493e-05 + 1.00006 * jax.random.normal(jax.random.fold_in(_gk, 13), (25000, 96), jnp.float32)
        return (x, src, dst, edge_attr_17, edge_attr_4, edge_attr_96)
    x, src, dst, edge_attr_17, edge_attr_4, edge_attr_96 = _rec_inputs()

    def _L0_gnn_setup():
        import jax, jax.numpy as jnp
        import numpy as np
        N_NODES = 50000
        N_EDGES = 12500
        D_FEAT = 96
        key = jax.random.key(seed)
        kx, ke = jax.random.split(key)
        x = jax.random.normal(kx, (N_NODES, D_FEAT), dtype=jnp.float32)
        edge_index = jax.random.randint(ke, (2, N_EDGES), 0, N_NODES, dtype=jnp.int64)
        return {'x': x, 'edge_index': edge_index, 'num_nodes': N_NODES}
    _L0_gnn_all = _L0_gnn_setup()
    _L0_gnn_in = {k: v for k, v in _L0_gnn_all.items() if k in ()}
    del _L0_gnn_all

    def _L1_gnn_setup():
        import jax, jax.numpy as jnp
        import numpy as np
        N = 50000
        E = 12500
        D = 96
        ED = 17
        key = jax.random.key(seed)
        ks = jax.random.split(key, 12)
        x = jax.random.normal(ks[0], (N, D), dtype=jnp.float32)
        edge_index = jax.random.randint(ks[1], (2, E), 0, N, dtype=jnp.int64)
        edge_attr = jax.random.uniform(ks[2], (E, ED), dtype=jnp.float32)
        s = 1.0 / np.sqrt(ED)
        W1 = jax.random.uniform(ks[3], (D, ED), jnp.float32, -s, s)
        b1 = jax.random.uniform(ks[4], (D,), jnp.float32, -s, s)
        s = 1.0 / np.sqrt(D)
        W2 = jax.random.uniform(ks[5], (D, D), jnp.float32, -s, s)
        b2 = jax.random.uniform(ks[6], (D,), jnp.float32, -s, s)
        Ws = jax.random.uniform(ks[7], (D, D), jnp.float32, -s, s)
        bs = jax.random.uniform(ks[8], (D,), jnp.float32, -s, s)
        Wn = jax.random.uniform(ks[9], (D, D), jnp.float32, -s, s)
        bn = jax.random.uniform(ks[10], (D,), jnp.float32, -s, s)
        return {'x': x, 'edge_index': edge_index, 'edge_attr': edge_attr, 'W1': W1, 'b1': b1, 'W2': W2, 'b2': b2, 'Ws': Ws, 'bs': bs, 'Wn': Wn, 'bn': bn}
    _L1_gnn_all = _L1_gnn_setup()
    _L1_gnn_in = {k: v for k, v in _L1_gnn_all.items() if k in ('W1', 'b1', 'W2', 'b2', 'Ws', 'bs', 'Wn', 'bn')}
    del _L1_gnn_all

    def _L2_gnn_setup():
        import jax, jax.numpy as jnp
        import numpy as np
        EPS = 1e-05

        def _mlp(h, W, b, gamma, beta):
            h = jax.nn.relu(h @ W + b)
            mu = jnp.mean(h, axis=0)
            var = jnp.mean(jnp.square(h - mu), axis=0)
            return gamma * (h - mu) * jax.lax.rsqrt(var + EPS) + beta
        key = jax.random.key(seed)
        ks = jax.random.split(key, 10)
        N, E, C_in, C_out, E_dim = (50000, 12500, 96, 96, 4)
        x = jax.random.normal(ks[0], (N, C_in), dtype=jnp.float32)
        edge_index = jax.random.randint(ks[1], (2, E), 0, N, dtype=jnp.int64)
        edge_attr = jax.random.normal(ks[2], (E, E_dim), dtype=jnp.float32)
        s = lambda fan_in: 1.0 / np.sqrt(fan_in)
        W_node = jax.random.uniform(ks[3], (C_in, C_out), jnp.float32, -s(C_in), s(C_in))
        b_node = jnp.zeros((C_out,), jnp.float32)
        g_node = jnp.ones((C_out,), jnp.float32)
        beta_node = jnp.zeros((C_out,), jnp.float32)
        W_edge = jax.random.uniform(ks[4], (E_dim, C_out), jnp.float32, -s(E_dim), s(E_dim))
        b_edge = jnp.zeros((C_out,), jnp.float32)
        g_edge = jnp.ones((C_out,), jnp.float32)
        beta_edge = jnp.zeros((C_out,), jnp.float32)
        M_in = 2 * C_in + C_out
        W_msg = jax.random.uniform(ks[5], (M_in, C_out), jnp.float32, -s(M_in), s(M_in))
        b_msg = jnp.zeros((C_out,), jnp.float32)
        g_msg = jnp.ones((C_out,), jnp.float32)
        beta_msg = jnp.zeros((C_out,), jnp.float32)
        return dict(x=x, edge_index=edge_index, edge_attr=edge_attr, W_node=W_node, b_node=b_node, g_node=g_node, beta_node=beta_node, W_edge=W_edge, b_edge=b_edge, g_edge=g_edge, beta_edge=beta_edge, W_msg=W_msg, b_msg=b_msg, g_msg=g_msg, beta_msg=beta_msg)
    _L2_gnn_all = _L2_gnn_setup()
    _L2_gnn_in = {k: v for k, v in _L2_gnn_all.items() if k in ('W_node', 'b_node', 'g_node', 'beta_node', 'W_edge', 'b_edge', 'g_edge', 'beta_edge', 'W_msg', 'b_msg', 'g_msg', 'beta_msg')}
    del _L2_gnn_all

    def _L3_gnn_setup():
        import jax, jax.numpy as jnp
        import numpy as np
        N_NODES = 50000
        N_EDGES = 12500
        IN_DIM = 96
        NUM_HEADS = 8
        HEAD_DIM = IN_DIM // NUM_HEADS
        key = jax.random.key(seed)
        ks = jax.random.split(key, 11)
        s = 1.0 / np.sqrt(IN_DIM)
        return {'x': jax.random.normal(ks[0], (N_NODES, IN_DIM), dtype=jnp.float32), 'edge_index': jax.random.randint(ks[1], (2, N_EDGES), 0, N_NODES, dtype=jnp.int64), 'edge_attr': jax.random.normal(ks[2], (N_EDGES, IN_DIM), dtype=jnp.float32), 'Wq': jax.random.normal(ks[3], (IN_DIM, IN_DIM), dtype=jnp.float32) * s, 'bq': jax.random.normal(ks[4], (IN_DIM,), dtype=jnp.float32) * s, 'Wk': jax.random.normal(ks[5], (IN_DIM, IN_DIM), dtype=jnp.float32) * s, 'bk': jax.random.normal(ks[6], (IN_DIM,), dtype=jnp.float32) * s, 'We': jax.random.normal(ks[7], (IN_DIM, IN_DIM), dtype=jnp.float32) * s, 'be': jax.random.normal(ks[8], (IN_DIM,), dtype=jnp.float32) * s, 'Wv': jax.random.normal(ks[9], (IN_DIM, IN_DIM), dtype=jnp.float32) * s, 'bv': jax.random.normal(ks[10], (IN_DIM,), dtype=jnp.float32) * s}
    _L3_gnn_all = _L3_gnn_setup()
    _L3_gnn_in = {k: v for k, v in _L3_gnn_all.items() if k in ('Wq', 'bq', 'Wk', 'bk', 'We', 'be', 'Wv', 'bv')}
    del _L3_gnn_all
    return {'x': x, 'src': src, 'dst': dst, 'edge_attr_17': edge_attr_17, 'edge_attr_4': edge_attr_4, 'edge_attr_96': edge_attr_96, 'L1_gnn_W1': _L1_gnn_in['W1'], 'L1_gnn_b1': _L1_gnn_in['b1'], 'L1_gnn_W2': _L1_gnn_in['W2'], 'L1_gnn_b2': _L1_gnn_in['b2'], 'L1_gnn_Ws': _L1_gnn_in['Ws'], 'L1_gnn_bs': _L1_gnn_in['bs'], 'L1_gnn_Wn': _L1_gnn_in['Wn'], 'L1_gnn_bn': _L1_gnn_in['bn'], 'L2_gnn_W_node': _L2_gnn_in['W_node'], 'L2_gnn_b_node': _L2_gnn_in['b_node'], 'L2_gnn_g_node': _L2_gnn_in['g_node'], 'L2_gnn_beta_node': _L2_gnn_in['beta_node'], 'L2_gnn_W_edge': _L2_gnn_in['W_edge'], 'L2_gnn_b_edge': _L2_gnn_in['b_edge'], 'L2_gnn_g_edge': _L2_gnn_in['g_edge'], 'L2_gnn_beta_edge': _L2_gnn_in['beta_edge'], 'L2_gnn_W_msg': _L2_gnn_in['W_msg'], 'L2_gnn_b_msg': _L2_gnn_in['b_msg'], 'L2_gnn_g_msg': _L2_gnn_in['g_msg'], 'L2_gnn_beta_msg': _L2_gnn_in['beta_msg'], 'L3_gnn_Wq': _L3_gnn_in['Wq'], 'L3_gnn_bq': _L3_gnn_in['bq'], 'L3_gnn_Wk': _L3_gnn_in['Wk'], 'L3_gnn_bk': _L3_gnn_in['bk'], 'L3_gnn_We': _L3_gnn_in['We'], 'L3_gnn_be': _L3_gnn_in['be'], 'L3_gnn_Wv': _L3_gnn_in['Wv'], 'L3_gnn_bv': _L3_gnn_in['bv']}

def reference(x, src, dst, edge_attr_17, edge_attr_4, edge_attr_96, L1_gnn_W1, L1_gnn_b1, L1_gnn_W2, L1_gnn_b2, L1_gnn_Ws, L1_gnn_bs, L1_gnn_Wn, L1_gnn_bn, L2_gnn_W_node, L2_gnn_b_node, L2_gnn_g_node, L2_gnn_beta_node, L2_gnn_W_edge, L2_gnn_b_edge, L2_gnn_g_edge, L2_gnn_beta_edge, L2_gnn_W_msg, L2_gnn_b_msg, L2_gnn_g_msg, L2_gnn_beta_msg, L3_gnn_Wq, L3_gnn_bq, L3_gnn_Wk, L3_gnn_bk, L3_gnn_We, L3_gnn_be, L3_gnn_Wv, L3_gnn_bv):
    import jax
    import jax.numpy as jnp

    def _L0_gnn_ref(x, edge_index, num_nodes):
        import jax, jax.numpy as jnp
        import numpy as np
        N_NODES = 50000
        N_EDGES = 12500
        D_FEAT = 96
        row, col = (edge_index[0], edge_index[1])
        deg = jnp.bincount(row, length=num_nodes).astype(x.dtype)
        deg_inv_sqrt = jnp.where(deg > 0, jax.lax.rsqrt(jnp.maximum(deg, 1.0)), 0.0)
        norm = deg_inv_sqrt[row] * deg_inv_sqrt[col]
        msg = x[col] * norm[:, None]
        out = jax.ops.segment_sum(msg, row, num_segments=num_nodes)
        return out

    def _L1_gnn_ref(x, edge_index, edge_attr, W1, b1, W2, b2, Ws, bs, Wn, bn):
        import jax, jax.numpy as jnp
        import numpy as np
        N = 50000
        E = 12500
        D = 96
        ED = 17
        src, dst = (edge_index[0], edge_index[1])
        h = jax.nn.relu(edge_attr @ W1.T + b1)
        w = h @ W2.T + b2
        msg = w * x[src]
        agg = jax.ops.segment_sum(msg, dst, num_segments=x.shape[0])
        return jax.nn.relu(x @ Ws.T + bs + agg @ Wn.T + bn)

    def _L2_gnn_ref(x, edge_index, edge_attr, W_node, b_node, g_node, beta_node, W_edge, b_edge, g_edge, beta_edge, W_msg, b_msg, g_msg, beta_msg):
        import jax, jax.numpy as jnp
        import numpy as np
        EPS = 1e-05

        def _mlp(h, W, b, gamma, beta):
            h = jax.nn.relu(h @ W + b)
            mu = jnp.mean(h, axis=0)
            var = jnp.mean(jnp.square(h - mu), axis=0)
            return gamma * (h - mu) * jax.lax.rsqrt(var + EPS) + beta
        node_feat = _mlp(x, W_node, b_node, g_node, beta_node)
        edge_feat = _mlp(edge_attr, W_edge, b_edge, g_edge, beta_edge)
        row, col = (edge_index[0], edge_index[1])
        message = jnp.concatenate([x[row], x[col], edge_feat], axis=1)
        message = _mlp(message, W_msg, b_msg, g_msg, beta_msg)
        agg = jax.ops.segment_sum(message, col, num_segments=node_feat.shape[0])
        return agg + node_feat

    def _L3_gnn_ref(x, edge_index, edge_attr, Wq, bq, Wk, bk, We, be, Wv, bv):
        import jax, jax.numpy as jnp
        import numpy as np
        N_NODES = 50000
        N_EDGES = 12500
        IN_DIM = 96
        NUM_HEADS = 8
        HEAD_DIM = IN_DIM // NUM_HEADS
        N = x.shape[0]
        H, D = (NUM_HEADS, HEAD_DIM)
        Q_h = (x @ Wq + bq).reshape(N, H, D)
        K_h = (x @ Wk + bk).reshape(N, H, D)
        V_h = (x @ Wv + bv).reshape(N, H, D)
        E = (edge_attr @ We + be).reshape(-1, H, D)
        src_idx = edge_index[0]
        dst_idx = edge_index[1]
        src = K_h[src_idx]
        dest = Q_h[dst_idx]
        score = src * dest / jnp.sqrt(jnp.asarray(D, x.dtype))
        score = score * E
        score = jnp.exp(jnp.clip(score.sum(-1, keepdims=True), -5.0, 5.0))
        msg = V_h[src_idx] * score
        wV = jax.ops.segment_sum(msg, dst_idx, num_segments=N)
        Z = jax.ops.segment_sum(score, dst_idx, num_segments=N)
        h_out = wV / (Z + 1e-06)
        return h_out.reshape(N, H * D)
    edge_index = jnp.stack([src, dst])
    h = jnp.maximum(_layernorm(x, axis=-1), 0.0)
    x = x + _L0_gnn_ref(h, edge_index, 100000)
    h = jnp.maximum(_layernorm(x, axis=-1), 0.0)
    x = x + _L1_gnn_ref(h, edge_index, edge_attr_17, L1_gnn_W1, L1_gnn_b1, L1_gnn_W2, L1_gnn_b2, L1_gnn_Ws, L1_gnn_bs, L1_gnn_Wn, L1_gnn_bn)
    h = jnp.maximum(_layernorm(x, axis=-1), 0.0)
    x = x + _L2_gnn_ref(h, edge_index, edge_attr_4, L2_gnn_W_node, L2_gnn_b_node, L2_gnn_g_node, L2_gnn_beta_node, L2_gnn_W_edge, L2_gnn_b_edge, L2_gnn_g_edge, L2_gnn_beta_edge, L2_gnn_W_msg, L2_gnn_b_msg, L2_gnn_g_msg, L2_gnn_beta_msg)
    h = jnp.maximum(_layernorm(x, axis=-1), 0.0)
    x = x + _L3_gnn_ref(h, edge_index, edge_attr_96, L3_gnn_Wq, L3_gnn_bq, L3_gnn_Wk, L3_gnn_bk, L3_gnn_We, L3_gnn_be, L3_gnn_Wv, L3_gnn_bv)
    return x

_drawn_inputs = setup_inputs


def setup_inputs(seed=0):
    import zlib

    import numpy as np

    out = dict(_drawn_inputs(seed))
    spreads = {'L2_gnn_b_node': (0.0, 0.1),
     'L2_gnn_g_node': (1.0, 0.2),
     'L2_gnn_beta_node': (0.0, 0.1),
     'L2_gnn_b_edge': (0.0, 0.1),
     'L2_gnn_g_edge': (1.0, 0.2),
     'L2_gnn_beta_edge': (0.0, 0.479),
     'L2_gnn_b_msg': (0.0, 0.1),
     'L2_gnn_g_msg': (1.0, 0.2),
     'L2_gnn_beta_msg': (0.0, 0.1)}
    factors = {'edge_attr_17': 4.886,
     'edge_attr_96': 3.541,
     'L1_gnn_b1': 5.08,
     'L1_gnn_b2': 4.662,
     'L3_gnn_Wq': 3.502,
     'L3_gnn_bq': 26.02,
     'L3_gnn_Wk': 3.473,
     'L3_gnn_bk': 26.425,
     'L3_gnn_We': 3.545,
     'L3_gnn_be': 163.313}
    for name, (base, spread) in spreads.items():
        noise = np.random.default_rng([zlib.crc32(name.encode()), seed]).standard_normal(out[name].shape)
        drawn = base * np.exp(spread * noise) if base else spread * noise
        out[name] = jnp.asarray(drawn.astype(out[name].dtype))
    for name, factor in factors.items():
        out[name] = (out[name] * factor).astype(out[name].dtype)
    return out
```

```python
from contextlib import ExitStack

import concourse.bass as bass
from concourse import mybir

F32 = mybir.dt.float32
F16 = mybir.dt.float16
I32 = mybir.dt.int32
ALU = mybir.AluOpType
ACT = mybir.ActivationFunctionType

D = 96
EP = 125
GT = 4
GE = GT * EP
NP = 128
NG = 8
BLK = NP * NG
HEADS = 8
HD = D // HEADS
WU = D + HEADS
LN_EPS = 1e-5
BN_EPS = 1e-5
Z_EPS = 1e-6
SCORE = float(HD) ** -0.5
SKIP = 1 << 20


class Steps:

    def __init__(self, eng, sem):
        self.eng, self.sem, self.n, self.base = eng, sem, 0, 0

    def done(self, ins):
        self.n += 1
        ins.then_inc(self.sem, 1)

    def settle(self):
        self.eng.wait_ge(self.sem, self.base + self.n)


def loop(eng, turns, body, me=None, last=None):
    before = me.n if me else 0
    body(0)
    per_turn = me.n - before if me else 0
    end = turns - 1 if last else turns
    if end > 1:
        with eng.Fori(1, end) as t:
            if me:
                me.base, me.n = per_turn * t, before
            body(t)
    if last:
        if me:
            me.base, me.n = 0, before + per_turn * (turns - 1)
        last(turns - 1)
    if me:
        me.base, me.n = 0, before + per_turn * turns


def started(t):
    return not (isinstance(t, int) and t == 0)


def build(nc, A, out):
    N = A["x"].shape[0]
    E = A["src"].shape[0]
    ET = E // EP
    TC = ET // 2
    GR = ET // GT
    PAIRS = GR // 2
    FULL = N // BLK
    TAILP = NP * 3 // 4
    TAILG = (N - FULL * BLK) // TAILP
    NB = FULL + 1
    BPAIRS = NB // 2
    HI = NB * NG
    HB = HI // 2
    IW = max(HI, NP)
    assert E == ET * EP and ET % (2 * GT) == 0 and NB % 2 == 0 and TAILP * TAILG == N - FULL * BLK
    assert HB <= 512 and TC <= 128

    def internal(name, rows, cols=D):
        return nc.dram_tensor(name, (rows, cols), F32, kind="Internal").ap()

    x1 = internal("x1_table", N + GE)
    agg1 = internal("agg1_table", N)
    x2 = internal("x2_table", N)
    dis_table = internal("dis_table", NB * BLK, 1)
    fd_rows = internal("fd_rows", E)
    keep_rows = internal("keep_rows", E)

    ctx = ExitStack()
    with ctx:
        def sb(name, shape, dt=F32, c=ctx):
            return c.enter_context(nc.sbuf_tensor(name, shape, dt))

        def pb(name, shape, c):
            return c.enter_context(nc.psum_tensor(name, shape, F32))

        def kept_sem(name):
            return ctx.enter_context(nc.semaphore(name))

        phase_sems = []

        def sem(name):
            phase_sems.append(nc.alloc_semaphore(name))
            return phase_sems[-1]

        def end_phase():
            nc.clear_and_free_semaphores(phase_sems)
            phase_sems.clear()
            nc.all_engine_barrier()

        def two(name):
            return [sem(f"{name}_even"), sem(f"{name}_odd")]

        ident = sb("ident", [128, 128])
        ones = sb("ones", [128, 128])
        zeros = sb("zeros", [128, NG * D])
        eps_col = sb("eps_col", [128, 1])
        first_row = sb("first_row", [TC, 2, EP])
        tile_sel = sb("tile_sel", [TC, 2, ET])
        joins = sb("joins", [TC, 2, ET])
        src_f = sb("src_f", [EP, ET])
        dst_f = sb("dst_f", [EP, ET])
        src_i = sb("src_i", [EP, ET + GT], I32)
        dst_i = sb("dst_i", [EP, ET + GT], I32)
        end_i = sb("end_i", [EP, ET + GT], I32)
        tails = sb("tails", [TC, 2, WU])
        carry = sb("carry", [TC, 2, WU])
        mean_n = sb("mean_n", [NP, NB, NG])
        rstd_n = sb("rstd_n", [NP, NB, NG])
        f_stats = sb("f_stats", [D, 2 * NB, 6])
        r_stats = sb("r_stats", [D, GR, 6])
        e_stats = sb("e_stats", [D, GR, 6])
        node_ac = sb("node_ac", [D, 2])
        msg_ac = sb("msg_ac", [D, 2])
        edge_ac = sb("edge_ac", [D, 2])
        affine = sb("affine", [NP, 4, D])
        W1T = sb("W1T", [18, D])
        W2T = sb("W2T", [D + 1, D])
        WsT = sb("WsT", [D + 1, D])
        WnT = sb("WnT", [D, D])
        bn_row = sb("bn_row", [D + 1, D])
        Wnode = sb("Wnode", [D + 1, D])
        Wedge = sb("Wedge", [5, D])
        Wmsg = sb("Wmsg", [D, 3, D])
        Wc = sb("Wc", [D, D])
        msg_bias = sb("msg_bias", [D, 1])
        cols = sb("cols", [D, 8])
        WkV = sb("WkV", [D + 1, 2 * D])
        Wq = sb("Wq", [D + 1, D])
        We = sb("We", [D + 1, D])
        bn_w = sb("bn_w", [D, 4])
        B_NODE, G_NODE, BETA_NODE, G_EDGE, BETA_EDGE, B_MSG, G_MSG, BETA_MSG = range(8)

        x1_ready, agg1_ready, zeros_ready = kept_sem("x1_ready"), kept_sem("agg1_ready"), kept_sem("zeros_ready")
        gate = kept_sem("gate")

        def seen(pool):
            pool.sem_inc(gate, 1)

        def spread(col, n, shape):
            return col.rearrange("p (a b) -> p a b", b=1).to_broadcast(shape)

        class Norm:

            def __init__(self, name, c, P, G):
                self.P, self.G = P, G
                self.st = sb(f"{name}_st", [P, G, 6], c=c)
                self.w = sb(f"{name}_w", [P, 6, G], c=c)
                self.mean = sb(f"{name}_mean", [P, G], c=c)
                self.rstd = sb(f"{name}_rstd", [P, G], c=c)
                self.var_ready, self.root_ready = sem(f"{name}_var_ready"), sem(f"{name}_root_ready")

            def stats(self, v, me, X, P, G, mean=None):
                mean = self.mean[0:P, 0:G] if mean is None else mean
                st, w = self.st, self.w
                for g in range(G):
                    me.done(v.bn_stats(st[0:P, g, :], X[0:P, g, :]))
                me.settle()
                me.done(v.tensor_tensor(w[0:P, 0, 0:G], st[0:P, 0:G, 1], st[0:P, 0:G, 4], ALU.add))
                me.done(v.tensor_tensor(w[0:P, 1, 0:G], st[0:P, 0:G, 1], st[0:P, 0:G, 4], ALU.subtract))
                me.done(v.tensor_tensor(w[0:P, 2, 0:G], st[0:P, 0:G, 2], st[0:P, 0:G, 5], ALU.add))
                me.settle()
                me.done(v.tensor_scalar(mean, w[0:P, 0, 0:G], 0.5, None, ALU.mult))
                me.done(v.tensor_tensor(w[0:P, 3, 0:G], w[0:P, 1, 0:G], w[0:P, 1, 0:G], ALU.mult))
                me.settle()
                v.scalar_tensor_tensor(w[0:P, 4, 0:G], w[0:P, 3, 0:G], D / 4.0, w[0:P, 2, 0:G],
                                       ALU.mult, ALU.add).then_inc(self.var_ready, 1)

            def root(self, act, n, P, G):
                act.wait_ge(self.var_ready, n)
                act.activation(self.w[0:P, 5, 0:G], self.w[0:P, 4, 0:G], ACT.Sqrt,
                               bias=eps_col[0:P, :], scale=1.0 / D).then_inc(self.root_ready, 1)

            def invert(self, v, me, n, P, G, rstd=None):
                v.wait_ge(self.root_ready, n)
                me.done(v.reciprocal(self.rstd[0:P, 0:G] if rstd is None else rstd, self.w[0:P, 5, 0:G]))
                me.settle()

        with ExitStack() as c:
            dnext_i = sb("dnext_i", [EP, ET], I32, c)
            dnext_f = sb("dnext_f", [EP, ET], c=c)
            last_f = sb("last_f", [EP, ET], c=c)
            dstrow_i = sb("dstrow_i", [TC, 2, EP], I32, c)
            dst_row = sb("dst_row", [TC, 2, EP], c=c)
            first_i = sb("first_i", [TC, ET], I32, c)
            first_f = sb("first_f", [TC, ET], c=c)
            hi_i = sb("hi_i", [EP, 3, ET], I32, c)
            hi_f = sb("hi_f", [EP, ET], c=c)
            lo_f = sb("lo_f", [EP, ET], c=c)
            iota_i = sb("iota_i", [EP, IW], I32, c)
            iota_h = sb("iota_h", [EP, IW], F16, c)
            hot_hi = sb("hot_hi", [EP, 2, HI], F16, c)
            hot_lo = sb("hot_lo", [EP, 2, NP], F16, c)
            zero_h = sb("zero_h", [1, NP + HB], F16, c)
            dg = sb("dg", [NP, 3, HI], c=c)
            dg_root = sb("dg_root", [NP, HI], c=c)
            e4 = sb("e4", [EP, 2, GT, 5], c=c)
            e4T = sb("e4T", [5, 2, GE], c=c)
            efs = sb("efs", [D, 2, GE], c=c)
            pdeg = pb("pdeg", [NP, 2, 512], c)
            pe4 = [pb(f"pe4_{k}", [5, 512], c) for k in range(2)]
            pef = [pb(f"pef_{k}", [D, 512], c) for k in range(2)]

            s_rows, s_w, s_dis = sem("rows_loaded"), sem("weights_loaded"), sem("dis_stored")
            s_fill, s_vs, s_const, s_sel = sem("fills_done"), sem("p0_steps"), sem("consts_ready"), sem("selects_ready")
            s_join = sem("joins_compared")
            s_hot, s_deg, s_degin = sem("hot_ready"), sem("degrees_added"), sem("degrees_read")
            s_root, s_dg = sem("root_ready"), sem("dis_ready")
            s_e4 = two("e4_loaded")
            s_e4t, s_e4c, s_ef, s_efr, s_efs = sem("e4_turned"), sem("e4_copied"), sem("ef_made"), sem("ef_relu"), sem("ef_counted")

            row = lambda n: A[n].rearrange("(a n) -> a n", a=1)
            turned = lambda n: A[n].rearrange("o i -> i o")
            loads = [
                (W1T[0:17, :], turned("L1_gnn_W1")), (W1T[17:18, :], row("L1_gnn_b1")),
                (W2T[0:D, :], turned("L1_gnn_W2")), (W2T[D:D + 1, :], row("L1_gnn_b2")),
                (WsT[0:D, :], turned("L1_gnn_Ws")), (WsT[D:D + 1, :], row("L1_gnn_bs")),
                (WnT[:, :], turned("L1_gnn_Wn")), (bn_row[D:D + 1, :], row("L1_gnn_bn")),
                (Wnode[0:D, :], A["L2_gnn_W_node"]), (Wnode[D:D + 1, :], row("L2_gnn_b_node")),
                (Wedge[0:4, :], A["L2_gnn_W_edge"]), (Wedge[4:5, :], row("L2_gnn_b_edge")),
                (Wmsg[:, :, :], A["L2_gnn_W_msg"].rearrange("(k i) o -> i k o", k=3)),
                (WkV[0:D, 0:D], A["L3_gnn_Wk"]), (WkV[0:D, D:2 * D], A["L3_gnn_Wv"]),
                (WkV[D:D + 1, 0:D], row("L3_gnn_bk")), (WkV[D:D + 1, D:2 * D], row("L3_gnn_bv")),
                (Wq[0:D, :], A["L3_gnn_Wq"]), (Wq[D:D + 1, :], row("L3_gnn_bq")),
                (We[0:D, :], A["L3_gnn_We"]), (We[D:D + 1, :], row("L3_gnn_be")),
            ] + [(cols[:, k:k + 1], A[n].rearrange("(p a) -> p a", a=1)) for k, n in enumerate(
                ("L2_gnn_b_node", "L2_gnn_g_node", "L2_gnn_beta_node", "L2_gnn_g_edge",
                 "L2_gnn_beta_edge", "L2_gnn_b_msg", "L2_gnn_g_msg", "L2_gnn_beta_msg"))]
            NW = 16 * len(loads)
            e4_groups = A["edge_attr_4"].rearrange("(g u p) k -> p g u k", u=GT, p=EP)

            with nc.Block() as block:
                @block.sync
                def _(sp):
                    half = TC * EP
                    with nc.allow_non_contiguous_dma(reason="indices by edge of a tile, and small weights, once"):
                        sp.dma_start(src_i[:, 0:ET], A["src"].rearrange("(t e) -> e t", e=EP)).then_inc(s_rows, 16)
                        sp.dma_start(dst_i[:, 0:ET], A["dst"].rearrange("(t e) -> e t", e=EP)).then_inc(s_rows, 16)
                        sp.dma_start(dnext_i[0:EP, 0:ET - 1], A["dst"][1:1 + E - EP].rearrange("(t e) -> e t", e=EP)).then_inc(s_rows, 16)
                        sp.wait_ge(s_fill, 1)
                        sp.dma_start(dnext_i[0:EP - 1, ET - 1:ET], A["dst"][E - EP + 1:E].rearrange("(e a) -> e a", a=1)).then_inc(s_rows, 16)
                        for h in range(2):
                            sp.dma_start(dstrow_i[:, h, :], A["dst"][h * half:(h + 1) * half].rearrange("(t e) -> t e", e=EP)).then_inc(s_rows, 16)
                        firsts = A["dst"].rearrange("(t e) -> e t", e=EP)[0:1, :]
                        sp.dma_start(first_i[:, :], firsts.to_broadcast([TC, ET])).then_inc(s_rows, 16)
                        for o, i in loads:
                            sp.dma_start(o, i).then_inc(s_w, 16)

                    sp.wait_ge(s_fill, 2)

                    def e4_loads(t):
                        for k in range(2):
                            if started(t):
                                sp.wait_ge(s_e4t, 2 * t + k - 1)
                            sp.dma_start(e4[:, k, :, 0:4], e4_groups[:, bass.ds(2 * t + k, 1), :, :]
                                         .rearrange("p g u k -> p (g u) k")).then_inc(s_e4[k], 16)
                    loop(sp, PAIRS, e4_loads)
                    sp.wait_ge(s_w, NW)
                    sp.wait_ge(s_dg, 1)
                    sp.dma_start(dis_table.rearrange("(b p g) a -> p b (g a)", p=NP, g=NG),
                                 dg[:, 2, :].rearrange("p (b g) -> p b g", g=NG)).then_inc(s_dis, 16)
                    sp.wait_ge(s_dis, 16)

                @block.gpsimd
                def _(pool):
                    pool.memset(dnext_i[:, ET - 1:ET], -1).then_inc(s_fill, 1)
                    pool.memset(e4[:, :, :, :], 1.0).then_inc(s_fill, 1)
                    pool.memset(ident[:, :], 0.0).then_inc(s_fill, 1)
                    pool.memset(tile_sel[:, :, :], 0.0).then_inc(s_fill, 1)
                    pool.memset(src_i[:, ET:ET + GT], 0).then_inc(s_const, 1)
                    pool.memset(dst_i[:, ET:ET + GT], 0).then_inc(s_const, 1)
                    pool.memset(end_i[:, ET:ET + GT], 0).then_inc(s_const, 1)
                    pool.memset(ones[:, :], 1.0).then_inc(s_const, 1)
                    pool.memset(zeros[:, :], 0.0).then_inc(zeros_ready, 1)
                    pool.memset(eps_col[:, :], LN_EPS).then_inc(s_const, 1)
                    pool.memset(zero_h[:, :], 0.0).then_inc(s_const, 1)
                    pool.iota(iota_i[:, :], pattern=[[1, IW]], base=0, channel_multiplier=0).then_inc(s_const, 1)
                    pool.wait_ge(s_fill, 4)
                    pool.affine_select(out=ident[:, :], in_=ident[:, :], compare_op=ALU.not_equal, fill=1.0,
                                       base=0, pattern=[[-1, 128]], channel_multiplier=1).then_inc(s_const, 1)
                    pool.affine_select(out=tile_sel[:, :, :], in_=tile_sel[:, :, :], compare_op=ALU.not_equal, fill=1.0,
                                       base=0, pattern=[[TC, 2], [-1, ET]], channel_multiplier=1).then_inc(s_const, 1)
                    pool.wait_ge(s_join, 2)
                    pool.affine_select(out=joins[:, :, :], in_=joins[:, :, :], compare_op=ALU.is_gt, fill=0.0,
                                       base=0, pattern=[[-TC, 2], [1, ET]], channel_multiplier=-1).then_inc(s_sel, 1)

                @block.scalar
                def _(act):
                    act.wait_ge(zeros_ready, 1)
                    act.dma_start(x1[N:N + GE, :].rearrange("(p a) b -> p (a b)", p=EP), zeros[0:EP, 0:GT * D]).then_inc(x1_ready, 16)
                    piece = N // 16
                    for k in range(16):
                        act.dma_start(x1[piece * k:piece * (k + 1), :], A["x"][piece * k:piece * (k + 1), :]).then_inc(x1_ready, 16)
                    full = agg1[0:FULL * BLK, :].rearrange("(b p g) f -> p b (g f)", p=NP, g=NG)
                    act.dma_start(full, zeros[:, :].rearrange("p (a n) -> p a n", a=1).to_broadcast([NP, FULL, NG * D])).then_inc(agg1_ready, 16)
                    act.dma_start(agg1[FULL * BLK:N, :].rearrange("(p g) f -> p (g f)", g=TAILG), zeros[0:TAILP, 0:TAILG * D]).then_inc(agg1_ready, 16)

                    def features(t):
                        for k in range(2):
                            g = 2 * t + k
                            act.wait_ge(s_e4t, g + 1)
                            act.activation(e4T[:, k, :], pe4[k][:, 0:GE], ACT.Copy).then_inc(s_e4c, 1)
                            act.wait_ge(s_ef, g + 1)
                            if started(t):
                                act.wait_ge(s_efs, g - 1)
                            act.activation(efs[:, k, :], pef[k][:, 0:GE], ACT.Relu).then_inc(s_efr, 1)
                    loop(act, PAIRS, features)
                    act.wait_ge(s_degin, 2)
                    act.activation(dg_root[:, :], dg[:, 1, :], ACT.Sqrt).then_inc(s_root, 1)

                @block.tensor
                def _(pe):
                    pe.wait_ge(s_const, 9)
                    for h in range(2):
                        pe.matmul(pdeg[:, h, 0:HB], zero_h[0:1, 0:NP], zero_h[0:1, NP:NP + HB], start=True, stop=False)

                    def degrees(t):
                        for k in range(2):
                            pe.wait_ge(s_hot, 2 * t + k + 1)
                            for h in range(2):
                                last = pe.matmul(pdeg[:, h, 0:HB], hot_lo[:, k, :], hot_hi[:, k, h * HB:(h + 1) * HB],
                                                 start=False, stop=False, skip_group_check=True)
                            last.then_inc(s_deg, 1)
                    loop(pe, ET // 2, degrees)
                    for h in range(2):
                        last = pe.matmul(pdeg[:, h, 0:HB], zero_h[0:1, 0:NP], zero_h[0:1, NP:NP + HB], start=False, stop=True)
                    last.then_inc(s_deg, 1)
                    pe.wait_ge(s_w, NW)

                    def features(t):
                        for k in range(2):
                            g = 2 * t + k
                            pe.wait_ge(s_e4[k], 16 * t + 16)
                            if started(t):
                                pe.wait_ge(s_e4c, g - 1)
                            for u in range(GT):
                                last = pe.transpose(pe4[k][:, u * EP:(u + 1) * EP], e4[:, k, u, :], ident[0:EP, 0:EP])
                            last.then_inc(s_e4t, 1)
                            pe.wait_ge(s_e4c, g + 1)
                            if started(t):
                                pe.wait_ge(s_efr, g - 1)
                            pe.matmul(pef[k][:, 0:GE], Wedge[:, :], e4T[:, k, :], start=True, stop=True).then_inc(s_ef, 1)
                    loop(pe, PAIRS, features)

                @block.vector
                def _(v):
                    me = Steps(v, s_vs)
                    v.wait_ge(s_rows, 16 * 7)
                    v.wait_ge(s_const, 9)
                    me.done(v.tensor_copy(src_f[:, :], src_i[:, 0:ET]))
                    me.done(v.tensor_copy(dst_f[:, :], dst_i[:, 0:ET]))
                    me.done(v.tensor_copy(dnext_f[:, :], dnext_i[:, :]))
                    me.done(v.tensor_copy(dst_row[:, :, :], dstrow_i[:, :, :]))
                    me.done(v.tensor_copy(first_f[:, :], first_i[:, :]))
                    me.done(v.tensor_copy(iota_h[:, :], iota_i[:, :]))
                    me.done(v.tensor_scalar(hi_i[:, 0, :], src_i[:, 0:ET], 10, 3, ALU.logical_shift_right, ALU.logical_shift_left))
                    me.done(v.tensor_scalar(hi_i[:, 1, :], src_i[:, 0:ET], NG - 1, None, ALU.bitwise_and))
                    me.done(v.tensor_scalar(hi_i[:, 2, :], src_i[:, 0:ET], 3, NP - 1, ALU.logical_shift_right, ALU.bitwise_and))
                    me.settle()
                    for h in range(2):
                        me.done(v.tensor_scalar(first_row[:, h, :], dst_row[:, h, :], dst_row[:, h, 0:1], None, ALU.is_equal))
                        v.tensor_scalar(joins[:, h, :], first_f[:, :], dst_row[:, h, EP - 1:EP], None, ALU.is_equal).then_inc(s_join, 1)
                    me.done(v.tensor_tensor(hi_f[:, :], hi_i[:, 0, :], hi_i[:, 1, :], ALU.add))
                    me.done(v.tensor_copy(lo_f[:, :], hi_i[:, 2, :]))
                    me.done(v.tensor_tensor(last_f[:, :], dst_f[:, :], dnext_f[:, :], ALU.not_equal))
                    me.settle()
                    me.done(v.scalar_tensor_tensor(dnext_f[:, :], dst_f[:, :], -float(SKIP), last_f[:, :], ALU.add, ALU.mult))
                    me.settle()
                    me.done(v.tensor_scalar(end_i[:, 0:ET], dnext_f[:, :], float(SKIP), None, ALU.add))
                    v.wait_ge(s_w, NW)
                    me.done(v.tensor_tensor(WsT[D:D + 1, :], WsT[D:D + 1, :], bn_row[D:D + 1, :], ALU.add))

                    def hots(t):
                        for k in range(2):
                            if started(t):
                                v.wait_ge(s_deg, 2 * t + k - 1)
                            v.tensor_scalar(hot_lo[:, k, :], iota_h[:, 0:NP], lo_f[:, bass.ds(2 * t + k, 1)], None, ALU.is_equal)
                            v.tensor_scalar(hot_hi[:, k, :], iota_h[:, 0:HI], hi_f[:, bass.ds(2 * t + k, 1)], None, ALU.is_equal).then_inc(s_hot, 1)
                    loop(v, ET // 2, hots)
                    v.wait_ge(s_deg, ET + 1)
                    for h in range(2):
                        v.tensor_scalar(dg[:, 1, h * HB:(h + 1) * HB], pdeg[:, h, 0:HB], 1.0, None, ALU.max).then_inc(s_degin, 1)
                        me.done(v.tensor_scalar(dg[:, 0, h * HB:(h + 1) * HB], pdeg[:, h, 0:HB], 1.0, None, ALU.min))

                    def features(t):
                        for k in range(2):
                            v.wait_ge(s_efr, 2 * t + k + 1)
                            v.bn_stats(e_stats[:, bass.ds(2 * t + k, 1), :].rearrange("p a b -> p (a b)"), efs[:, k, :]).then_inc(s_efs, 1)
                    loop(v, PAIRS, features)
                    v.wait_ge(s_root, 1)
                    me.done(v.reciprocal(dg_root[:, :], dg_root[:, :]))
                    me.settle()
                    v.tensor_tensor(dg[:, 2, :], dg_root[:, :], dg[:, 0, :], ALU.mult).then_inc(s_dg, 1)
            end_phase()

        def one_group(groups, g):
            return groups[:, bass.ds(g, 1), :, :].rearrange("p g u k -> p (g u) k")

        def edge_row(src, g):
            return src.rearrange("(a n) -> a n", a=1)[:, bass.ds(g * GE, GE)].to_broadcast([EP, GE])

        with ExitStack() as c:
            X = [sb(f"l0_x{k}", [EP, GT, D], c=c) for k in range(2)]
            MSG = [sb(f"l0_msg{k}", [EP, GT, D], c=c) for k in range(2)]
            TOT = [sb(f"l0_tot{k}", [EP, GT, D], c=c) for k in range(2)]
            S = [sb(f"l0_same{k}", [EP, GT, GE], c=c) for k in range(2)]
            ROW = [sb(f"l0_row{k}", [EP, GE], I32, c) for k in range(2)]
            earlier = sb("l0_earlier", [EP, GT, GE], c=c)
            scrap = sb("l0_scrap", [EP, GT, GE], c=c)
            idx = [sb(f"l0_idx{k}", [EP, 2, GT], I32, c) for k in range(2)]
            dis = [sb(f"l0_dis{k}", [EP, 2, GT], c=c) for k in range(2)]
            to = [sb(f"l0_to{k}", [EP, GT], I32, c) for k in range(2)]
            spare_i = sb("l0_spare_i", [EP, GT], I32, c)
            spare = sb("l0_spare", [EP, GT], c=c)
            dup = sb("l0_dup", [EP, GT], c=c)
            off = sb("l0_off", [EP, 2, GT], c=c)
            fac = [sb(f"l0_fac{k}", [EP, 3, GT], c=c) for k in range(2)]
            norm = Norm("l0", c, EP, GT)
            ptot = [pb(f"l0_ptot{k}", [EP, 512], c) for k in range(2)]

            s_fill, s_cst, s_vs = sem("l0_filled"), sem("l0_consts"), sem("l0_steps")
            s_row, s_staged, s_gat = two("l0_rows_loaded"), sem("l0_indices_staged"), two("l0_gathered")
            s_same, s_fac, s_msg, s_sum = sem("l0_same_ready"), sem("l0_factors_ready"), sem("l0_messages_ready"), sem("l0_summed")
            s_tot, s_to, s_sent = sem("l0_totals_ready"), sem("l0_targets_ready"), sem("l0_added")
            PER_G = 16 * 3 * GT

            with nc.Block() as block:
                @block.sync
                def _(sp):
                    def rows(t):
                        for k in range(2):
                            g = 2 * t + k
                            if started(t):
                                sp.wait_ge(s_same, g - 1)
                            sp.dma_start(ROW[k][:, :], edge_row(A["src"], g)).then_inc(s_row[k], 16)
                    loop(sp, PAIRS, rows)

                @block.gpsimd
                def _(pool):
                    pool.memset(earlier[:, :, :], 1.0).then_inc(s_fill, 1)
                    pool.iota(spare_i[:, :], pattern=[[EP, GT]], base=N, channel_multiplier=1).then_inc(s_cst, 1)
                    pool.wait_ge(s_fill, 1)
                    pool.affine_select(out=earlier[:, :, :], in_=earlier[:, :, :], compare_op=ALU.is_gt, fill=0.0,
                                       base=0, pattern=[[EP, GT], [-1, GE]], channel_multiplier=1).then_inc(s_cst, 1)
                    pool.wait_ge(x1_ready, 16 * 17)

                    def gathers(g, k):
                        pool.wait_ge(s_staged, g + 1)
                        seen(pool)
                        for u in range(GT):
                            pool.indirect_dma_start(X[k][:, u, :], None, A["x"], bass.IndirectOffsetOnAxis(ap=idx[k][:, 0, u:u + 1], axis=0)).then_inc(s_gat[k], 16)
                            for h in range(2):
                                pool.indirect_dma_start(dis[k][:, h, u:u + 1], None, dis_table, bass.IndirectOffsetOnAxis(ap=idx[k][:, h, u:u + 1], axis=0)).then_inc(s_gat[k], 16)

                    def adds(g, k):
                        pool.wait_ge(s_tot, g + 1)
                        seen(pool)
                        if not (isinstance(g, int) and g == 0):
                            pool.wait_ge(s_sent, 16 * GT * g)
                            seen(pool)
                        for u in range(GT):
                            pool.indirect_dma_start(x1, bass.IndirectOffsetOnAxis(ap=to[k][:, u:u + 1], axis=0), TOT[k][:, u, :], None,
                                                    compute_op=ALU.add).then_inc(s_sent, 16)

                    def body(t):
                        gathers(2 * t, 0)
                        if started(t):
                            adds(2 * t - 1, 1)
                        gathers(2 * t + 1, 1)
                        adds(2 * t, 0)
                    loop(pool, PAIRS, body)
                    adds(GR - 1, 1)
                    pool.wait_ge(s_sent, 16 * GT * GR)

                @block.scalar
                def _(act):
                    def body(t):
                        for k in range(2):
                            g = 2 * t + k
                            norm.root(act, g + 1, EP, GT)
                            act.wait_ge(s_fac, g + 1)
                            if started(t):
                                act.wait_ge(s_sum, g - 1)
                            for u in range(GT):
                                last = act.activation(MSG[k][:, u, :], X[k][:, u, :], ACT.Relu,
                                                      bias=fac[k][:, 2, u:u + 1], scale=fac[k][:, 1, u:u + 1])
                            last.then_inc(s_msg, 1)
                            act.wait_ge(s_sum, g + 1)
                            if started(t):
                                act.wait_ge(s_sent, 16 * GT * (g - 1))
                            act.activation(TOT[k][:, :, :], ptot[k][:, 0:GT * D].rearrange("p (u d) -> p u d", u=GT), ACT.Copy).then_inc(s_tot, 1)
                    loop(act, PAIRS, body)

                @block.tensor
                def _(pe):
                    def body(t):
                        for k in range(2):
                            g = 2 * t + k
                            pe.wait_ge(s_msg, g + 1)
                            pe.wait_ge(s_same, g + 1)
                            if started(t):
                                pe.wait_ge(s_tot, g - 1)
                            for i in range(GT):
                                for j in range(GT):
                                    last = pe.matmul(ptot[k][:, i * D:(i + 1) * D], S[k][:, j, i * EP:(i + 1) * EP], MSG[k][:, j, :],
                                                     start=(j == 0), stop=(j == GT - 1))
                            last.then_inc(s_sum, 1)
                    loop(pe, PAIRS, body)

                @block.vector
                def _(v):
                    me = Steps(v, s_vs)
                    v.wait_ge(s_cst, 2)
                    me.done(v.tensor_copy(spare[:, :], spare_i[:, :]))

                    def stage(g, k):
                        v.tensor_copy(idx[k][:, 0, :], dst_i[:, bass.ds(GT * g, GT)])
                        v.tensor_copy(idx[k][:, 1, :], src_i[:, bass.ds(GT * g, GT)]).then_inc(s_staged, 1)
                    stage(0, 0)

                    def body(t):
                        for k in range(2):
                            g = 2 * t + k
                            stage(g + 1, 1 - k)
                            v.wait_ge(s_row[k], 16 * t + 16)
                            if started(t):
                                v.wait_ge(s_sum, g - 1)
                            for a in range(GT):
                                last = v.tensor_scalar(S[k][:, a, :], ROW[k][:, :], src_f[:, bass.ds(GT * g + a, 1)], None, ALU.is_equal)
                            me.done(last)
                            me.settle()
                            v.sem_inc(s_same, 1)
                            for a in range(GT):
                                me.done(v.scalar_tensor_tensor(scrap[:, a, :], S[k][:, a, :], 1.0, earlier[:, a, :], ALU.mult, ALU.mult,
                                                               accum_out=dup[:, a:a + 1]))
                            me.done(v.tensor_tensor(off[:, 0, :], spare[:, :], src_f[:, bass.ds(GT * g, GT)], ALU.subtract))
                            me.settle()
                            me.done(v.scalar_tensor_tensor(off[:, 1, :], dup[:, :], 1.0, off[:, 0, :], ALU.min, ALU.mult))
                            me.settle()
                            if started(t):
                                v.wait_ge(s_sent, 16 * GT * (g - 1))
                            me.done(v.tensor_tensor(to[k][:, :], off[:, 1, :], src_f[:, bass.ds(GT * g, GT)], ALU.add))
                            v.wait_ge(s_gat[k], PER_G * t + PER_G)
                            norm.stats(v, me, X[k], EP, GT)
                            me.done(v.tensor_tensor(fac[k][:, 0, :], dis[k][:, 0, :], dis[k][:, 1, :], ALU.mult))
                            norm.invert(v, me, g + 1, EP, GT)
                            me.done(v.tensor_tensor(fac[k][:, 1, :], fac[k][:, 0, :], norm.rstd[:, :], ALU.mult))
                            me.settle()
                            v.scalar_tensor_tensor(fac[k][:, 2, :], norm.mean[:, :], -1.0, fac[k][:, 1, :], ALU.mult, ALU.mult).then_inc(s_fac, 1)
                            v.wait_ge(s_msg, g + 1)
                    loop(v, PAIRS, body, me)
            end_phase()

        def carry_block(U, width, tag):
            with ExitStack() as c:
                pc = pb(f"{tag}_pc", [TC, 2, 512], c)
                s_t, s_c, s_e = sem(f"{tag}_tails_loaded"), sem(f"{tag}_carried"), sem(f"{tag}_carry_ready")
                with nc.Block() as block:
                    @block.sync
                    def _(sp):
                        for h in range(2):
                            sp.dma_start(tails[:, h, 0:width], U[EP - 1:EP, h * TC:(h + 1) * TC, 0:width]).then_inc(s_t, 16)
                        sp.wait_ge(s_t, 32)

                    @block.tensor
                    def _(pe):
                        pe.wait_ge(s_t, 32)
                        for h in range(2):
                            for j in range(2):
                                last = pe.matmul(pc[:, h, 0:width], joins[:, j, h * TC:(h + 1) * TC], tails[:, j, 0:width],
                                                 start=(j == 0), stop=(j == 1))
                        last.then_inc(s_c, 1)

                    @block.scalar
                    def _(act):
                        act.wait_ge(s_c, 1)
                        act.activation(carry[:, :, 0:width], pc[:, :, 0:width], ACT.Copy).then_inc(s_e, 1)
                end_phase()

        class Totals:

            def __init__(self, tag, c, width):
                self.w = width
                self.pick = [sb(f"{tag}_pick{k}", [TC, 2, GT, EP], c=c) for k in range(2)]
                self.pcar = [pb(f"{tag}_pcar{k}", [EP, 512], c) for k in range(2)]
                self.s_pick, self.s_car, self.s_used = sem(f"{tag}_picked"), sem(f"{tag}_carries_placed"), sem(f"{tag}_carries_used")

            def vector(self, v, t, k):
                g = 2 * t + k
                if started(t):
                    v.wait_ge(self.s_car, g - 1)
                for h in range(2):
                    for u in range(GT):
                        last = v.tensor_scalar(self.pick[k][:, h, u, :], first_row[:, h, :], tile_sel[:, h, bass.ds(GT * g + u, 1)], None, ALU.mult)
                last.then_inc(self.s_pick, 1)

            def tensor(self, pe, t, k):
                g = 2 * t + k
                pe.wait_ge(self.s_pick, g + 1)
                if started(t):
                    pe.wait_ge(self.s_used, g - 1)
                for u in range(GT):
                    for h in range(2):
                        last = pe.matmul(self.pcar[k][:, u * self.w:(u + 1) * self.w], self.pick[k][:, h, u, :], carry[:, h, 0:self.w],
                                         start=(h == 0), stop=(h == 1))
                last.then_inc(self.s_car, 1)

            def add(self, v, t, k, U, to):
                g = 2 * t + k
                v.wait_ge(self.s_car, g + 1)
                return v.tensor_tensor(to, U[:, bass.ds(GT * g, GT), 0:self.w],
                                       self.pcar[k][:, 0:GT * self.w].rearrange("p (u d) -> p u d", u=GT), ALU.add).then_inc(self.s_used, 1)

        lo = ExitStack()
        U = sb("l1_U", [EP, ET, D], c=lo)
        with ExitStack() as c:
            X = [sb(f"l1_x{k}", [EP, GT, D], c=c) for k in range(2)]
            C = [sb(f"l1_c{k}", [EP, GT, D], c=c) for k in range(2)]
            MSG = [sb(f"l1_msg{k}", [EP, GT, D], c=c) for k in range(2)]
            EA = [sb(f"l1_ea{k}", [EP, GT, 18], c=c) for k in range(2)]
            EAT = [sb(f"l1_eat{k}", [18, GE], c=c) for k in range(2)]
            HT = [sb(f"l1_ht{k}", [D + 1, GE], c=c) for k in range(2)]
            ST = [sb(f"l1_st{k}", [D, GE], c=c) for k in range(2)]
            S = [sb(f"l1_same{k}", [EP, GT, EP], c=c) for k in range(2)]
            ROW = [sb(f"l1_row{k}", [EP, GE], I32, c) for k in range(2)]
            idx = [sb(f"l1_idx{k}", [EP, GT], I32, c) for k in range(2)]
            norm = Norm("l1", c, EP, GT)
            pT = [pb(f"l1_pt{k}", [128, 512], c) for k in range(2)]
            pW = [pb(f"l1_pw{k}", [128, 512], c) for k in range(2)]
            pS = [pb(f"l1_ps{k}", [128, 512], c) for k in range(2)]
            pU = [pb(f"l1_pu{k}", [128, 512], c) for k in range(2)]
            s_one, s_vs = sem("l1_ones"), sem("l1_steps")
            s_row, s_ea, s_staged, s_gat = two("l1_rows_loaded"), two("l1_attr_loaded"), sem("l1_staged"), two("l1_gathered")
            s_same, s_c, s_msg = sem("l1_same_ready"), sem("l1_normed"), sem("l1_messages_ready")
            s_at, s_atc, s_h, s_hc, s_w = sem("l1_attr_turned"), sem("l1_attr_copied"), sem("l1_hidden"), sem("l1_hidden_copied"), sem("l1_weights_made")
            s_sum, s_sumc, s_u, s_uc = sem("l1_summed"), sem("l1_sums_copied"), sem("l1_multiplied"), sem("l1_kept")
            ea_groups = A["edge_attr_17"].rearrange("(g u p) k -> p g u k", u=GT, p=EP)

            with nc.Block() as block:
                @block.sync
                def _(sp):
                    sp.wait_ge(s_one, 4)

                    def body(t):
                        for k in range(2):
                            g = 2 * t + k
                            if started(t):
                                sp.wait_ge(s_same, g - 1)
                                sp.wait_ge(s_at, g - 1)
                            sp.dma_start(ROW[k][:, :], edge_row(A["dst"], g)).then_inc(s_row[k], 16)
                            sp.dma_start(EA[k][:, :, 0:17], ea_groups[:, bass.ds(g, 1), :, :].rearrange("p g u k -> p (g u) k")).then_inc(s_ea[k], 16)
                    loop(sp, PAIRS, body)

                @block.gpsimd
                def _(pool):
                    def body(t):
                        for k in range(2):
                            pool.wait_ge(s_staged, 2 * t + k + 1)
                            seen(pool)
                            for u in range(GT):
                                pool.indirect_dma_start(X[k][:, u, :], None, x1, bass.IndirectOffsetOnAxis(ap=idx[k][:, u:u + 1], axis=0)).then_inc(s_gat[k], 16)
                    loop(pool, PAIRS, body)

                @block.scalar
                def _(act):
                    def body(t):
                        for k in range(2):
                            g = 2 * t + k
                            act.wait_ge(s_at, g + 1)
                            act.activation(EAT[k][:, :], pT[k][0:18, 0:GE], ACT.Copy).then_inc(s_atc, 1)
                            act.wait_ge(s_h, g + 1)
                            act.activation(HT[k][0:D, :], pT[k][0:D, 0:GE], ACT.Relu).then_inc(s_hc, 1)
                            norm.root(act, g + 1, EP, GT)
                            act.wait_ge(s_sum, g + 1)
                            act.activation(ST[k][:, :], pS[k][0:D, 0:GE], ACT.Copy).then_inc(s_sumc, 1)
                            act.wait_ge(s_u, g + 1)
                            act.activation(U[:, bass.ds(GT * g, GT), :], pU[k][0:EP, 0:GT * D].rearrange("p (u d) -> p u d", u=GT), ACT.Copy).then_inc(s_uc, 1)
                    loop(act, PAIRS, body)

                @block.tensor
                def _(pe):
                    pe.wait_ge(s_one, 4)

                    def body(t):
                        for k in range(2):
                            g = 2 * t + k
                            pe.wait_ge(s_ea[k], 16 * t + 16)
                            if started(t):
                                pe.wait_ge(s_hc, g - 1)
                            for u in range(GT):
                                last = pe.transpose(pT[k][0:18, u * EP:(u + 1) * EP], EA[k][:, u, :], ident[0:EP, 0:EP])
                            last.then_inc(s_at, 1)
                            pe.wait_ge(s_atc, g + 1)
                            pe.matmul(pT[k][0:D, 0:GE], W1T[:, :], EAT[k][:, :], start=True, stop=True).then_inc(s_h, 1)
                            pe.wait_ge(s_hc, g + 1)
                            if started(t):
                                pe.wait_ge(s_msg, g - 1)
                            for u in range(GT):
                                last = pe.matmul(pW[k][0:EP, u * D:(u + 1) * D], HT[k][:, u * EP:(u + 1) * EP], W2T[:, :], start=True, stop=True)
                            last.then_inc(s_w, 1)
                            pe.wait_ge(s_same, g + 1)
                            pe.wait_ge(s_msg, g + 1)
                            if started(t):
                                pe.wait_ge(s_sumc, g - 1)
                            for u in range(GT):
                                last = pe.matmul(pS[k][0:D, u * EP:(u + 1) * EP], MSG[k][:, u, :], S[k][:, u, :], start=True, stop=True)
                            last.then_inc(s_sum, 1)
                            pe.wait_ge(s_sumc, g + 1)
                            if started(t):
                                pe.wait_ge(s_uc, g - 1)
                            for u in range(GT):
                                last = pe.matmul(pU[k][0:EP, u * D:(u + 1) * D], ST[k][:, u * EP:(u + 1) * EP], WnT[:, :], start=True, stop=True)
                            last.then_inc(s_u, 1)
                    loop(pe, PAIRS, body)

                @block.vector
                def _(v):
                    me = Steps(v, s_vs)
                    for k in range(2):
                        v.memset(EA[k][:, :, 17:18], 1.0).then_inc(s_one, 1)
                        v.memset(HT[k][D:D + 1, :], 1.0).then_inc(s_one, 1)

                    def stage(g, k):
                        v.tensor_copy(idx[k][:, :], src_i[:, bass.ds(GT * g, GT)]).then_inc(s_staged, 1)
                    stage(0, 0)

                    def body(t):
                        for k in range(2):
                            g = 2 * t + k
                            stage(g + 1, 1 - k)
                            v.wait_ge(s_row[k], 16 * t + 16)
                            if started(t):
                                v.wait_ge(s_sum, g - 1)
                            for u in range(GT):
                                last = v.tensor_scalar(S[k][:, u, :], ROW[k][:, u * EP:(u + 1) * EP], dst_f[:, bass.ds(GT * g + u, 1)], None, ALU.is_equal)
                            last.then_inc(s_same, 1)
                            v.wait_ge(s_gat[k], 64 * t + 64)
                            norm.stats(v, me, X[k], EP, GT)
                            norm.invert(v, me, g + 1, EP, GT)
                            for u in range(GT):
                                me.done(v.tensor_scalar(C[k][:, u, :], X[k][:, u, :], norm.mean[:, u:u + 1], norm.rstd[:, u:u + 1], ALU.subtract, ALU.mult))
                            me.settle()
                            v.wait_ge(s_w, g + 1)
                            v.scalar_tensor_tensor(MSG[k][:, :, :], C[k][:, :, :], 0.0, pW[k][0:EP, 0:GT * D].rearrange("p (u d) -> p u d", u=GT),
                                                   ALU.max, ALU.mult).then_inc(s_msg, 1)
                    loop(v, PAIRS, body, me)
            end_phase()

        carry_block(U, D, "l1")

        with ExitStack() as c:
            tot = Totals("l1b", c, D)
            H = [sb(f"l1b_h{k}", [EP, GT, D], c=c) for k in range(2)]
            idx = [sb(f"l1b_idx{k}", [EP, GT], I32, c) for k in range(2)]
            s_put, s_h = two("l1b_stored"), sem("l1b_totals_ready")
            with nc.Block() as block:
                @block.gpsimd
                def _(pool):
                    pool.wait_ge(agg1_ready, 32)
                    top = pool.to_reg(N - 1)

                    def body(t):
                        for k in range(2):
                            pool.wait_ge(s_h, 2 * t + k + 1)
                            seen(pool)
                            for u in range(GT):
                                pool.indirect_dma_start(agg1, bass.IndirectOffsetOnAxis(ap=idx[k][:, u:u + 1], axis=0), H[k][:, u, :], None,
                                                        bounds_check=top, oob_is_err=False).then_inc(s_put[k], 16)
                    loop(pool, PAIRS, body)
                    for k in range(2):
                        pool.wait_ge(s_put[k], 64 * PAIRS)

                @block.tensor
                def _(pe):
                    def body(t):
                        for k in range(2):
                            tot.tensor(pe, t, k)
                    loop(pe, PAIRS, body)

                @block.vector
                def _(v):
                    def body(t):
                        for k in range(2):
                            tot.vector(v, t, k)
                            if started(t):
                                v.wait_ge(s_put[k], 64 * t)
                            v.tensor_copy(idx[k][:, :], end_i[:, bass.ds(GT * (2 * t + k), GT)])
                            tot.add(v, t, k, U, H[k][:, :, :])
                            v.wait_ge(tot.s_used, 2 * t + k + 1)
                            v.sem_inc(s_h, 1)
                    loop(v, PAIRS, body)
            end_phase()
        lo.close()

        def block_view(table, b, P, G, n=None):
            if isinstance(b, int):
                rows = table[BLK * b:BLK * b + P * G, :]
            else:
                rows = table[bass.ds(BLK * b, P * G), :]
            return rows.rearrange("(p g) f -> p (g f)", g=G)

        def halves(G):
            return [(0, 4), (4, G - 4)]

        with ExitStack() as c:
            X = [sb(f"n1_x{k}", [NP, NG, D], c=c) for k in range(2)]
            AG = [sb(f"n1_ag{k}", [NP, NG, D], c=c) for k in range(2)]
            X2 = [sb(f"n1_x2{k}", [NP, NG, D], c=c) for k in range(2)]
            C1 = [sb(f"n1_c1{k}", [NP, NG, D], c=c) for k in range(2)]
            C2 = [sb(f"n1_c2{k}", [NP, NG, D], c=c) for k in range(2)]
            ZA = [sb(f"n1_za{k}", [NP, NG, D], c=c) for k in range(2)]
            H1 = [sb(f"n1_h1{k}", [D + 1, NG, NP], c=c) for k in range(2)]
            H2 = [sb(f"n1_h2{k}", [D, NG, NP], c=c) for k in range(2)]
            F = [sb(f"n1_f{k}", [D, NG, NP], c=c) for k in range(2)]
            norm1, norm2 = Norm("n1a", c, NP, NG), Norm("n1b", c, NP, NG)
            pT1 = pb("n1_pt1", [D, 2, 512], c)
            pZ = pb("n1_pz", [NP, 2, 512], c)
            pT2 = pb("n1_pt2", [D, 2, 512], c)
            pF = pb("n1_pf", [D, 2, 512], c)
            s_one, s_vs = sem("n1_ones"), sem("n1_steps")
            s_x, s_a, s_st = two("n1_x_loaded"), two("n1_agg_loaded"), two("n1_stored")
            s_c1, s_t1, s_h1, s_z, s_zr, s_x2 = (sem(f"n1_{n}") for n in ("c1_ready", "c1_turned", "h1_ready", "z_made", "z_read", "x2_ready"))
            s_c2, s_t2, s_h2, s_f, s_fr, s_fs = (sem(f"n1_{n}") for n in ("c2_ready", "c2_turned", "h2_ready", "f_made", "f_relu", "f_counted"))

            def shape(b):
                return (TAILP, TAILG) if isinstance(b, int) and b == FULL else (NP, NG)

            def pairs(eng, body, me=None):
                def last(t):
                    body(t)
                loop(eng, BPAIRS, body, me, last)

            with nc.Block() as block:
                @block.sync
                def _(sp):
                    def body(t):
                        for k in range(2):
                            b = 2 * t + k
                            P, G = shape(b)
                            if started(t):
                                sp.wait_ge(s_x2, b - 1)
                            sp.dma_start(X[k][0:P, 0:G, :].rearrange("p g f -> p (g f)"), block_view(x1, b, P, G)).then_inc(s_x[k], 16)
                            sp.dma_start(AG[k][0:P, 0:G, :].rearrange("p g f -> p (g f)"), block_view(agg1, b, P, G)).then_inc(s_a[k], 16)
                    pairs(sp, body)

                @block.gpsimd
                def _(pool):
                    def body(t):
                        for k in range(2):
                            b = 2 * t + k
                            P, G = shape(b)
                            pool.wait_ge(s_x2, b + 1)
                            seen(pool)
                            pool.dma_start(block_view(x2, b, P, G), X2[k][0:P, 0:G, :].rearrange("p g f -> p (g f)")).then_inc(s_st[k], 16)
                    pairs(pool, body)
                    for k in range(2):
                        pool.wait_ge(s_st[k], 16 * BPAIRS)

                @block.scalar
                def _(act):
                    def body(t):
                        for k in range(2):
                            b = 2 * t + k
                            P, G = shape(b)
                            norm1.root(act, b + 1, P, G)
                            act.wait_ge(s_t1, b + 1)
                            if started(t):
                                act.wait_ge(s_z, b - 1)
                            for h, (g0, n) in enumerate(halves(G)):
                                last = act.activation(H1[k][0:D, g0:g0 + n, 0:P], pT1[:, h, 0:n * P].rearrange("p (g n) -> p g n", g=n), ACT.Relu)
                            last.then_inc(s_h1, 1)
                            norm2.root(act, b + 1, P, G)
                            act.wait_ge(s_t2, b + 1)
                            if started(t):
                                act.wait_ge(s_f, b - 1)
                            for h, (g0, n) in enumerate(halves(G)):
                                last = act.activation(H2[k][:, g0:g0 + n, 0:P], pT2[:, h, 0:n * P].rearrange("p (g n) -> p g n", g=n), ACT.Relu)
                            last.then_inc(s_h2, 1)
                            act.wait_ge(s_f, b + 1)
                            if started(t):
                                act.wait_ge(s_fs, b - 1)
                            for h, (g0, n) in enumerate(halves(G)):
                                last = act.activation(F[k][:, g0:g0 + n, 0:P], pF[:, h, 0:n * P].rearrange("p (g n) -> p g n", g=n), ACT.Relu,
                                                      bias=cols[:, B_NODE:B_NODE + 1])
                            last.then_inc(s_fr, 1)
                    pairs(act, body)

                @block.tensor
                def _(pe):
                    pe.wait_ge(s_one, 2)

                    def body(t):
                        for k in range(2):
                            b = 2 * t + k
                            P, G = shape(b)
                            not_first = started(t) or k > 0
                            pe.wait_ge(s_c1, b + 1)
                            if not_first:
                                pe.wait_ge(s_h1, b)
                            for g in range(G):
                                last = pe.transpose(pT1[:, g // 4, (g % 4) * P:(g % 4 + 1) * P], C1[k][0:P, g, :], ident[0:P, 0:P])
                            last.then_inc(s_t1, 1)
                            pe.wait_ge(s_h1, b + 1)
                            if not_first:
                                pe.wait_ge(s_zr, b)
                            for g in range(G):
                                last = pe.matmul(pZ[0:P, g // 4, (g % 4) * D:(g % 4 + 1) * D], H1[k][:, g, 0:P], WsT[:, :], start=True, stop=True)
                            last.then_inc(s_z, 1)
                            pe.wait_ge(s_c2, b + 1)
                            if not_first:
                                pe.wait_ge(s_h2, b)
                            for g in range(G):
                                last = pe.transpose(pT2[:, g // 4, (g % 4) * P:(g % 4 + 1) * P], C2[k][0:P, g, :], ident[0:P, 0:P])
                            last.then_inc(s_t2, 1)
                            pe.wait_ge(s_h2, b + 1)
                            if not_first:
                                pe.wait_ge(s_fr, b)
                            for h, (g0, n) in enumerate(halves(G)):
                                last = pe.matmul(pF[:, h, 0:n * P], Wnode[0:D, :], H2[k][:, g0:g0 + n, 0:P], start=True, stop=True)
                            last.then_inc(s_f, 1)
                    pairs(pe, body)

                @block.vector
                def _(v):
                    me = Steps(v, s_vs)
                    for k in range(2):
                        v.memset(H1[k][D:D + 1, :, :], 1.0).then_inc(s_one, 1)

                    def body(t):
                        for k in range(2):
                            b = 2 * t + k
                            P, G = shape(b)
                            at = bass.ds(b, 1) if not isinstance(b, int) else slice(b, b + 1)
                            mean = mean_n[0:P, at, 0:G].rearrange("p a g -> p (a g)")
                            rstd = rstd_n[0:P, at, 0:G].rearrange("p a g -> p (a g)")
                            v.wait_ge(s_x[k], 16 * t + 16)
                            norm1.stats(v, me, X[k], P, G)
                            norm1.invert(v, me, b + 1, P, G)
                            if started(t):
                                v.wait_ge(s_t1, b - 1)
                            for g in range(G):
                                last = v.tensor_scalar(C1[k][0:P, g, :], X[k][0:P, g, :], norm1.mean[0:P, g:g + 1], norm1.rstd[0:P, g:g + 1],
                                                       ALU.subtract, ALU.mult)
                            last.then_inc(s_c1, 1)
                            v.wait_ge(s_a[k], 16 * t + 16)
                            v.wait_ge(s_z, b + 1)
                            for h, (g0, n) in enumerate(halves(G)):
                                last = v.tensor_tensor(ZA[k][0:P, g0:g0 + n, :], pZ[0:P, h, 0:n * D].rearrange("p (g f) -> p g f", g=n),
                                                       AG[k][0:P, g0:g0 + n, :], ALU.add)
                            last.then_inc(s_zr, 1)
                            v.wait_ge(s_zr, b + 1)
                            if started(t):
                                v.wait_ge(s_st[k], 16 * t)
                            v.scalar_tensor_tensor(X2[k][0:P, 0:G, :], ZA[k][0:P, 0:G, :], 0.0, X[k][0:P, 0:G, :], ALU.max, ALU.add).then_inc(s_x2, 1)
                            v.wait_ge(s_x2, b + 1)
                            norm2.stats(v, me, X2[k], P, G, mean=mean)
                            norm2.invert(v, me, b + 1, P, G, rstd=norm2.rstd[0:P, 0:G])
                            me.done(v.tensor_copy(rstd, norm2.rstd[0:P, 0:G]))
                            me.done(v.tensor_copy(norm2.mean[0:P, 0:G], mean))
                            me.settle()
                            if started(t):
                                v.wait_ge(s_t2, b - 1)
                            for g in range(G):
                                last = v.tensor_scalar(C2[k][0:P, g, :], X2[k][0:P, g, :], norm2.mean[0:P, g:g + 1], norm2.rstd[0:P, g:g + 1],
                                                       ALU.subtract, ALU.mult)
                            last.then_inc(s_c2, 1)
                            v.wait_ge(s_fr, b + 1)
                            for h, (g0, n) in enumerate(halves(G)):
                                if P == NP:
                                    f = F[k][:, g0:g0 + n, :].rearrange("p g n -> p (g n)")
                                else:
                                    f = F[k][:, g0:g0 + n, 0:P]
                                last = v.bn_stats(f_stats[:, bass.ds(2 * b + h, 1), :].rearrange("p a s -> p (a s)"), f)
                            last.then_inc(s_fs, 1)
                    pairs(v, body, me)
            end_phase()

        def fold(v, me, stats, n, g, beta, ac, root, root_ready, turn):
            me.done(v.bn_aggr(bn_w[:, 0:2], stats))
            me.settle()
            me.done(v.tensor_scalar(bn_w[:, 2:3], bn_w[:, 1:2], BN_EPS, None, ALU.add))
            me.settle()
            v.sem_inc(root, 1)
            v.wait_ge(root_ready, turn)
            me.done(v.reciprocal(bn_w[:, 3:4], bn_w[:, 3:4]))
            me.settle()
            me.done(v.tensor_tensor(ac[:, 0:1], bn_w[:, 3:4], cols[:, g:g + 1], ALU.mult))
            me.settle()
            me.done(v.tensor_tensor(bn_w[:, 2:3], bn_w[:, 0:1], ac[:, 0:1], ALU.mult))
            me.settle()
            me.done(v.tensor_tensor(ac[:, 1:2], cols[:, beta:beta + 1], bn_w[:, 2:3], ALU.subtract))
            me.settle()

        def affine_rows(pe, p, ac, done):
            for j in range(2):
                last = pe.matmul(p[:, j * D:(j + 1) * D], ac[:, j:j + 1].to_broadcast([D, NP]), ident[0:D, 0:D], start=True, stop=True)
            last.then_inc(done, 1)

        with ExitStack() as c:
            pA = pb("bn_pa", [NP, 512], c)
            pB = pb("bn_pb", [D, 512], c)
            s_vs, s_var, s_root, s_ac, s_mm, s_bias = (sem(f"bn_{n}") for n in ("steps", "var_ready", "root_ready", "folded", "multiplied", "rows_kept"))
            with nc.Block() as block:
                @block.scalar
                def _(act):
                    for n in range(2):
                        act.wait_ge(s_var, n + 1)
                        act.activation(bn_w[:, 3:4], bn_w[:, 2:3], ACT.Sqrt).then_inc(s_root, 1)

                @block.vector
                def _(v):
                    me = Steps(v, s_vs)
                    fold(v, me, f_stats[:, :, :].rearrange("p a s -> p (a s)"), 0, G_NODE, BETA_NODE, node_ac, s_var, s_root, 1)
                    fold(v, me, e_stats[:, :, :].rearrange("p a s -> p (a s)"), 0, G_EDGE, BETA_EDGE, edge_ac, s_var, s_root, 2)
                    me.done(v.tensor_scalar(Wc[:, :], Wmsg[:, 2, :], edge_ac[:, 0:1], None, ALU.mult))
                    me.settle()
                    v.sem_inc(s_ac, 1)
                    v.wait_ge(s_mm, 2)
                    me.done(v.tensor_copy(affine[:, 0:2, :], pA[:, 0:2 * D].rearrange("p (a f) -> p a f", a=2)))
                    me.done(v.tensor_tensor(msg_bias[:, :], pB[:, 0:1], cols[:, B_MSG:B_MSG + 1], ALU.add))
                    me.settle()

                @block.tensor
                def _(pe):
                    pe.wait_ge(s_ac, 1)
                    affine_rows(pe, pA, node_ac, s_mm)
                    pe.matmul(pB[:, 0:1], Wmsg[:, 2, :], edge_ac[:, 1:2], start=True, stop=True).then_inc(s_mm, 1)
            end_phase()

        with ExitStack() as c:
            X = [sb(f"n2_x{k}", [NP, NG, D], c=c) for k in range(2)]
            XC = [sb(f"n2_xc{k}", [NP, NG, D], c=c) for k in range(2)]
            C2 = [sb(f"n2_c{k}", [NP, NG, D], c=c) for k in range(2)]
            Y = [sb(f"n2_y{k}", [NP, NG, D], c=c) for k in range(2)]
            O = [sb(f"n2_o{k}", [NP, NG, D], c=c) for k in range(2)]
            H2 = [sb(f"n2_h{k}", [D + 1, NG, NP], c=c) for k in range(2)]
            mr = [sb(f"n2_mr{k}", [NP, 2, NG], c=c) for k in range(2)]
            pT = [pb(f"n2_pt{k}", [D, 2, 512], c) for k in range(2)]
            pZ = [pb(f"n2_pz{k}", [NP, 2, 512], c) for k in range(2)]
            s_one, s_vs, s_x, s_st = sem("n2_ones"), sem("n2_steps"), two("n2_x_loaded"), two("n2_stored")
            s_c, s_t, s_h, s_z, s_y, s_xc, s_o = (sem(f"n2_{n}") for n in ("c_ready", "c_turned", "h_ready", "z_made", "y_ready", "xc_ready", "o_ready"))

            with nc.Block() as block:
                @block.sync
                def _(sp):
                    def body(t):
                        for k in range(2):
                            b = 2 * t + k
                            P, G = shape(b)
                            if started(t):
                                sp.wait_ge(s_c, b - 1)
                                sp.wait_ge(s_xc, b - 1)
                            sp.dma_start(X[k][0:P, 0:G, :].rearrange("p g f -> p (g f)"), block_view(x2, b, P, G)).then_inc(s_x[k], 16)
                    pairs(sp, body)

                @block.gpsimd
                def _(pool):
                    def body(t):
                        for k in range(2):
                            b = 2 * t + k
                            P, G = shape(b)
                            pool.wait_ge(s_x[k], 16 * t + 16)
                            seen(pool)
                            if started(t):
                                pool.wait_ge(s_o, b - 1)
                                seen(pool)
                            pool.tensor_tensor(XC[k][0:P, 0:G, :], X[k][0:P, 0:G, :],
                                               affine[0:P, 1:2, :].to_broadcast([P, G, D]), ALU.add).then_inc(s_xc, 1)
                    pairs(pool, body)

                @block.scalar
                def _(act):
                    def body(t):
                        for k in range(2):
                            b = 2 * t + k
                            P, G = shape(b)
                            act.wait_ge(s_t, b + 1)
                            if started(t):
                                act.wait_ge(s_z, b - 1)
                            for h, (g0, n) in enumerate(halves(G)):
                                last = act.activation(H2[k][0:D, g0:g0 + n, 0:P], pT[k][:, h, 0:n * P].rearrange("p (g n) -> p g n", g=n), ACT.Relu)
                            last.then_inc(s_h, 1)
                            act.wait_ge(s_o, b + 1)
                            act.dma_start(block_view(out, b, P, G), O[k][0:P, 0:G, :].rearrange("p g f -> p (g f)")).then_inc(s_st[k], 16)
                    pairs(act, body)
                    for k in range(2):
                        act.wait_ge(s_st[k], 16 * BPAIRS)

                @block.tensor
                def _(pe):
                    pe.wait_ge(s_one, 2)

                    def body(t):
                        for k in range(2):
                            b = 2 * t + k
                            P, G = shape(b)
                            pe.wait_ge(s_c, b + 1)
                            if started(t):
                                pe.wait_ge(s_h, b - 1)
                            for g in range(G):
                                last = pe.transpose(pT[k][:, g // 4, (g % 4) * P:(g % 4 + 1) * P], C2[k][0:P, g, :], ident[0:P, 0:P])
                            last.then_inc(s_t, 1)
                            pe.wait_ge(s_h, b + 1)
                            if started(t):
                                pe.wait_ge(s_y, b - 1)
                            for g in range(G):
                                last = pe.matmul(pZ[k][0:P, g // 4, (g % 4) * D:(g % 4 + 1) * D], H2[k][:, g, 0:P], Wnode[:, :], start=True, stop=True)
                            last.then_inc(s_z, 1)
                    pairs(pe, body)

                @block.vector
                def _(v):
                    me = Steps(v, s_vs)
                    for k in range(2):
                        v.memset(H2[k][D:D + 1, :, :], 1.0).then_inc(s_one, 1)

                    def centre(b, k, t):
                        P, G = shape(b)
                        at = bass.ds(b, 1) if not isinstance(b, int) else slice(b, b + 1)
                        if started(t):
                            v.wait_ge(s_t, b - 1)
                        me.done(v.tensor_copy(mr[k][0:P, 0, 0:G], mean_n[0:P, at, 0:G].rearrange("p a g -> p (a g)")))
                        me.done(v.tensor_copy(mr[k][0:P, 1, 0:G], rstd_n[0:P, at, 0:G].rearrange("p a g -> p (a g)")))
                        me.settle()
                        v.wait_ge(s_x[k], 16 * t + 16)
                        for g in range(G):
                            last = v.tensor_scalar(C2[k][0:P, g, :], X[k][0:P, g, :], mr[k][0:P, 0, g:g + 1], mr[k][0:P, 1, g:g + 1],
                                                   ALU.subtract, ALU.mult)
                        last.then_inc(s_c, 1)

                    def finish(b, k, t):
                        P, G = shape(b)
                        v.wait_ge(s_z, b + 1)
                        for h, (g0, n) in enumerate(halves(G)):
                            last = v.scalar_tensor_tensor(Y[k][0:P, g0:g0 + n, :], pZ[k][0:P, h, 0:n * D].rearrange("p (g f) -> p g f", g=n), 0.0,
                                                          affine[0:P, 0:1, :].to_broadcast([P, n, D]), ALU.max, ALU.mult)
                        last.then_inc(s_y, 1)
                        v.wait_ge(s_y, b + 1)
                        v.wait_ge(s_xc, b + 1)
                        if started(t):
                            v.wait_ge(s_st[k], 16 * t)
                        v.tensor_tensor(O[k][0:P, 0:G, :], Y[k][0:P, 0:G, :], XC[k][0:P, 0:G, :], ALU.add).then_inc(s_o, 1)

                    def body(t):
                        for k in range(2):
                            centre(2 * t + k, k, t)
                        for k in range(2):
                            finish(2 * t + k, k, t)
                    pairs(v, body, me)
            end_phase()

        hi = ExitStack()
        U = sb("l2_U", [EP, ET, WU], c=hi)
        keep_groups = keep_rows.rearrange("(g u p) k -> p g u k", u=GT, p=EP)
        fd_groups = fd_rows.rearrange("(g u p) k -> p g u k", u=GT, p=EP)
        with ExitStack() as c:
            X = [sb(f"l2_x{k}", [EP, 2 * GT, D], c=c) for k in range(2)]
            C = sb("l2_c", [EP, 2 * GT, D], c=c)
            HT = sb("l2_ht", [D + 1, 2, GE], c=c)
            E4 = [sb(f"l2_e4{k}", [EP, GT, 5], c=c) for k in range(2)]
            E4T = sb("l2_e4t", [5, GE], c=c)
            EF = sb("l2_ef", [D, GE], c=c)
            R = sb("l2_r", [D, GE], c=c)
            RN = sb("l2_rn", [EP, GT, D + 1], c=c)
            FD = sb("l2_fd", [EP, GT, D], c=c)
            S = sb("l2_same", [EP, GT, EP], c=c)
            ROW = [sb(f"l2_row{k}", [EP, GE], I32, c) for k in range(2)]
            idx = [sb(f"l2_idx{k}", [EP, 2, GT], I32, c) for k in range(2)]
            norm = Norm("l2", c, EP, 2 * GT)
            pT = pb("l2_pt", [D, 2, 512], c)
            pE = pb("l2_pe", [D, 512], c)
            pR = pb("l2_pr", [D, 512], c)
            pN = pb("l2_pn", [EP, 512], c)
            pF = pb("l2_pf", [EP, 512], c)
            pU = pb("l2_pu", [EP, 512], c)
            s_one, s_vs = sem("l2_ones"), sem("l2_steps")
            s_row, s_e4, s_gat, s_fdst, s_keep = two("l2_row_loaded"), two("l2_attr_loaded"), two("l2_gathered"), sem("l2_fd_stored"), two("l2_kept")
            s_staged, s_same, s_c = (sem(f"l2_{n}") for n in ("staged", "same_ready", "normed"))
            s_t, s_h, s_et, s_etc, s_ef, s_efc = (sem(f"l2_{n}") for n in ("turned", "h_ready", "attr_turned", "attr_copied", "ef_made", "ef_relu"))
            s_r, s_rr, s_n, s_nc, s_f, s_fc, s_u, s_uc = (sem(f"l2_{n}") for n in ("r_made", "r_relu", "r_turned", "rn_ready", "fd_made", "fd_relu", "summed", "sums_kept"))

            with nc.Block() as block:
                @block.sync
                def _(sp):
                    sp.wait_ge(s_one, 4)

                    def keep(g, k, t):
                        sp.wait_ge(s_gat[k], 128 * t + 128)
                        sp.dma_start(one_group(keep_groups, g), X[k][:, GT:2 * GT, :]).then_inc(s_keep[k], 16)

                    def body(t):
                        for k in range(2):
                            g = 2 * t + k
                            if started(t):
                                sp.wait_ge(s_same, g - 1)
                                sp.wait_ge(s_et, g - 1)
                            sp.dma_start(ROW[k][:, :], edge_row(A["dst"], g)).then_inc(s_row[k], 16)
                            sp.dma_start(E4[k][:, :, 0:4], one_group(e4_groups, g)).then_inc(s_e4[k], 16)
                            if k:
                                keep(g - 1, 0, t)
                            elif started(t):
                                keep(g - 1, 1, t - 1)
                    loop(sp, PAIRS, body)
                    keep(GR - 1, 1, PAIRS - 1)
                    for k in range(2):
                        sp.wait_ge(s_keep[k], 16 * PAIRS)

                @block.gpsimd
                def _(pool):
                    def body(t):
                        for k in range(2):
                            g = 2 * t + k
                            pool.wait_ge(s_staged, g + 1)
                            seen(pool)
                            if started(t):
                                pool.wait_ge(s_c, g - 1)
                                seen(pool)
                                pool.wait_ge(s_keep[k], 16 * t)
                                seen(pool)
                            for h in range(2):
                                for u in range(GT):
                                    pool.indirect_dma_start(X[k][:, h * GT + u, :], None, x2, bass.IndirectOffsetOnAxis(ap=idx[k][:, h, u:u + 1], axis=0)).then_inc(s_gat[k], 16)
                    loop(pool, PAIRS, body)

                @block.scalar
                def _(act):
                    def body(g):
                        act.wait_ge(s_et, g + 1)
                        act.activation(E4T[:, :], pE[0:5, 0:GE], ACT.Copy).then_inc(s_etc, 1)
                        act.wait_ge(s_ef, g + 1)
                        act.activation(EF[:, :], pE[:, 0:GE], ACT.Relu).then_inc(s_efc, 1)
                        norm.root(act, g + 1, EP, 2 * GT)
                        act.wait_ge(s_t, g + 1)
                        act.activation(HT[0:D, :, :], pT[:, :, 0:GE], ACT.Relu).then_inc(s_h, 1)
                        act.wait_ge(s_r, g + 1)
                        act.activation(R[:, :], pR[:, 0:GE], ACT.Relu, bias=msg_bias[:, :]).then_inc(s_rr, 1)
                        act.wait_ge(s_f, g + 1)
                        if started(g):
                            act.wait_ge(s_fdst, 16 * g)
                        act.activation(FD[:, :, :], pF[:, 0:GT * D].rearrange("p (u d) -> p u d", u=GT), ACT.Relu).then_inc(s_fc, 1)
                        act.wait_ge(s_fc, g + 1)
                        act.dma_start(one_group(fd_groups, g), FD[:, :, :]).then_inc(s_fdst, 16)
                        act.wait_ge(s_n, g + 1)
                        act.activation(RN[:, :, 0:D], pN[:, 0:GT * D].rearrange("p (u d) -> p u d", u=GT), ACT.Copy).then_inc(s_nc, 1)
                        act.wait_ge(s_u, g + 1)
                        act.activation(U[:, bass.ds(GT * g, GT), 0:D + 1], pU[:, 0:GT * (D + 1)].rearrange("p (u d) -> p u d", u=GT), ACT.Copy).then_inc(s_uc, 1)
                    loop(act, GR, body)
                    act.wait_ge(s_fdst, 16 * GR)

                @block.tensor
                def _(pe):
                    pe.wait_ge(s_one, 4)

                    def group(g, k, t):
                        pe.wait_ge(s_e4[k], 16 * t + 16)
                        if started(t) or k:
                            pe.wait_ge(s_efc, g)
                        for u in range(GT):
                            last = pe.transpose(pE[0:5, u * EP:(u + 1) * EP], E4[k][:, u, :], ident[0:EP, 0:EP])
                        last.then_inc(s_et, 1)
                        pe.wait_ge(s_etc, g + 1)
                        pe.matmul(pE[:, 0:GE], Wedge[:, :], E4T[:, :], start=True, stop=True).then_inc(s_ef, 1)
                        pe.wait_ge(s_c, g + 1)
                        for h in range(2):
                            for u in range(GT):
                                last = pe.transpose(pT[:, h, u * EP:(u + 1) * EP], C[:, h * GT + u, :], ident[0:EP, 0:EP])
                        last.then_inc(s_t, 1)
                        pe.wait_ge(s_h, g + 1)
                        pe.wait_ge(s_efc, g + 1)
                        if started(t) or k:
                            pe.wait_ge(s_rr, g)
                        pe.matmul(pR[:, 0:GE], Wmsg[:, 0, :], HT[0:D, 0, :], start=True, stop=False)
                        pe.matmul(pR[:, 0:GE], Wmsg[:, 1, :], HT[0:D, 1, :], start=False, stop=False)
                        pe.matmul(pR[:, 0:GE], Wc[:, :], EF[:, :], start=False, stop=True).then_inc(s_r, 1)
                        if started(t) or k:
                            pe.wait_ge(s_fc, g)
                        for u in range(GT):
                            last = pe.matmul(pF[:, u * D:(u + 1) * D], HT[:, 1, u * EP:(u + 1) * EP], Wnode[:, :], start=True, stop=True)
                        last.then_inc(s_f, 1)
                        pe.wait_ge(s_rr, g + 1)
                        if started(t) or k:
                            pe.wait_ge(s_nc, g)
                        for u in range(GT):
                            last = pe.transpose(pN[:, u * D:(u + 1) * D], R[:, u * EP:(u + 1) * EP], ident[0:D, 0:D])
                        last.then_inc(s_n, 1)
                        pe.wait_ge(s_nc, g + 1)
                        pe.wait_ge(s_same, g + 1)
                        if started(t) or k:
                            pe.wait_ge(s_uc, g)
                        for u in range(GT):
                            last = pe.matmul(pU[:, u * (D + 1):(u + 1) * (D + 1)], S[:, u, :], RN[:, u, :], start=True, stop=True)
                        last.then_inc(s_u, 1)

                    def body(t):
                        for k in range(2):
                            group(2 * t + k, k, t)
                    loop(pe, PAIRS, body)

                @block.vector
                def _(v):
                    me = Steps(v, s_vs)
                    for k in range(2):
                        v.memset(E4[k][:, :, 4:5], 1.0).then_inc(s_one, 1)
                    v.memset(HT[D:D + 1, :, :], 1.0).then_inc(s_one, 1)
                    v.memset(RN[:, :, D:D + 1], 1.0).then_inc(s_one, 1)

                    def stage(g, k):
                        v.tensor_copy(idx[k][:, 0, :], src_i[:, bass.ds(GT * g, GT)])
                        v.tensor_copy(idx[k][:, 1, :], dst_i[:, bass.ds(GT * g, GT)]).then_inc(s_staged, 1)
                    stage(0, 0)

                    def body(t):
                        for k in range(2):
                            g = 2 * t + k
                            later = started(t) or k
                            stage(g + 1, 1 - k)
                            v.wait_ge(s_row[k], 16 * t + 16)
                            if later:
                                v.wait_ge(s_u, g)
                            for u in range(GT):
                                last = v.tensor_scalar(S[:, u, :], ROW[k][:, u * EP:(u + 1) * EP], dst_f[:, bass.ds(GT * g + u, 1)], None, ALU.is_equal)
                            last.then_inc(s_same, 1)
                            v.wait_ge(s_gat[k], 128 * t + 128)
                            norm.stats(v, me, X[k], EP, 2 * GT)
                            norm.invert(v, me, g + 1, EP, 2 * GT)
                            if later:
                                v.wait_ge(s_t, g)
                            for u in range(2 * GT):
                                last = v.tensor_scalar(C[:, u, :], X[k][:, u, :], norm.mean[:, u:u + 1], norm.rstd[:, u:u + 1], ALU.subtract, ALU.mult)
                            last.then_inc(s_c, 1)
                            v.wait_ge(s_rr, g + 1)
                            me.done(v.bn_stats(r_stats[:, bass.ds(g, 1), :].rearrange("p a s -> p (a s)"), R[:, :]))
                            me.settle()
                    loop(v, PAIRS, body, me)
            end_phase()

        carry_block(U, D + 1, "l2")

        with ExitStack() as c:
            pA = pb("bm_pa", [NP, 512], c)
            s_vs, s_var, s_root, s_ac, s_mm = (sem(f"bm_{n}") for n in ("steps", "var_ready", "root_ready", "folded", "multiplied"))
            with nc.Block() as block:
                @block.scalar
                def _(act):
                    act.wait_ge(s_var, 1)
                    act.activation(bn_w[:, 3:4], bn_w[:, 2:3], ACT.Sqrt).then_inc(s_root, 1)

                @block.vector
                def _(v):
                    me = Steps(v, s_vs)
                    fold(v, me, r_stats[:, :, :].rearrange("p a s -> p (a s)"), 0, G_MSG, BETA_MSG, msg_ac, s_var, s_root, 1)
                    v.sem_inc(s_ac, 1)
                    v.wait_ge(s_mm, 1)
                    me.done(v.tensor_copy(affine[:, 2:4, :], pA[:, 0:2 * D].rearrange("p (a f) -> p a f", a=2)))
                    me.settle()

                @block.tensor
                def _(pe):
                    pe.wait_ge(s_ac, 1)
                    affine_rows(pe, pA, msg_ac, s_mm)
            end_phase()

        with ExitStack() as c:
            tot = Totals("l2b", c, D + 1)
            T = [sb(f"l2b_t{k}", [EP, GT, D + 1], c=c) for k in range(2)]
            FD = [sb(f"l2b_fd{k}", [EP, GT, D], c=c) for k in range(2)]
            KP = [sb(f"l2b_keep{k}", [EP, GT, D], c=c) for k in range(2)]
            X3 = [sb(f"l2b_x3{k}", [EP, GT, D], c=c) for k in range(2)]
            W = [sb(f"l2b_w{k}", [EP, GT, D], c=c) for k in range(2)]
            idx = [sb(f"l2b_idx{k}", [EP, GT], I32, c) for k in range(2)]
            s_vs, s_fd, s_put, s_x3, s_use = sem("l2b_steps"), two("l2b_fd_loaded"), two("l2b_stored"), sem("l2b_x3_ready"), sem("l2b_fd_used")
            with nc.Block() as block:
                @block.sync
                def _(sp):
                    def body(t):
                        for k in range(2):
                            g = 2 * t + k
                            if started(t):
                                sp.wait_ge(s_use, g - 1)
                            sp.dma_start(FD[k][:, :, :], one_group(fd_groups, g)).then_inc(s_fd[k], 16)
                            sp.dma_start(KP[k][:, :, :], one_group(keep_groups, g)).then_inc(s_fd[k], 16)
                    loop(sp, PAIRS, body)

                @block.gpsimd
                def _(pool):
                    top = pool.to_reg(N - 1)

                    def body(t):
                        for k in range(2):
                            pool.wait_ge(s_x3, 2 * t + k + 1)
                            seen(pool)
                            for u in range(GT):
                                pool.indirect_dma_start(out, bass.IndirectOffsetOnAxis(ap=idx[k][:, u:u + 1], axis=0), X3[k][:, u, :], None,
                                                        bounds_check=top, oob_is_err=False).then_inc(s_put[k], 16)
                    loop(pool, PAIRS, body)
                    for k in range(2):
                        pool.wait_ge(s_put[k], 64 * PAIRS)

                @block.tensor
                def _(pe):
                    def body(t):
                        for k in range(2):
                            tot.tensor(pe, t, k)
                    loop(pe, PAIRS, body)

                @block.vector
                def _(v):
                    me = Steps(v, s_vs)
                    row = lambda j: affine[0:EP, j:j + 1, :].to_broadcast([EP, GT, D])

                    def body(t):
                        for k in range(2):
                            g = 2 * t + k
                            tot.vector(v, t, k)
                            tot.add(v, t, k, U, T[k][:, :, :])
                            v.wait_ge(s_fd[k], 32 * t + 32)
                            v.wait_ge(tot.s_used, g + 1)
                            me.done(v.tensor_tensor(FD[k][:, :, :], FD[k][:, :, :], row(0), ALU.mult))
                            me.done(v.tensor_tensor(W[k][:, :, :], T[k][:, :, 0:D], row(2), ALU.mult))
                            me.settle()
                            me.done(v.tensor_tensor(W[k][:, :, :], W[k][:, :, :], FD[k][:, :, :], ALU.add))
                            me.settle()
                            for u in range(GT):
                                me.done(v.scalar_tensor_tensor(T[k][:, u, 0:D], affine[0:EP, 3, :], T[k][:, u, D:D + 1], affine[0:EP, 1, :], ALU.mult, ALU.add))
                            me.done(v.tensor_tensor(W[k][:, :, :], W[k][:, :, :], KP[k][:, :, :], ALU.add))
                            me.settle()
                            v.sem_inc(s_use, 1)
                            if started(t):
                                v.wait_ge(s_put[k], 64 * t)
                            v.tensor_copy(idx[k][:, :], end_i[:, bass.ds(GT * g, GT)])
                            v.tensor_tensor(X3[k][:, :, :], W[k][:, :, :], T[k][:, :, 0:D], ALU.add).then_inc(s_x3, 1)
                            me.settle()
                    loop(v, PAIRS, body, me)
            end_phase()

        with ExitStack() as c:
            X = [sb(f"l3_x{k}", [EP, 2 * GT, D], c=c) for k in range(2)]
            C = sb("l3_c", [EP, 2 * GT, D], c=c)
            HT = sb("l3_ht", [D + 1, 3, GE], c=c)
            EA = [sb(f"l3_ea{k}", [EP, GT, D], c=c) for k in range(2)]
            QE = sb("l3_qe", [EP, 2, GT, D], c=c)
            KQ = sb("l3_kq", [EP, GT, D], c=c)
            P3 = sb("l3_p", [EP, GT, D], c=c)
            SC = sb("l3_sc", [EP, 3, GT, HEADS], c=c)
            M = sb("l3_m", [EP, GT, WU], c=c)
            S = sb("l3_same", [EP, GT, EP], c=c)
            ROW = [sb(f"l3_row{k}", [EP, GE], I32, c) for k in range(2)]
            idx = [sb(f"l3_idx{k}", [EP, 2, GT], I32, c) for k in range(2)]
            norm = Norm("l3", c, EP, 2 * GT)
            pT = pb("l3_pt", [D, 3, 512], c)
            pKQEV = pb("l3_pk", [EP, 4, 512], c)
            pU = pb("l3_pu", [EP, 512], c)
            s_one, s_vs = sem("l3_ones"), sem("l3_steps")
            s_row, s_ea, s_gat, s_keep = two("l3_row_loaded"), two("l3_attr_loaded"), two("l3_gathered"), two("l3_kept")
            s_staged, s_same, s_c, s_sc, s_m = (sem(f"l3_{n}") for n in ("staged", "same_ready", "normed", "scores_ready", "messages_ready"))
            s_t, s_at, s_h, s_ah, s_p, s_qe, s_ex, s_u, s_uc = (sem(f"l3_{n}") for n in ("turned", "attr_turned", "h_ready", "attr_copied", "projected", "qe_copied", "exp_ready", "summed", "sums_kept"))
            ea_groups = A["edge_attr_96"].rearrange("(g u p) k -> p g u k", u=GT, p=EP)

            with nc.Block() as block:
                @block.sync
                def _(sp):
                    def keep(g, k, t):
                        sp.wait_ge(s_gat[k], 128 * t + 128)
                        sp.dma_start(one_group(keep_groups, g), X[k][:, GT:2 * GT, :]).then_inc(s_keep[k], 16)

                    def body(t):
                        for k in range(2):
                            g = 2 * t + k
                            if started(t):
                                sp.wait_ge(s_same, g - 1)
                                sp.wait_ge(s_at, g - 1)
                            sp.dma_start(ROW[k][:, :], edge_row(A["dst"], g)).then_inc(s_row[k], 16)
                            sp.dma_start(EA[k][:, :, :], one_group(ea_groups, g)).then_inc(s_ea[k], 16)
                            if k:
                                keep(g - 1, 0, t)
                            elif started(t):
                                keep(g - 1, 1, t - 1)
                    loop(sp, PAIRS, body)
                    keep(GR - 1, 1, PAIRS - 1)
                    for k in range(2):
                        sp.wait_ge(s_keep[k], 16 * PAIRS)

                @block.gpsimd
                def _(pool):
                    def body(t):
                        for k in range(2):
                            g = 2 * t + k
                            pool.wait_ge(s_staged, g + 1)
                            seen(pool)
                            if started(t):
                                pool.wait_ge(s_c, g - 1)
                                seen(pool)
                                pool.wait_ge(s_keep[k], 16 * t)
                                seen(pool)
                            for h in range(2):
                                for u in range(GT):
                                    pool.indirect_dma_start(X[k][:, h * GT + u, :], None, out, bass.IndirectOffsetOnAxis(ap=idx[k][:, h, u:u + 1], axis=0)).then_inc(s_gat[k], 16)
                    loop(pool, PAIRS, body)

                @block.scalar
                def _(act):
                    def body(g):
                        act.wait_ge(s_at, g + 1)
                        act.activation(HT[0:D, 2, :], pT[:, 2, 0:GE], ACT.Copy).then_inc(s_ah, 1)
                        norm.root(act, g + 1, EP, 2 * GT)
                        act.wait_ge(s_t, g + 1)
                        act.activation(HT[0:D, 0:2, :], pT[:, 0:2, 0:GE], ACT.Relu).then_inc(s_h, 1)
                        act.wait_ge(s_p, g + 1)
                        act.activation(QE[:, :, :, :].rearrange("p a u d -> p a (u d)"), pKQEV[:, 1:3, 0:GT * D], ACT.Copy).then_inc(s_qe, 1)
                        act.wait_ge(s_sc, g + 1)
                        act.activation(M[:, :, D:WU], SC[:, 2, :, :], ACT.Exp).then_inc(s_ex, 1)
                        act.wait_ge(s_u, g + 1)
                        act.activation(U[:, bass.ds(GT * g, GT), :], pU[:, 0:GT * WU].rearrange("p (u d) -> p u d", u=GT), ACT.Copy).then_inc(s_uc, 1)
                    loop(act, GR, body)

                @block.tensor
                def _(pe):
                    pe.wait_ge(s_one, 1)

                    def group(g, k, t):
                        pe.wait_ge(s_ea[k], 16 * t + 16)
                        for u in range(GT):
                            last = pe.transpose(pT[:, 2, u * EP:(u + 1) * EP], EA[k][:, u, :], ident[0:EP, 0:EP])
                        last.then_inc(s_at, 1)
                        pe.wait_ge(s_c, g + 1)
                        for h in range(2):
                            for u in range(GT):
                                last = pe.transpose(pT[:, h, u * EP:(u + 1) * EP], C[:, h * GT + u, :], ident[0:EP, 0:EP])
                        last.then_inc(s_t, 1)
                        pe.wait_ge(s_h, g + 1)
                        pe.wait_ge(s_ah, g + 1)
                        if started(t) or k:
                            pe.wait_ge(s_m, g)
                        for u in range(GT):
                            at = slice(u * EP, (u + 1) * EP)
                            to = slice(u * D, (u + 1) * D)
                            pe.matmul(pKQEV[:, 0, to], HT[:, 0, at], WkV[:, 0:D], start=True, stop=True)
                            pe.matmul(pKQEV[:, 1, to], HT[:, 1, at], Wq[:, :], start=True, stop=True)
                            pe.matmul(pKQEV[:, 2, to], HT[:, 2, at], We[:, :], start=True, stop=True)
                            last = pe.matmul(pKQEV[:, 3, to], HT[:, 0, at], WkV[:, D:2 * D], start=True, stop=True)
                        last.then_inc(s_p, 1)
                        pe.wait_ge(s_m, g + 1)
                        pe.wait_ge(s_same, g + 1)
                        if started(t) or k:
                            pe.wait_ge(s_uc, g)
                        for u in range(GT):
                            last = pe.matmul(pU[:, u * WU:(u + 1) * WU], S[:, u, :], M[:, u, :], start=True, stop=True)
                        last.then_inc(s_u, 1)

                    def body(t):
                        for k in range(2):
                            group(2 * t + k, k, t)
                    loop(pe, PAIRS, body)

                @block.vector
                def _(v):
                    me = Steps(v, s_vs)
                    v.memset(HT[D:D + 1, :, :], 1.0).then_inc(s_one, 1)

                    def stage(g, k):
                        v.tensor_copy(idx[k][:, 0, :], src_i[:, bass.ds(GT * g, GT)])
                        v.tensor_copy(idx[k][:, 1, :], dst_i[:, bass.ds(GT * g, GT)]).then_inc(s_staged, 1)
                    stage(0, 0)

                    def bank(j):
                        return pKQEV[:, j, 0:GT * D].rearrange("p (u d) -> p u d", u=GT)

                    def body(t):
                        for k in range(2):
                            g = 2 * t + k
                            later = started(t) or k
                            stage(g + 1, 1 - k)
                            v.wait_ge(s_row[k], 16 * t + 16)
                            if later:
                                v.wait_ge(s_u, g)
                            for u in range(GT):
                                last = v.tensor_scalar(S[:, u, :], ROW[k][:, u * EP:(u + 1) * EP], dst_f[:, bass.ds(GT * g + u, 1)], None, ALU.is_equal)
                            last.then_inc(s_same, 1)
                            v.wait_ge(s_gat[k], 128 * t + 128)
                            norm.stats(v, me, X[k], EP, 2 * GT)
                            norm.invert(v, me, g + 1, EP, 2 * GT)
                            for u in range(2 * GT):
                                last = v.tensor_scalar(C[:, u, :], X[k][:, u, :], norm.mean[:, u:u + 1], norm.rstd[:, u:u + 1], ALU.subtract, ALU.mult)
                            last.then_inc(s_c, 1)
                            v.wait_ge(s_qe, g + 1)
                            me.done(v.tensor_tensor(KQ[:, :, :], bank(0), QE[:, 0, :, :], ALU.mult))
                            me.settle()
                            me.done(v.tensor_tensor(P3[:, :, :], KQ[:, :, :], QE[:, 1, :, :], ALU.mult))
                            me.settle()
                            me.done(v.tensor_reduce(SC[:, 0, :, :].rearrange("p u h -> p (u h)"), P3[:, :, :].rearrange("p u (h d) -> p (u h) d", d=HD),
                                                    mybir.AxisListType.X, ALU.add))
                            me.settle()
                            me.done(v.tensor_scalar(SC[:, 1, :, :], SC[:, 0, :, :], SCORE, 5.0, ALU.mult, ALU.min))
                            me.settle()
                            v.tensor_scalar(SC[:, 2, :, :], SC[:, 1, :, :], -5.0, None, ALU.max).then_inc(s_sc, 1)
                            v.wait_ge(s_ex, g + 1)
                            for u in range(GT):
                                last = v.tensor_tensor(M[:, u, 0:D].rearrange("p (h d) -> p h d", d=HD), bank(3)[:, u, :].rearrange("p (h d) -> p h d", d=HD),
                                                       M[:, u, D:WU].rearrange("p (h a) -> p h a", a=1).to_broadcast([EP, HEADS, HD]), ALU.mult)
                            last.then_inc(s_m, 1)
                    loop(v, PAIRS, body, me)
            end_phase()

        carry_block(U, WU, "l3")

        with ExitStack() as c:
            tot = Totals("l3b", c, WU)
            T = [sb(f"l3b_t{k}", [EP, GT, WU], c=c) for k in range(2)]
            Z = [sb(f"l3b_z{k}", [EP, 2, GT, HEADS], c=c) for k in range(2)]
            W = [sb(f"l3b_w{k}", [EP, GT, D], c=c) for k in range(2)]
            KP = [sb(f"l3b_keep{k}", [EP, GT, D], c=c) for k in range(2)]
            O = [sb(f"l3b_o{k}", [EP, GT, D], c=c) for k in range(2)]
            idx = [sb(f"l3b_idx{k}", [EP, GT], I32, c) for k in range(2)]
            s_vs, s_kp, s_put, s_o = sem("l3b_steps"), two("l3b_keep_loaded"), two("l3b_stored"), sem("l3b_out_ready")
            with nc.Block() as block:
                @block.sync
                def _(sp):
                    def body(t):
                        for k in range(2):
                            g = 2 * t + k
                            if started(t):
                                sp.wait_ge(s_o, g - 1)
                            sp.dma_start(KP[k][:, :, :], one_group(keep_groups, g)).then_inc(s_kp[k], 16)
                    loop(sp, PAIRS, body)

                @block.gpsimd
                def _(pool):
                    top = pool.to_reg(N - 1)

                    def body(t):
                        for k in range(2):
                            pool.wait_ge(s_o, 2 * t + k + 1)
                            seen(pool)
                            for u in range(GT):
                                pool.indirect_dma_start(out, bass.IndirectOffsetOnAxis(ap=idx[k][:, u:u + 1], axis=0), O[k][:, u, :], None,
                                                        bounds_check=top, oob_is_err=False).then_inc(s_put[k], 16)
                    loop(pool, PAIRS, body)
                    for k in range(2):
                        pool.wait_ge(s_put[k], 64 * PAIRS)

                @block.tensor
                def _(pe):
                    def body(t):
                        for k in range(2):
                            tot.tensor(pe, t, k)
                    loop(pe, PAIRS, body)

                @block.vector
                def _(v):
                    me = Steps(v, s_vs)

                    def body(t):
                        for k in range(2):
                            g = 2 * t + k
                            tot.vector(v, t, k)
                            tot.add(v, t, k, U, T[k][:, :, :])
                            v.wait_ge(tot.s_used, g + 1)
                            me.done(v.tensor_scalar(Z[k][:, 0, :, :], T[k][:, :, D:WU], Z_EPS, None, ALU.add))
                            me.settle()
                            me.done(v.reciprocal(Z[k][:, 1, :, :], Z[k][:, 0, :, :]))
                            me.settle()
                            for u in range(GT):
                                me.done(v.tensor_tensor(W[k][:, u, :].rearrange("p (h d) -> p h d", d=HD), T[k][:, u, 0:D].rearrange("p (h d) -> p h d", d=HD),
                                                        Z[k][:, 1, u, :].rearrange("p (h a) -> p h a", a=1).to_broadcast([EP, HEADS, HD]), ALU.mult))
                            me.settle()
                            if started(t):
                                v.wait_ge(s_put[k], 64 * t)
                            v.tensor_copy(idx[k][:, :], end_i[:, bass.ds(GT * g, GT)])
                            v.wait_ge(s_kp[k], 16 * t + 16)
                            v.tensor_tensor(O[k][:, :, :], W[k][:, :, :], KP[k][:, :, :], ALU.add).then_inc(s_o, 1)
                    loop(v, PAIRS, body, me)
            end_phase()
        hi.close()


_INS = ['x', 'src', 'dst', 'edge_attr_17', 'edge_attr_4', 'edge_attr_96', 'L1_gnn_W1', 'L1_gnn_b1', 'L1_gnn_W2',
        'L1_gnn_b2', 'L1_gnn_Ws', 'L1_gnn_bs', 'L1_gnn_Wn', 'L1_gnn_bn', 'L2_gnn_W_node', 'L2_gnn_b_node',
        'L2_gnn_g_node', 'L2_gnn_beta_node', 'L2_gnn_W_edge', 'L2_gnn_b_edge', 'L2_gnn_g_edge', 'L2_gnn_beta_edge',
        'L2_gnn_W_msg', 'L2_gnn_b_msg', 'L2_gnn_g_msg', 'L2_gnn_beta_msg', 'L3_gnn_Wq', 'L3_gnn_bq', 'L3_gnn_Wk',
        'L3_gnn_bk', 'L3_gnn_We', 'L3_gnn_be', 'L3_gnn_Wv', 'L3_gnn_bv']
_OUTS = [((100000, 96), 'float32')]


def kernel(**inputs):
    import numpy as _np
    import concourse.bacc as _bacc
    from concourse import mybir as _mybir
    from concourse.bass_utils import run_bass_kernel_spmd as _run

    nc = _bacc.Bacc("TRN2", target_bir_lowering=False, num_devices=1)
    arrays, args = {}, {}
    for name in _INS:
        a = _np.ascontiguousarray(inputs[name])
        arrays[f"in_{name}_dram"] = a
        args[name] = nc.dram_tensor(f"in_{name}_dram", a.shape, _mybir.dt.from_np(a.dtype), kind="ExternalInput").ap()
    shape, dtype = _OUTS[0]
    out = nc.dram_tensor("out_0_dram", shape, _mybir.dt.from_np(_np.dtype(dtype)), kind="ExternalOutput").ap()
    build(nc, args, out)
    r = _run(nc, [arrays], core_ids=[0])
    return r.results[0]["out_0_dram"]
```

```python
from contextlib import ExitStack

import concourse.bass as bass
from concourse import mybir

F32 = mybir.dt.float32
F16 = mybir.dt.float16
I32 = mybir.dt.int32
ALU = mybir.AluOpType
ACT = mybir.ActivationFunctionType

D = 96
EP = 125
GT = 4
GE = GT * EP
NP = 128
NG = 8
BLK = NP * NG
HEADS = 8
HD = D // HEADS
WU = D + HEADS
LN_EPS = 1e-5
BN_EPS = 1e-5
Z_EPS = 1e-6
SCORE = float(HD) ** -0.5
SKIP = 1 << 20


class Steps:

    def __init__(self, eng, sem):
        self.eng, self.sem, self.n, self.base = eng, sem, 0, 0

    def done(self, ins):
        self.n += 1
        ins.then_inc(self.sem, 1)

    def settle(self):
        self.eng.wait_ge(self.sem, self.base + self.n)


def loop(eng, turns, body, me=None, last=None):
    before = me.n if me else 0
    body(0)
    per_turn = me.n - before if me else 0
    end = turns - 1 if last else turns
    if end > 1:
        with eng.Fori(1, end) as t:
            if me:
                me.base, me.n = per_turn * t, before
            body(t)
    if last:
        if me:
            me.base, me.n = 0, before + per_turn * (turns - 1)
        last(turns - 1)
    if me:
        me.base, me.n = 0, before + per_turn * turns


def started(t):
    return not (isinstance(t, int) and t == 0)


AHEAD = 2
R = 4


class At:

    def __init__(self, turn, slot):
        self.turn, self.slot = turn, slot
        self.n = R * turn + slot
        self.fixed = isinstance(turn, int)

    def back(self, lag):
        return At(self.turn + (self.slot - lag) // R, (self.slot - lag) % R)

    def pair(self):
        return self.slot % 2


def pipeline(eng, items, depth, step, me=None):
    head = 2 * R
    tail = max(head, (items - 1) // R * R)
    for i in range(head):
        before = me.n if me else 0
        step(At(i // R, i % R))
    per_turn = R * (me.n - before) if me else 0
    count = me.n if me else 0
    if tail > head:
        with eng.Fori(head // R, tail // R) as t:
            if me:
                me.base, me.n = per_turn * (t - head // R), count
            for r in range(R):
                step(At(t, r))
    if me:
        me.base, me.n = 0, count + per_turn * (tail - head) // R
    for i in range(tail, items + depth):
        step(At(i // R, i % R))


def ready(eng, sem, at):
    eng.wait_ge(sem, at.n + 1)


def free(eng, sem, at, ring):
    if not (at.fixed and at.n < ring):
        eng.wait_ge(sem, at.n - ring + 1)


def landed(eng, sems, at, each=16):
    eng.wait_ge(sems[at.slot], each * at.turn + each)


def left(eng, sems, at, each=16):
    if not (at.fixed and at.turn == 0):
        eng.wait_ge(sems[at.slot], each * at.turn)


def build(nc, A, out):
    N = A["x"].shape[0]
    E = A["src"].shape[0]
    ET = E // EP
    TC = ET // 2
    GR = ET // GT
    PAIRS = GR // 2
    FULL = N // BLK
    TAILP = NP * 3 // 4
    TAILG = (N - FULL * BLK) // TAILP
    NB = FULL + 1
    HI = NB * NG
    HB = HI // 2
    IW = max(HI, NP)
    assert E == ET * EP and ET % (2 * GT) == 0 and NB % 2 == 0 and TAILP * TAILG == N - FULL * BLK
    assert HB <= 512 and TC <= 128

    def internal(name, rows, cols=D):
        return nc.dram_tensor(name, (rows, cols), F32, kind="Internal").ap()

    x1 = internal("x1_table", N + GE)
    agg1 = internal("agg1_table", N)
    x2 = internal("x2_table", N)
    dis_table = internal("dis_table", NB * BLK, 1)
    keep_rows = internal("keep_rows", E)

    ctx = ExitStack()
    with ctx:
        def sb(name, shape, dt=F32, c=ctx):
            return c.enter_context(nc.sbuf_tensor(name, shape, dt))

        def pb(name, shape, c):
            return c.enter_context(nc.psum_tensor(name, shape, F32))

        def kept_sem(name):
            return ctx.enter_context(nc.semaphore(name))

        phase_sems = []

        def sem(name):
            phase_sems.append(nc.alloc_semaphore(name))
            return phase_sems[-1]

        def end_phase():
            nc.clear_and_free_semaphores(phase_sems)
            phase_sems.clear()
            nc.all_engine_barrier()

        def ring_sems(name):
            return [sem(f"{name}{k}") for k in range(R)]

        def two(name):
            return [sem(f"{name}_even"), sem(f"{name}_odd")]

        ident = sb("ident", [128, 128])
        ones = sb("ones", [128, 128])
        zeros = sb("zeros", [128, NG * D])
        eps_col = sb("eps_col", [128, 1])
        first_row = sb("first_row", [TC, 2, EP])
        tile_sel = sb("tile_sel", [TC, 2, ET])
        joins = sb("joins", [TC, 2, ET])
        src_f = sb("src_f", [EP, ET])
        dst_f = sb("dst_f", [EP, ET])
        src_i = sb("src_i", [EP, ET + AHEAD * GT], I32)
        dst_i = sb("dst_i", [EP, ET + AHEAD * GT], I32)
        end_i = sb("end_i", [EP, ET + AHEAD * GT], I32)
        tails = sb("tails", [TC, 2, WU])
        carry = sb("carry", [TC, 2, WU])
        mean_n = sb("mean_n", [NP, NB, NG])
        rstd_n = sb("rstd_n", [NP, NB, NG])
        f_stats = sb("f_stats", [D, 2 * NB, 6])
        r_stats = sb("r_stats", [D, GR, 6])
        e_stats = sb("e_stats", [D, GR, 6])
        node_ac = sb("node_ac", [D, 2])
        msg_ac = sb("msg_ac", [D, 2])
        edge_ac = sb("edge_ac", [D, 2])
        affine = sb("affine", [NP, 4, D])
        W1T = sb("W1T", [18, D])
        W2T = sb("W2T", [D + 1, D])
        WsT = sb("WsT", [D + 1, D])
        WnT = sb("WnT", [D, D])
        bn_row = sb("bn_row", [D + 1, D])
        Wnode = sb("Wnode", [D + 1, D])
        Wedge = sb("Wedge", [5, D])
        Wmsg = sb("Wmsg", [D, 3, D])
        Wc = sb("Wc", [D, D])
        msg_bias = sb("msg_bias", [D, 1])
        cols = sb("cols", [D, 8])
        WkV = sb("WkV", [D + 1, 2 * D])
        Wq = sb("Wq", [D + 1, D])
        We = sb("We", [D + 1, D])
        bn_w = sb("bn_w", [D, 4])
        B_NODE, G_NODE, BETA_NODE, G_EDGE, BETA_EDGE, B_MSG, G_MSG, BETA_MSG = range(8)

        x1_ready, agg1_ready, zeros_ready = kept_sem("x1_ready"), kept_sem("agg1_ready"), kept_sem("zeros_ready")
        pool_gate, sp_gate = kept_sem("pool_gate"), kept_sem("sp_gate")

        def seen(pool):
            pool.sem_inc(pool_gate, 1)

        def sp_seen(sp):
            sp.sem_inc(sp_gate, 1)

        def spread(col, n, shape):
            return col.rearrange("p (a b) -> p a b", b=1).to_broadcast(shape)

        class Norm:

            def __init__(self, name, c, P, G):
                self.st = sb(f"{name}_st", [P, G, 6], c=c)
                self.w = sb(f"{name}_w", [P, 6, G], c=c)
                self.mean = sb(f"{name}_mean", [P, G], c=c)
                self.rstd = sb(f"{name}_rstd", [P, G], c=c)
                self.var_ready, self.root_ready = sem(f"{name}_var_ready"), sem(f"{name}_root_ready")

            def stats(self, v, me, X, P, G, mean=None):
                mean = self.mean[0:P, 0:G] if mean is None else mean
                st, w = self.st, self.w
                for g in range(G):
                    me.done(v.bn_stats(st[0:P, g, :], X[0:P, g, :]))
                me.settle()
                me.done(v.tensor_tensor(w[0:P, 0, 0:G], st[0:P, 0:G, 1], st[0:P, 0:G, 4], ALU.add))
                me.done(v.tensor_tensor(w[0:P, 1, 0:G], st[0:P, 0:G, 1], st[0:P, 0:G, 4], ALU.subtract))
                me.done(v.tensor_tensor(w[0:P, 2, 0:G], st[0:P, 0:G, 2], st[0:P, 0:G, 5], ALU.add))
                me.settle()
                me.done(v.tensor_scalar(mean, w[0:P, 0, 0:G], 0.5, None, ALU.mult))
                me.done(v.tensor_tensor(w[0:P, 3, 0:G], w[0:P, 1, 0:G], w[0:P, 1, 0:G], ALU.mult))
                me.settle()
                v.scalar_tensor_tensor(w[0:P, 4, 0:G], w[0:P, 3, 0:G], D / 4.0, w[0:P, 2, 0:G],
                                       ALU.mult, ALU.add).then_inc(self.var_ready, 1)

            def spread(self, what, P, G):
                return what[0:P, 0:G].rearrange("p (g a) -> p g a", a=1).to_broadcast([P, G, D])

            def apply(self, v, me, X, C, P, G):
                me.done(v.tensor_tensor(C[0:P, 0:G, :], X[0:P, 0:G, :], self.spread(self.mean, P, G), ALU.subtract))
                me.settle()
                return v.tensor_tensor(C[0:P, 0:G, :], C[0:P, 0:G, :], self.spread(self.rstd, P, G), ALU.mult)

            def root(self, act, n, P, G):
                act.wait_ge(self.var_ready, n)
                act.activation(self.w[0:P, 5, 0:G], self.w[0:P, 4, 0:G], ACT.Sqrt,
                               bias=eps_col[0:P, :], scale=1.0 / D).then_inc(self.root_ready, 1)

            def invert(self, v, me, n, P, G, rstd=None):
                v.wait_ge(self.root_ready, n)
                me.done(v.reciprocal(self.rstd[0:P, 0:G] if rstd is None else rstd, self.w[0:P, 5, 0:G]))
                me.settle()

        def half_count(at):
            return (R // 2) * at.turn + at.slot // 2 + 1

        def is_item(at, items):
            return not at.fixed or 0 <= at.n < items

        def one_group(groups, g):
            return groups[:, bass.ds(g, 1), :, :].rearrange("p g u k -> p (g u) k")

        def edge_row(src, g):
            return src.rearrange("(a n) -> a n", a=1)[:, bass.ds(g * GE, GE)].to_broadcast([EP, GE])

        keep_groups = keep_rows.rearrange("(g u p) k -> p g u k", u=GT, p=EP)
        e4_groups = A["edge_attr_4"].rearrange("(g u p) k -> p g u k", u=GT, p=EP)

        with ExitStack() as c:
            dnext_i = sb("dnext_i", [EP, ET], I32, c)
            dnext_f = sb("dnext_f", [EP, ET], c=c)
            last_f = sb("last_f", [EP, ET], c=c)
            dstrow_i = sb("dstrow_i", [TC, 2, EP], I32, c)
            dst_row = sb("dst_row", [TC, 2, EP], c=c)
            first_i = sb("first_i", [TC, ET], I32, c)
            first_f = sb("first_f", [TC, ET], c=c)
            hi_i = sb("hi_i", [EP, 3, ET], I32, c)
            hi_f = sb("hi_f", [EP, ET], c=c)
            lo_f = sb("lo_f", [EP, ET], c=c)
            iota_i = sb("iota_i", [EP, IW], I32, c)
            iota_h = sb("iota_h", [EP, IW], F16, c)
            hot_hi = sb("hot_hi", [EP, 2, HI], F16, c)
            hot_lo = sb("hot_lo", [EP, 2, NP], F16, c)
            zero_h = sb("zero_h", [1, NP + HB], F16, c)
            dg = sb("dg", [NP, 3, HI], c=c)
            dg_root = sb("dg_root", [NP, HI], c=c)
            X = [sb(f"p0_x{k}", [EP, GT, D], c=c) for k in range(R)]
            idx = [sb(f"p0_idx{k}", [EP, GT], I32, c) for k in range(R)]
            pdeg = pb("pdeg", [NP, 2, 512], c)

            s_rows, s_w, s_dis = sem("rows_loaded"), sem("weights_loaded"), sem("dis_stored")
            s_fill, s_vs, s_const, s_sel = sem("fills_done"), sem("p0_steps"), sem("consts_ready"), sem("selects_ready")
            s_join = sem("joins_compared")
            s_hot, s_deg, s_degin = sem("hot_ready"), sem("degrees_added"), sem("degrees_read")
            s_root, s_dg = sem("root_ready"), sem("dis_ready")
            s_dst, s_idx, s_gat, s_st = sem("dst_loaded"), sem("indices_staged"), ring_sems("xd_gathered"), ring_sems("xd_stored")

            row = lambda n: A[n].rearrange("(a n) -> a n", a=1)
            turned = lambda n: A[n].rearrange("o i -> i o")
            loads = [
                (W1T[0:17, :], turned("L1_gnn_W1")), (W1T[17:18, :], row("L1_gnn_b1")),
                (W2T[0:D, :], turned("L1_gnn_W2")), (W2T[D:D + 1, :], row("L1_gnn_b2")),
                (WsT[0:D, :], turned("L1_gnn_Ws")), (WsT[D:D + 1, :], row("L1_gnn_bs")),
                (WnT[:, :], turned("L1_gnn_Wn")), (bn_row[D:D + 1, :], row("L1_gnn_bn")),
                (Wnode[0:D, :], A["L2_gnn_W_node"]), (Wnode[D:D + 1, :], row("L2_gnn_b_node")),
                (Wedge[0:4, :], A["L2_gnn_W_edge"]), (Wedge[4:5, :], row("L2_gnn_b_edge")),
                (Wmsg[:, :, :], A["L2_gnn_W_msg"].rearrange("(k i) o -> i k o", k=3)),
                (WkV[0:D, 0:D], A["L3_gnn_Wk"]), (WkV[0:D, D:2 * D], A["L3_gnn_Wv"]),
                (WkV[D:D + 1, 0:D], row("L3_gnn_bk")), (WkV[D:D + 1, D:2 * D], row("L3_gnn_bv")),
                (Wq[0:D, :], A["L3_gnn_Wq"]), (Wq[D:D + 1, :], row("L3_gnn_bq")),
                (We[0:D, :], A["L3_gnn_We"]), (We[D:D + 1, :], row("L3_gnn_be")),
            ] + [(cols[:, k:k + 1], A[n].rearrange("(p a) -> p a", a=1)) for k, n in enumerate(
                ("L2_gnn_b_node", "L2_gnn_g_node", "L2_gnn_beta_node", "L2_gnn_g_edge",
                 "L2_gnn_beta_edge", "L2_gnn_b_msg", "L2_gnn_g_msg", "L2_gnn_beta_msg"))]
            NW = 16 * len(loads)

            with nc.Block() as block:
                @block.sync
                def _(sp):
                    half = TC * EP
                    with nc.allow_non_contiguous_dma(reason="indices by edge of a tile, and small weights, once"):
                        sp.dma_start(dst_i[:, 0:ET], A["dst"].rearrange("(t e) -> e t", e=EP)).then_inc(s_dst, 16)
                        sp.dma_start(src_i[:, 0:ET], A["src"].rearrange("(t e) -> e t", e=EP)).then_inc(s_rows, 16)
                        sp.dma_start(dnext_i[0:EP, 0:ET - 1], A["dst"][1:1 + E - EP].rearrange("(t e) -> e t", e=EP)).then_inc(s_rows, 16)
                        sp.wait_ge(s_fill, 1)
                        sp.dma_start(dnext_i[0:EP - 1, ET - 1:ET], A["dst"][E - EP + 1:E].rearrange("(e a) -> e a", a=1)).then_inc(s_rows, 16)
                        for h in range(2):
                            sp.dma_start(dstrow_i[:, h, :], A["dst"][h * half:(h + 1) * half].rearrange("(t e) -> t e", e=EP)).then_inc(s_rows, 16)
                        firsts = A["dst"].rearrange("(t e) -> e t", e=EP)[0:1, :]
                        sp.dma_start(first_i[:, :], firsts.to_broadcast([TC, ET])).then_inc(s_rows, 16)
                        for o, i in loads:
                            sp.dma_start(o, i).then_inc(s_w, 16)

                    def step(at):
                        if is_item(at, GR):
                            landed(sp, s_gat, at, 16 * GT)
                            sp_seen(sp)
                            sp.dma_start(one_group(keep_groups, at.n), X[at.slot][:, :, :]).then_inc(s_st[at.slot], 16)
                    pipeline(sp, GR, 0, step)
                    for k in range(R):
                        sp.wait_ge(s_st[k], 16 * ((GR - 1 - k) // R + 1))
                    sp.wait_ge(s_w, NW)
                    sp.wait_ge(s_dg, 1)
                    sp.dma_start(dis_table.rearrange("(b p g) a -> p b (g a)", p=NP, g=NG),
                                 dg[:, 2, :].rearrange("p (b g) -> p b g", g=NG)).then_inc(s_dis, 16)
                    sp.wait_ge(s_dis, 16)

                @block.gpsimd
                def _(pool):
                    pool.memset(dnext_i[:, ET - 1:ET], -1).then_inc(s_fill, 1)
                    pool.memset(ident[:, :], 0.0).then_inc(s_fill, 1)
                    pool.memset(tile_sel[:, :, :], 0.0).then_inc(s_fill, 1)
                    pool.memset(src_i[:, ET:ET + AHEAD * GT], 0).then_inc(s_const, 1)
                    pool.memset(dst_i[:, ET:ET + AHEAD * GT], 0).then_inc(s_const, 1)
                    pool.memset(end_i[:, ET:ET + AHEAD * GT], 0).then_inc(s_const, 1)
                    pool.memset(ones[:, :], 1.0).then_inc(s_const, 1)
                    pool.memset(zeros[:, :], 0.0).then_inc(zeros_ready, 1)
                    pool.memset(eps_col[:, :], LN_EPS).then_inc(s_const, 1)
                    pool.memset(zero_h[:, :], 0.0).then_inc(s_const, 1)
                    pool.iota(iota_i[:, :], pattern=[[1, IW]], base=0, channel_multiplier=0).then_inc(s_const, 1)
                    pool.wait_ge(s_fill, 3)
                    pool.affine_select(out=ident[:, :], in_=ident[:, :], compare_op=ALU.not_equal, fill=1.0,
                                       base=0, pattern=[[-1, 128]], channel_multiplier=1).then_inc(s_const, 1)
                    pool.affine_select(out=tile_sel[:, :, :], in_=tile_sel[:, :, :], compare_op=ALU.not_equal, fill=1.0,
                                       base=0, pattern=[[TC, 2], [-1, ET]], channel_multiplier=1).then_inc(s_const, 1)
                    pool.wait_ge(s_dst, 16)

                    def step(at):
                        if is_item(at, GR):
                            left(pool, s_st, at)
                            pool.tensor_copy(idx[at.slot][:, :], dst_i[:, bass.ds(GT * at.n, GT)]).then_inc(s_idx, 1)
                            ready(pool, s_idx, at)
                            seen(pool)
                            for u in range(GT):
                                pool.indirect_dma_start(X[at.slot][:, u, :], None, A["x"], bass.IndirectOffsetOnAxis(ap=idx[at.slot][:, u:u + 1], axis=0)).then_inc(s_gat[at.slot], 16)
                    pipeline(pool, GR, 0, step)
                    pool.wait_ge(s_join, 2)
                    pool.affine_select(out=joins[:, :, :], in_=joins[:, :, :], compare_op=ALU.is_gt, fill=0.0,
                                       base=0, pattern=[[-TC, 2], [1, ET]], channel_multiplier=-1).then_inc(s_sel, 1)

                @block.scalar
                def _(act):
                    act.wait_ge(s_rows, 16 * 6)
                    act.wait_ge(zeros_ready, 1)
                    act.dma_start(x1[N:N + GE, :].rearrange("(p a) b -> p (a b)", p=EP), zeros[0:EP, 0:GT * D]).then_inc(x1_ready, 16)
                    piece = N // 16
                    for k in range(16):
                        act.wait_ge(s_idx, min(GR, GR * k // 16 + 1))
                        act.dma_start(x1[piece * k:piece * (k + 1), :], A["x"][piece * k:piece * (k + 1), :]).then_inc(x1_ready, 16)
                    act.wait_ge(s_degin, 2)
                    act.activation(dg_root[:, :], dg[:, 1, :], ACT.Sqrt).then_inc(s_root, 1)

                @block.tensor
                def _(pe):
                    pe.wait_ge(s_const, 9)
                    for h in range(2):
                        pe.matmul(pdeg[:, h, 0:HB], zero_h[0:1, 0:NP], zero_h[0:1, NP:NP + HB], start=True, stop=False)

                    def degrees(t):
                        for k in range(2):
                            pe.wait_ge(s_hot, 2 * t + k + 1)
                            for h in range(2):
                                last = pe.matmul(pdeg[:, h, 0:HB], hot_lo[:, k, :], hot_hi[:, k, h * HB:(h + 1) * HB],
                                                 start=False, stop=False, skip_group_check=True)
                            last.then_inc(s_deg, 1)
                    loop(pe, ET // 2, degrees)
                    for h in range(2):
                        last = pe.matmul(pdeg[:, h, 0:HB], zero_h[0:1, 0:NP], zero_h[0:1, NP:NP + HB], start=False, stop=True)
                    last.then_inc(s_deg, 1)
                @block.vector
                def _(v):
                    me = Steps(v, s_vs)
                    v.wait_ge(s_dst, 16)
                    v.wait_ge(s_rows, 16 * 6)
                    v.wait_ge(s_const, 9)
                    me.done(v.tensor_copy(src_f[:, :], src_i[:, 0:ET]))
                    me.done(v.tensor_copy(dst_f[:, :], dst_i[:, 0:ET]))
                    me.done(v.tensor_copy(dnext_f[:, :], dnext_i[:, :]))
                    me.done(v.tensor_copy(dst_row[:, :, :], dstrow_i[:, :, :]))
                    me.done(v.tensor_copy(first_f[:, :], first_i[:, :]))
                    me.done(v.tensor_copy(iota_h[:, :], iota_i[:, :]))
                    me.done(v.tensor_scalar(hi_i[:, 0, :], src_i[:, 0:ET], 10, 3, ALU.logical_shift_right, ALU.logical_shift_left))
                    me.done(v.tensor_scalar(hi_i[:, 1, :], src_i[:, 0:ET], NG - 1, None, ALU.bitwise_and))
                    me.done(v.tensor_scalar(hi_i[:, 2, :], src_i[:, 0:ET], 3, NP - 1, ALU.logical_shift_right, ALU.bitwise_and))
                    me.settle()
                    for h in range(2):
                        me.done(v.tensor_scalar(first_row[:, h, :], dst_row[:, h, :], dst_row[:, h, 0:1], None, ALU.is_equal))
                        v.tensor_scalar(joins[:, h, :], first_f[:, :], dst_row[:, h, EP - 1:EP], None, ALU.is_equal).then_inc(s_join, 1)
                    me.done(v.tensor_tensor(hi_f[:, :], hi_i[:, 0, :], hi_i[:, 1, :], ALU.add))
                    me.done(v.tensor_copy(lo_f[:, :], hi_i[:, 2, :]))
                    me.done(v.tensor_tensor(last_f[:, :], dst_f[:, :], dnext_f[:, :], ALU.not_equal))
                    me.settle()
                    me.done(v.scalar_tensor_tensor(dnext_f[:, :], dst_f[:, :], -float(SKIP), last_f[:, :], ALU.add, ALU.mult))
                    me.settle()
                    me.done(v.tensor_scalar(end_i[:, 0:ET], dnext_f[:, :], float(SKIP), None, ALU.add))
                    def hots(t):
                        for k in range(2):
                            if started(t):
                                v.wait_ge(s_deg, 2 * t + k - 1)
                            v.tensor_scalar(hot_lo[:, k, :], iota_h[:, 0:NP], lo_f[:, bass.ds(2 * t + k, 1)], None, ALU.is_equal)
                            v.tensor_scalar(hot_hi[:, k, :], iota_h[:, 0:HI], hi_f[:, bass.ds(2 * t + k, 1)], None, ALU.is_equal).then_inc(s_hot, 1)
                    loop(v, ET // 2, hots)
                    v.wait_ge(s_deg, ET + 1)
                    for h in range(2):
                        v.tensor_scalar(dg[:, 1, h * HB:(h + 1) * HB], pdeg[:, h, 0:HB], 1.0, None, ALU.max).then_inc(s_degin, 1)
                        me.done(v.tensor_scalar(dg[:, 0, h * HB:(h + 1) * HB], pdeg[:, h, 0:HB], 1.0, None, ALU.min))

                    v.wait_ge(s_w, NW)
                    me.done(v.tensor_tensor(WsT[D:D + 1, :], WsT[D:D + 1, :], bn_row[D:D + 1, :], ALU.add))
                    v.wait_ge(s_root, 1)
                    me.done(v.reciprocal(dg_root[:, :], dg_root[:, :]))
                    me.settle()
                    v.tensor_tensor(dg[:, 2, :], dg_root[:, :], dg[:, 0, :], ALU.mult).then_inc(s_dg, 1)
            end_phase()

        def per_tile(col, g, shape):
            return col[:, bass.ds(GT * g, GT)].rearrange("p (u a) -> p u a", a=1).to_broadcast(shape)

        def same_target(v, S, ROW, g):
            return v.tensor_tensor(S[:, :, :], ROW[:, :].rearrange("p (u e) -> p u e", u=GT), per_tile(dst_f, g, [EP, GT, EP]), ALU.is_equal)

        def by_tile(p, width=D):
            return p[0:EP, 0:GT * width].rearrange("p (u d) -> p u d", u=GT)

        with ExitStack() as c:
            X = [sb(f"l0_x{k}", [EP, GT, D], c=c) for k in range(2)]
            MSG = [sb(f"l0_msg{k}", [EP, GT, D], c=c) for k in range(2)]
            TOT = [sb(f"l0_tot{k}", [EP, GT, D], c=c) for k in range(2)]
            S = [sb(f"l0_same{k}", [EP, GT, GE], c=c) for k in range(2)]
            ROW = [sb(f"l0_row{k}", [EP, GE], I32, c) for k in range(2)]
            earlier = sb("l0_earlier", [EP, GT, GE], c=c)
            scrap = sb("l0_scrap", [EP, GT, GE], c=c)
            idx = [sb(f"l0_idx{k}", [EP, 2, GT], I32, c) for k in range(2)]
            dis = [sb(f"l0_dis{k}", [EP, 2, GT], c=c) for k in range(2)]
            to = [sb(f"l0_to{k}", [EP, GT], I32, c) for k in range(2)]
            spare_i = sb("l0_spare_i", [EP, GT], I32, c)
            spare = sb("l0_spare", [EP, GT], c=c)
            dup = sb("l0_dup", [EP, GT], c=c)
            off = sb("l0_off", [EP, 2, GT], c=c)
            fac = [sb(f"l0_fac{k}", [EP, 3, GT], c=c) for k in range(2)]
            norm = Norm("l0", c, EP, GT)
            e4 = sb("e4", [EP, 2, GT, 5], c=c)
            e4T = sb("e4T", [5, 2, GE], c=c)
            efs = sb("efs", [D, 2, GE], c=c)
            ptot = [pb(f"l0_ptot{k}", [EP, 512], c) for k in range(2)]
            pe4 = [pb(f"pe4_{k}", [5, 512], c) for k in range(2)]
            pef = [pb(f"pef_{k}", [D, 512], c) for k in range(2)]

            s_fill, s_cst, s_vs = sem("l0_filled"), sem("l0_consts"), sem("l0_steps")
            s_row, s_staged, s_gat = two("l0_rows_loaded"), sem("l0_indices_staged"), two("l0_gathered")
            s_same, s_fac, s_msg, s_sum = sem("l0_same_ready"), sem("l0_factors_ready"), sem("l0_messages_ready"), sem("l0_summed")
            s_tot, s_sent = sem("l0_totals_ready"), sem("l0_added")
            s_x, s_e4 = two("l0_x_loaded"), two("e4_loaded")
            s_e4t, s_e4c, s_ef, s_efr, s_efs = sem("e4_turned"), sem("e4_copied"), sem("ef_made"), sem("ef_relu"), sem("ef_counted")
            PER_G = 16 * 2 * GT
            PER_TURN = FULL // PAIRS

            with nc.Block() as block:
                @block.sync
                def _(sp):
                    def rows(t):
                        for k in range(2):
                            g = 2 * t + k
                            if started(t):
                                sp.wait_ge(s_same, g - 1)
                            sp.dma_start(ROW[k][:, :], edge_row(A["src"], g)).then_inc(s_row[k], 16)
                            if started(t):
                                sp.wait_ge(s_msg, g - 1)
                                sp_seen(sp)
                            sp.dma_start(X[k][:, :, :], one_group(keep_groups, g)).then_inc(s_x[k], 16)
                            if started(t):
                                sp.wait_ge(s_e4t, g - 1)
                                sp_seen(sp)
                            sp.dma_start(e4[:, k, :, 0:4], one_group(e4_groups, g)).then_inc(s_e4[k], 16)
                    sp.wait_ge(s_fill, 2)
                    loop(sp, PAIRS, rows)

                @block.gpsimd
                def _(pool):
                    pool.memset(earlier[:, :, :], 1.0).then_inc(s_fill, 1)
                    pool.iota(spare_i[:, :], pattern=[[EP, GT]], base=N, channel_multiplier=1).then_inc(s_cst, 1)
                    pool.memset(e4[:, :, :, :], 1.0).then_inc(s_fill, 1)
                    pool.wait_ge(s_fill, 2)
                    pool.affine_select(out=earlier[:, :, :], in_=earlier[:, :, :], compare_op=ALU.is_gt, fill=0.0,
                                       base=0, pattern=[[EP, GT], [-1, GE]], channel_multiplier=1).then_inc(s_cst, 1)

                    def gathers(g, k):
                        pool.wait_ge(s_staged, g + 1)
                        seen(pool)
                        for u in range(GT):
                            for h in range(2):
                                pool.indirect_dma_start(dis[k][:, h, u:u + 1], None, dis_table, bass.IndirectOffsetOnAxis(ap=idx[k][:, h, u:u + 1], axis=0)).then_inc(s_gat[k], 16)

                    def adds(g, k):
                        pool.wait_ge(s_tot, g + 1)
                        seen(pool)
                        if isinstance(g, int) and g == 0:
                            pool.wait_ge(x1_ready, 16 * 17)
                        else:
                            pool.wait_ge(s_sent, 16 * GT * g)
                            seen(pool)
                        for u in range(GT):
                            pool.indirect_dma_start(x1, bass.IndirectOffsetOnAxis(ap=to[k][:, u:u + 1], axis=0), TOT[k][:, u, :], None,
                                                    compute_op=ALU.add).then_inc(s_sent, 16)

                    def body(t):
                        gathers(2 * t, 0)
                        if started(t):
                            adds(2 * t - 1, 1)
                        gathers(2 * t + 1, 1)
                        adds(2 * t, 0)
                    loop(pool, PAIRS, body)
                    adds(GR - 1, 1)
                    pool.wait_ge(s_sent, 16 * GT * GR)

                @block.scalar
                def _(act):
                    full = agg1[0:FULL * BLK, :].rearrange("(b p g) f -> p b (g f)", p=NP, g=NG)

                    def clear(b, n):
                        act.dma_start(full[:, bass.ds(b, n), :], zeros[:, :].rearrange("p (a n) -> p a n", a=1).to_broadcast([NP, n, NG * D])).then_inc(agg1_ready, 16)
                    act.dma_start(agg1[FULL * BLK:N, :].rearrange("(p g) f -> p (g f)", g=TAILG), zeros[0:TAILP, 0:TAILG * D]).then_inc(agg1_ready, 16)

                    def body(t):
                        clear(PER_TURN * t, PER_TURN)
                        for k in range(2):
                            g = 2 * t + k
                            norm.root(act, g + 1, EP, GT)
                            act.wait_ge(s_fac, g + 1)
                            if started(t):
                                act.wait_ge(s_sum, g - 1)
                            for u in range(GT):
                                last = act.activation(MSG[k][:, u, :], X[k][:, u, :], ACT.Relu,
                                                      bias=fac[k][:, 2, u:u + 1], scale=fac[k][:, 1, u:u + 1])
                            last.then_inc(s_msg, 1)
                            act.wait_ge(s_sum, g + 1)
                            if started(t):
                                act.wait_ge(s_sent, 16 * GT * (g - 1))
                            act.activation(TOT[k][:, :, :], ptot[k][:, 0:GT * D].rearrange("p (u d) -> p u d", u=GT), ACT.Copy).then_inc(s_tot, 1)
                            act.wait_ge(s_e4t, g + 1)
                            act.activation(e4T[:, k, :], pe4[k][:, 0:GE], ACT.Copy).then_inc(s_e4c, 1)
                            act.wait_ge(s_ef, g + 1)
                            if started(t):
                                act.wait_ge(s_efs, g - 1)
                            act.activation(efs[:, k, :], pef[k][:, 0:GE], ACT.Relu).then_inc(s_efr, 1)
                    loop(act, PAIRS, body)
                    clear(PER_TURN * PAIRS, FULL - PER_TURN * PAIRS)

                @block.tensor
                def _(pe):
                    def body(t):
                        for k in range(2):
                            g = 2 * t + k
                            pe.wait_ge(s_msg, g + 1)
                            pe.wait_ge(s_same, g + 1)
                            if started(t):
                                pe.wait_ge(s_tot, g - 1)
                            for i in range(GT):
                                for j in range(i, GT):
                                    last = pe.matmul(ptot[k][:, i * D:(i + 1) * D], S[k][:, j, i * EP:(i + 1) * EP], MSG[k][:, j, :],
                                                     start=(j == i), stop=(j == GT - 1))
                            last.then_inc(s_sum, 1)
                            pe.wait_ge(s_e4[k], 16 * t + 16)
                            if started(t):
                                pe.wait_ge(s_e4c, g - 1)
                            for u in range(GT):
                                last = pe.transpose(pe4[k][:, u * EP:(u + 1) * EP], e4[:, k, u, :], ident[0:EP, 0:EP])
                            last.then_inc(s_e4t, 1)
                            pe.wait_ge(s_e4c, g + 1)
                            if started(t):
                                pe.wait_ge(s_efr, g - 1)
                            pe.matmul(pef[k][:, 0:GE], Wedge[:, :], e4T[:, k, :], start=True, stop=True).then_inc(s_ef, 1)
                    loop(pe, PAIRS, body)

                @block.vector
                def _(v):
                    me = Steps(v, s_vs)
                    v.wait_ge(s_cst, 2)
                    me.done(v.tensor_copy(spare[:, :], spare_i[:, :]))

                    def stage(g, k):
                        v.tensor_copy(idx[k][:, 0, :], dst_i[:, bass.ds(GT * g, GT)])
                        v.tensor_copy(idx[k][:, 1, :], src_i[:, bass.ds(GT * g, GT)]).then_inc(s_staged, 1)
                    stage(0, 0)

                    def features(g, k):
                        v.wait_ge(s_efr, g + 1)
                        v.bn_stats(e_stats[:, bass.ds(g, 1), :].rearrange("p a b -> p (a b)"), efs[:, k, :]).then_inc(s_efs, 1)

                    def body(t):
                        for k in range(2):
                            g = 2 * t + k
                            stage(g + 1, 1 - k)
                            v.wait_ge(s_row[k], 16 * t + 16)
                            if started(t):
                                v.wait_ge(s_sum, g - 1)
                            for a in range(GT):
                                last = v.tensor_scalar(S[k][:, a, :], ROW[k][:, :], src_f[:, bass.ds(GT * g + a, 1)], None, ALU.is_equal)
                            me.done(last)
                            me.settle()
                            v.sem_inc(s_same, 1)
                            for a in range(GT):
                                me.done(v.scalar_tensor_tensor(scrap[:, a, :], S[k][:, a, :], 1.0, earlier[:, a, :], ALU.mult, ALU.mult,
                                                               accum_out=dup[:, a:a + 1]))
                            me.done(v.tensor_tensor(off[:, 0, :], spare[:, :], src_f[:, bass.ds(GT * g, GT)], ALU.subtract))
                            me.settle()
                            me.done(v.scalar_tensor_tensor(off[:, 1, :], dup[:, :], 1.0, off[:, 0, :], ALU.min, ALU.mult))
                            me.settle()
                            if started(t):
                                v.wait_ge(s_sent, 16 * GT * (g - 1))
                            me.done(v.tensor_tensor(to[k][:, :], off[:, 1, :], src_f[:, bass.ds(GT * g, GT)], ALU.add))
                            v.wait_ge(s_x[k], 16 * t + 16)
                            norm.stats(v, me, X[k], EP, GT)
                            if started(t) or k > 0:
                                features(g - 1, 1 - k)
                            norm.invert(v, me, g + 1, EP, GT)
                            if started(t):
                                v.wait_ge(s_msg, g - 1)
                            v.wait_ge(s_gat[k], PER_G * t + PER_G)
                            me.done(v.tensor_tensor(fac[k][:, 0, :], dis[k][:, 0, :], dis[k][:, 1, :], ALU.mult))
                            me.settle()
                            me.done(v.tensor_tensor(fac[k][:, 1, :], fac[k][:, 0, :], norm.rstd[:, :], ALU.mult))
                            me.settle()
                            v.scalar_tensor_tensor(fac[k][:, 2, :], norm.mean[:, :], -1.0, fac[k][:, 1, :], ALU.mult, ALU.mult).then_inc(s_fac, 1)
                    loop(v, PAIRS, body, me)
                    features(GR - 1, 1)
            end_phase()

        def carry_block(U, width, tag):
            with ExitStack() as c:
                pc = pb(f"{tag}_pc", [TC, 2, 512], c)
                s_t, s_c, s_e = sem(f"{tag}_tails_loaded"), sem(f"{tag}_carried"), sem(f"{tag}_carry_ready")
                with nc.Block() as block:
                    @block.sync
                    def _(sp):
                        for h in range(2):
                            sp.dma_start(tails[:, h, 0:width], U[EP - 1:EP, h * TC:(h + 1) * TC, 0:width]).then_inc(s_t, 16)
                        sp.wait_ge(s_t, 32)

                    @block.tensor
                    def _(pe):
                        pe.wait_ge(s_t, 32)
                        for h in range(2):
                            for j in range(2):
                                last = pe.matmul(pc[:, h, 0:width], joins[:, j, h * TC:(h + 1) * TC], tails[:, j, 0:width],
                                                 start=(j == 0), stop=(j == 1))
                        last.then_inc(s_c, 1)

                    @block.scalar
                    def _(act):
                        act.wait_ge(s_c, 1)
                        act.activation(carry[:, :, 0:width], pc[:, :, 0:width], ACT.Copy).then_inc(s_e, 1)
                end_phase()

        class Totals:

            def __init__(self, tag, c, width):
                self.w = width
                self.pick = [sb(f"{tag}_pick{k}", [TC, 2, GT, EP], c=c) for k in range(2)]
                self.pcar = [pb(f"{tag}_pcar{k}", [EP, 512], c) for k in range(2)]
                self.s_pick, self.s_car, self.s_used = sem(f"{tag}_picked"), sem(f"{tag}_carries_placed"), sem(f"{tag}_carries_used")

            def pick_first(self, v, at):
                free(v, self.s_car, at, 2)
                shape = [TC, GT, EP]
                for h in range(2):
                    last = v.tensor_tensor(self.pick[at.pair()][:, h, :, :], first_row[:, h:h + 1, :].to_broadcast(shape),
                                           tile_sel[:, h, bass.ds(GT * at.n, GT)].rearrange("p (u a) -> p u a", a=1).to_broadcast(shape), ALU.mult)
                last.then_inc(self.s_pick, 1)

            def place(self, pe, at):
                k = at.pair()
                ready(pe, self.s_pick, at)
                free(pe, self.s_used, at, 2)
                for u in range(GT):
                    for h in range(2):
                        last = pe.matmul(self.pcar[k][:, u * self.w:(u + 1) * self.w], self.pick[k][:, h, u, :], carry[:, h, 0:self.w],
                                         start=(h == 0), stop=(h == 1))
                last.then_inc(self.s_car, 1)

            def add(self, v, at, U, to):
                ready(v, self.s_car, at)
                v.tensor_tensor(to, U[:, bass.ds(GT * at.n, GT), 0:self.w], by_tile(self.pcar[at.pair()], self.w), ALU.add).then_inc(self.s_used, 1)

        def send(pool, table, rows, idx, s_ready, s_put, top):
            def step(at):
                if is_item(at, GR):
                    ready(pool, s_ready, at)
                    seen(pool)
                    for u in range(GT):
                        pool.indirect_dma_start(table, bass.IndirectOffsetOnAxis(ap=idx[at.slot][:, u:u + 1], axis=0), rows[at.slot][:, u, :], None,
                                                bounds_check=top, oob_is_err=False).then_inc(s_put[at.slot], 16)
            pipeline(pool, GR, 0, step)
            for k in range(R):
                pool.wait_ge(s_put[k], 16 * GT * ((GR - 1 - k) // R + 1))

        lo = ExitStack()
        U = sb("l1_U", [EP, ET, D], c=lo)
        with ExitStack() as c:
            X = [sb(f"l1_x{k}", [EP, GT, D], c=c) for k in range(R)]
            C = [sb(f"l1_c{k}", [EP, GT, D], c=c) for k in range(R)]
            MSG = [sb(f"l1_msg{k}", [EP, GT, D], c=c) for k in range(2)]
            EA = [sb(f"l1_ea{k}", [EP, GT, 18], c=c) for k in range(R)]
            EAT = [sb(f"l1_eat{k}", [18, GE], c=c) for k in range(2)]
            HT = [sb(f"l1_ht{k}", [D + 1, GE], c=c) for k in range(2)]
            ST = [sb(f"l1_st{k}", [D, GE], c=c) for k in range(2)]
            S = [sb(f"l1_same{k}", [EP, GT, EP], c=c) for k in range(R)]
            ROW = [sb(f"l1_row{k}", [EP, GE], I32, c) for k in range(R)]
            idx = [sb(f"l1_idx{k}", [EP, GT], I32, c) for k in range(R)]
            norm = [Norm(f"l1{k}", c, EP, GT) for k in range(2)]
            pA = pb("l1_pa", [18, 512], c)
            pH = pb("l1_ph", [D, 512], c)
            pW = [pb(f"l1_pw{k}", [EP, 512], c) for k in range(2)]
            pS = [pb(f"l1_ps{k}", [D, 512], c) for k in range(2)]
            pU = [pb(f"l1_pu{k}", [EP, 512], c) for k in range(2)]
            s_one, s_vs = sem("l1_ones"), sem("l1_steps")
            s_row, s_ea, s_gat, s_staged = ring_sems("l1_rows_loaded"), ring_sems("l1_attr_loaded"), ring_sems("l1_gathered"), sem("l1_staged")
            s_same, s_c, s_msg = sem("l1_same_ready"), sem("l1_normed"), sem("l1_messages_ready")
            s_at, s_atc, s_h, s_hc, s_w = sem("l1_attr_turned"), sem("l1_attr_copied"), sem("l1_hidden"), sem("l1_hidden_copied"), sem("l1_weights_made")
            s_sum, s_sumc, s_u, s_uc = sem("l1_summed"), sem("l1_sums_copied"), sem("l1_multiplied"), sem("l1_kept")
            ea_groups = A["edge_attr_17"].rearrange("(g u p) k -> p g u k", u=GT, p=EP)

            with nc.Block() as block:
                @block.sync
                def _(sp):
                    sp.wait_ge(s_one, R + 2)

                    def step(at):
                        if is_item(at, GR):
                            free(sp, s_same, at, R)
                            sp_seen(sp)
                            sp.dma_start(ROW[at.slot][:, :], edge_row(A["dst"], at.n)).then_inc(s_row[at.slot], 16)
                            free(sp, s_at, at, R)
                            sp_seen(sp)
                            sp.dma_start(EA[at.slot][:, :, 0:17], one_group(ea_groups, at.n)).then_inc(s_ea[at.slot], 16)
                    pipeline(sp, GR, 0, step)

                @block.gpsimd
                def _(pool):
                    def step(at):
                        if is_item(at, GR):
                            ready(pool, s_staged, at)
                            seen(pool)
                            if not (at.fixed and at.n < R):
                                free(pool, s_c, at, R)
                                seen(pool)
                            for u in range(GT):
                                pool.indirect_dma_start(X[at.slot][:, u, :], None, x1, bass.IndirectOffsetOnAxis(ap=idx[at.slot][:, u:u + 1], axis=0)).then_inc(s_gat[at.slot], 16)
                    pipeline(pool, GR, 0, step)

                @block.scalar
                def _(act):
                    def step(at):
                        if is_item(at, GR):
                            ready(act, s_at, at)
                            free(act, s_h, at, 2)
                            act.activation(EAT[at.pair()][:, :], pA[:, 0:GE], ACT.Copy).then_inc(s_atc, 1)
                        o = at.back(1)
                        if is_item(o, GR):
                            ready(act, s_h, o)
                            free(act, s_w, o, 2)
                            act.activation(HT[o.pair()][0:D, :], pH[:, 0:GE], ACT.Relu).then_inc(s_hc, 1)
                        if is_item(at, GR):
                            norm[at.pair()].root(act, half_count(at), EP, GT)
                        o = at.back(3)
                        if is_item(o, GR):
                            ready(act, s_sum, o)
                            free(act, s_u, o, 2)
                            act.activation(ST[o.pair()][:, :], pS[o.pair()][:, 0:GE], ACT.Copy).then_inc(s_sumc, 1)
                        o = at.back(4)
                        if is_item(o, GR):
                            ready(act, s_u, o)
                            act.activation(U[:, bass.ds(GT * o.n, GT), :], by_tile(pU[o.pair()]), ACT.Copy).then_inc(s_uc, 1)
                    pipeline(act, GR, 4, step)

                @block.tensor
                def _(pe):
                    pe.wait_ge(s_one, R + 2)

                    def step(at):
                        if is_item(at, GR):
                            landed(pe, s_ea, at)
                            free(pe, s_atc, at, 1)
                            for u in range(GT):
                                last = pe.transpose(pA[:, u * EP:(u + 1) * EP], EA[at.slot][:, u, :], ident[0:EP, 0:EP])
                            last.then_inc(s_at, 1)
                        o = at.back(1)
                        if is_item(o, GR):
                            ready(pe, s_atc, o)
                            free(pe, s_hc, o, 1)
                            pe.matmul(pH[:, 0:GE], W1T[:, :], EAT[o.pair()][:, :], start=True, stop=True).then_inc(s_h, 1)
                        o = at.back(2)
                        if is_item(o, GR):
                            k = o.pair()
                            ready(pe, s_hc, o)
                            free(pe, s_msg, o, 2)
                            for u in range(GT):
                                last = pe.matmul(pW[k][:, u * D:(u + 1) * D], HT[k][:, u * EP:(u + 1) * EP], W2T[:, :], start=True, stop=True)
                            last.then_inc(s_w, 1)
                        o = at.back(3)
                        if is_item(o, GR):
                            k = o.pair()
                            ready(pe, s_same, o)
                            ready(pe, s_msg, o)
                            free(pe, s_sumc, o, 2)
                            for u in range(GT):
                                last = pe.matmul(pS[k][:, u * EP:(u + 1) * EP], MSG[k][:, u, :], S[o.slot][:, u, :], start=True, stop=True)
                            last.then_inc(s_sum, 1)
                        o = at.back(4)
                        if is_item(o, GR):
                            k = o.pair()
                            ready(pe, s_sumc, o)
                            free(pe, s_uc, o, 2)
                            for u in range(GT):
                                last = pe.matmul(pU[k][:, u * D:(u + 1) * D], ST[k][:, u * EP:(u + 1) * EP], WnT[:, :], start=True, stop=True)
                            last.then_inc(s_u, 1)
                    pipeline(pe, GR, 4, step)

                @block.vector
                def _(v):
                    me = Steps(v, s_vs)
                    for k in range(R):
                        v.memset(EA[k][:, :, 17:18], 1.0).then_inc(s_one, 1)
                    for k in range(2):
                        v.memset(HT[k][D:D + 1, :], 1.0).then_inc(s_one, 1)

                    def stage(at):
                        v.tensor_copy(idx[at.slot][:, :], src_i[:, bass.ds(GT * at.n, GT)]).then_inc(s_staged, 1)
                    for n in range(AHEAD):
                        stage(At(0, n))

                    def step(at):
                        if is_item(at, GR):
                            stage(at.back(-AHEAD))
                            landed(v, s_row, at)
                            free(v, s_sum, at, R)
                            same_target(v, S[at.slot], ROW[at.slot], at.n).then_inc(s_same, 1)
                            landed(v, s_gat, at, 16 * GT)
                            norm[at.pair()].stats(v, me, X[at.slot], EP, GT)
                        o = at.back(2)
                        if is_item(o, GR):
                            ready(v, s_w, o)
                            free(v, s_sum, o, 2)
                            v.scalar_tensor_tensor(MSG[o.pair()][:, :, :], C[o.slot][:, :, :], 0.0, by_tile(pW[o.pair()]), ALU.max, ALU.mult).then_inc(s_msg, 1)
                        if is_item(at, GR):
                            norm[at.pair()].invert(v, me, half_count(at), EP, GT)
                            norm[at.pair()].apply(v, me, X[at.slot], C[at.slot], EP, GT).then_inc(s_c, 1)
                            ready(v, s_c, at)
                    pipeline(v, GR, 2, step, me)

        carry_block(U, D, "l1")

        with ExitStack() as c:
            tot = Totals("l1b", c, D)
            H = [sb(f"l1b_h{k}", [EP, GT, D], c=c) for k in range(R)]
            idx = [sb(f"l1b_idx{k}", [EP, GT], I32, c) for k in range(R)]
            s_put = ring_sems("l1b_stored")
            with nc.Block() as block:
                @block.gpsimd
                def _(pool):
                    pool.wait_ge(agg1_ready, 16 * (PAIRS + 2))
                    send(pool, agg1, H, idx, tot.s_used, s_put, pool.to_reg(N - 1))

                @block.tensor
                def _(pe):
                    def step(at):
                        if is_item(at, GR):
                            tot.place(pe, at)
                    pipeline(pe, GR, 0, step)

                @block.vector
                def _(v):
                    def step(at):
                        if is_item(at, GR):
                            tot.pick_first(v, at)
                        o = at.back(1)
                        if is_item(o, GR):
                            left(v, s_put, o, 16 * GT)
                            v.tensor_copy(idx[o.slot][:, :], end_i[:, bass.ds(GT * o.n, GT)])
                            tot.add(v, o, U, H[o.slot][:, :, :])
                    pipeline(v, GR, 1, step)
        lo.close()

        def block_view(table, b, P, G, n=None):
            if isinstance(b, int):
                rows = table[BLK * b:BLK * b + P * G, :]
            else:
                rows = table[bass.ds(BLK * b, P * G), :]
            return rows.rearrange("(p g) f -> p (g f)", g=G)

        def halves(G):
            return [(0, 4), (4, G - 4)]

        def shape(at):
            return (TAILP, TAILG) if at.fixed and at.n == FULL else (NP, NG)

        def one_block(table, at):
            P, G = shape(at)
            return block_view(table, at.n, P, G)

        with ExitStack() as c:
            X = [sb(f"n1_x{k}", [NP, NG, D], c=c) for k in range(R)]
            AG = [sb(f"n1_ag{k}", [NP, NG, D], c=c) for k in range(R)]
            X2 = [sb(f"n1_x2{k}", [NP, NG, D], c=c) for k in range(R)]
            C1 = [sb(f"n1_c1{k}", [NP, NG, D], c=c) for k in range(2)]
            C2 = [sb(f"n1_c2{k}", [NP, NG, D], c=c) for k in range(2)]
            H1 = [sb(f"n1_h1{k}", [D + 1, NG, NP], c=c) for k in range(2)]
            H2 = [sb(f"n1_h2{k}", [D, NG, NP], c=c) for k in range(2)]
            F = [sb(f"n1_f{k}", [D, NG, NP], c=c) for k in range(2)]
            norm = [Norm(f"n1{k}", c, NP, 2 * NG) for k in range(2)]
            LAG = 3
            pT1 = pb("n1_pt1", [D, 2, 512], c)
            pZ = pb("n1_pz", [NP, 2, 512], c)
            pT2 = pb("n1_pt2", [D, 2, 512], c)
            pF = pb("n1_pf", [D, 2, 512], c)
            s_one, s_vs = sem("n1_ones"), sem("n1_steps")
            s_x, s_a, s_st = ring_sems("n1_x_loaded"), ring_sems("n1_agg_loaded"), ring_sems("n1_stored")
            s_var, s_root, s_m, s_d1, s_c1, s_t1, s_h1, s_z, s_x2 = (sem(f"n1_{n}") for n in ("variances_ready", "roots_ready", "norms_ready", "c1_centred", "c1_ready", "c1_turned", "h1_ready", "z_made", "x2_ready"))
            s_d2, s_c2, s_t2, s_h2, s_f, s_fr, s_fs = (sem(f"n1_{n}") for n in ("c2_centred", "c2_ready", "c2_turned", "h2_ready", "f_made", "f_relu", "f_counted"))

            def parts(at):
                mine = [(shape(o)[0], first, first + shape(o)[1]) for o, first in ((at, 0), (at.back(LAG), NG)) if is_item(o, NB)]
                return [(NP, 0, 2 * NG)] if mine == [(NP, 0, NG), (NP, NG, 2 * NG)] else mine

            def combine(v, me, at):
                T = norm[at.pair()]
                st, w = T.st, T.w
                me.settle()
                for P, a, z in parts(at):
                    me.done(v.tensor_tensor(w[0:P, 0, a:z], st[0:P, a:z, 1], st[0:P, a:z, 4], ALU.add))
                    me.done(v.tensor_tensor(w[0:P, 1, a:z], st[0:P, a:z, 1], st[0:P, a:z, 4], ALU.subtract))
                    me.done(v.tensor_tensor(w[0:P, 2, a:z], st[0:P, a:z, 2], st[0:P, a:z, 5], ALU.add))
                me.settle()
                for P, a, z in parts(at):
                    me.done(v.tensor_scalar(T.mean[0:P, a:z], w[0:P, 0, a:z], 0.5, None, ALU.mult))
                    me.done(v.tensor_tensor(w[0:P, 3, a:z], w[0:P, 1, a:z], w[0:P, 1, a:z], ALU.mult))
                me.settle()
                for P, a, z in parts(at):
                    last = v.scalar_tensor_tensor(w[0:P, 4, a:z], w[0:P, 3, a:z], D / 4.0, w[0:P, 2, a:z], ALU.mult, ALU.add)
                last.then_inc(s_var, 1)

            def over_row(what, P, a, G):
                return what[0:P, a:a + G].rearrange("p (g a) -> p g a", a=1).to_broadcast([P, G, D])

            with nc.Block() as block:
                @block.sync
                def _(sp):
                    def step(at):
                        if is_item(at, NB):
                            P, G = shape(at)
                            free(sp, s_x2, at, R)
                            sp_seen(sp)
                            sp.dma_start(X[at.slot][0:P, 0:G, :].rearrange("p g f -> p (g f)"), one_block(x1, at)).then_inc(s_x[at.slot], 16)
                            free(sp, s_z, at, R)
                            sp_seen(sp)
                            sp.dma_start(AG[at.slot][0:P, 0:G, :].rearrange("p g f -> p (g f)"), one_block(agg1, at)).then_inc(s_a[at.slot], 16)
                        o = at.back(R)
                        if is_item(o, NB):
                            P, G = shape(o)
                            ready(sp, s_x2, o)
                            sp_seen(sp)
                            sp.dma_start(one_block(x2, o), X2[o.slot][0:P, 0:G, :].rearrange("p g f -> p (g f)")).then_inc(s_st[o.slot], 16)
                    pipeline(sp, NB, R, step)
                    for k in range(R):
                        sp.wait_ge(s_st[k], 16 * ((NB - 1 - k) // R + 1))

                @block.gpsimd
                def _(pool):
                    def normalise(at, T, a, src, C, s_d, s_c, s_turned):
                        P, G = shape(at)
                        k = at.pair()
                        if not (at.fixed and at.n < 2):
                            free(pool, s_turned, at, 2)
                            seen(pool)
                        pool.tensor_tensor(C[k][0:P, 0:G, :], src[at.slot][0:P, 0:G, :], over_row(T.mean, P, a, G), ALU.subtract).then_inc(s_d, 1)
                        ready(pool, s_d, at)
                        seen(pool)
                        pool.tensor_tensor(C[k][0:P, 0:G, :], C[k][0:P, 0:G, :], over_row(T.rstd, P, a, G), ALU.mult).then_inc(s_c, 1)

                    def step(at):
                        ready(pool, s_m, at)
                        seen(pool)
                        if is_item(at, NB):
                            normalise(at, norm[at.pair()], 0, X, C1, s_d1, s_c1, s_t1)
                        o = at.back(LAG)
                        if is_item(o, NB):
                            normalise(o, norm[at.pair()], NG, X2, C2, s_d2, s_c2, s_t2)
                    pipeline(pool, NB, LAG, step)

                @block.scalar
                def _(act):
                    def turned(at, p, H, func, s_t, s_used, s_h):
                        P, G = shape(at)
                        k = at.pair()
                        ready(act, s_t, at)
                        free(act, s_used, at, 2)
                        for h, (g0, n) in enumerate(halves(G)):
                            last = act.activation(H[k][0:D, g0:g0 + n, 0:P], p[:, h, 0:n * P].rearrange("p (g n) -> p g n", g=n), func)
                        last.then_inc(s_h, 1)

                    def step(at):
                        o = at.back(LAG + 2)
                        if is_item(o, NB):
                            turned(o, pT2, H2, ACT.Relu, s_t2, s_f, s_h2)
                        o = at.back(2)
                        if is_item(o, NB):
                            turned(o, pT1, H1, ACT.Relu, s_t1, s_z, s_h1)
                        o = at.back(LAG + 2)
                        if is_item(o, NB):
                            P, G = shape(o)
                            ready(act, s_f, o)
                            free(act, s_fs, o, 2)
                            for h, (g0, n) in enumerate(halves(G)):
                                last = act.activation(F[o.pair()][:, g0:g0 + n, 0:P], pF[:, h, 0:n * P].rearrange("p (g n) -> p g n", g=n), ACT.Relu,
                                                      bias=cols[:, B_NODE:B_NODE + 1])
                            last.then_inc(s_fr, 1)
                        if parts(at):
                            ready(act, s_var, at)
                            w = norm[at.pair()].w
                            for P, a, z in parts(at):
                                last = act.activation(w[0:P, 5, a:z], w[0:P, 4, a:z], ACT.Sqrt, bias=eps_col[0:P, :], scale=1.0 / D)
                            last.then_inc(s_root, 1)
                    pipeline(act, NB, LAG + 2, step)

                @block.tensor
                def _(pe):
                    pe.wait_ge(s_one, 2)

                    def turn(at, C, p, s_c, s_h, s_t):
                        P, G = shape(at)
                        ready(pe, s_c, at)
                        free(pe, s_h, at, 1)
                        for g in range(G):
                            last = pe.transpose(p[:, g // 4, (g % 4) * P:(g % 4 + 1) * P], C[at.pair()][0:P, g, :], ident[0:P, 0:P])
                        last.then_inc(s_t, 1)

                    def step(at):
                        o = at.back(LAG + 2)
                        if is_item(o, NB):
                            turn(o, C2, pT2, s_c2, s_h2, s_t2)
                        o = at.back(2)
                        if is_item(o, NB):
                            turn(o, C1, pT1, s_c1, s_h1, s_t1)
                        o = at.back(LAG + 2)
                        if is_item(o, NB):
                            P, G = shape(o)
                            ready(pe, s_h2, o)
                            free(pe, s_fr, o, 1)
                            for h, (g0, n) in enumerate(halves(G)):
                                last = pe.matmul(pF[:, h, 0:n * P], Wnode[0:D, :], H2[o.pair()][:, g0:g0 + n, 0:P], start=True, stop=True)
                            last.then_inc(s_f, 1)
                        o = at.back(2)
                        if is_item(o, NB):
                            P, G = shape(o)
                            ready(pe, s_h1, o)
                            landed(pe, s_a, o)
                            free(pe, s_x2, o, 1)
                            for g in range(G):
                                to = slice((g % 4) * D, (g % 4 + 1) * D)
                                pe.matmul(pZ[0:P, g // 4, to], H1[o.pair()][:, g, 0:P], WsT[:, :], start=True, stop=False)
                                last = pe.matmul(pZ[0:P, g // 4, to], ident[0:P, 0:P], AG[o.slot][0:P, g, :], start=False, stop=True)
                            last.then_inc(s_z, 1)
                    pipeline(pe, NB, LAG + 2, step)

                @block.vector
                def _(v):
                    me = Steps(v, s_vs)
                    for k in range(2):
                        v.memset(H1[k][D:D + 1, :, :], 1.0).then_inc(s_one, 1)

                    def step(at):
                        o = at.back(3)
                        if is_item(o, NB):
                            P, G = shape(o)
                            ready(v, s_z, o)
                            left(v, s_st, o)
                            free(v, s_c2, o, R)
                            for h, (g0, n) in enumerate(halves(G)):
                                last = v.scalar_tensor_tensor(X2[o.slot][0:P, g0:g0 + n, :], pZ[0:P, h, 0:n * D].rearrange("p (g f) -> p g f", g=n), 0.0,
                                                              X[o.slot][0:P, g0:g0 + n, :], ALU.max, ALU.add)
                            last.then_inc(s_x2, 1)
                            ready(v, s_x2, o)
                            free(v, s_c2, o, 2)
                            for g in range(G):
                                me.done(v.bn_stats(norm[at.pair()].st[0:P, NG + g, :], X2[o.slot][0:P, g, :]))
                        if is_item(at, NB):
                            P, G = shape(at)
                            landed(v, s_x, at)
                            free(v, s_c1, at, 2)
                            for g in range(G):
                                me.done(v.bn_stats(norm[at.pair()].st[0:P, g, :], X[at.slot][0:P, g, :]))
                        if parts(at):
                            combine(v, me, at)
                        o = at.back(LAG + 3)
                        if is_item(o, NB):
                            P, G = shape(o)
                            ready(v, s_fr, o)
                            for h, (g0, n) in enumerate(halves(G)):
                                f = F[o.pair()][:, g0:g0 + n, :].rearrange("p g n -> p (g n)") if P == NP else F[o.pair()][:, g0:g0 + n, 0:P]
                                last = v.bn_stats(f_stats[:, bass.ds(2 * o.n + h, 1), :].rearrange("p a s -> p (a s)"), f)
                            last.then_inc(s_fs, 1)
                        if parts(at):
                            T = norm[at.pair()]
                            ready(v, s_root, at)
                            for P, a, z in parts(at):
                                me.done(v.reciprocal(T.rstd[0:P, a:z], T.w[0:P, 5, a:z]))
                            me.settle()
                            v.sem_inc(s_m, 1)
                        o = at.back(LAG)
                        if is_item(o, NB):
                            P, G = shape(o)
                            where = bass.ds(o.n, 1)
                            me.done(v.tensor_copy(mean_n[0:P, where, 0:G].rearrange("p a g -> p (a g)"), T.mean[0:P, NG:NG + G]))
                            me.done(v.tensor_copy(rstd_n[0:P, where, 0:G].rearrange("p a g -> p (a g)"), T.rstd[0:P, NG:NG + G]))
                    pipeline(v, NB, LAG + 3, step, me)

        def fold(v, me, stats, g, beta, ac, root, root_ready, turn):
            me.done(v.bn_aggr(bn_w[:, 0:2], stats))
            me.settle()
            me.done(v.tensor_scalar(bn_w[:, 2:3], bn_w[:, 1:2], BN_EPS, None, ALU.add))
            me.settle()
            v.sem_inc(root, 1)
            v.wait_ge(root_ready, turn)
            me.done(v.reciprocal(bn_w[:, 3:4], bn_w[:, 3:4]))
            me.settle()
            me.done(v.tensor_tensor(ac[:, 0:1], bn_w[:, 3:4], cols[:, g:g + 1], ALU.mult))
            me.settle()
            me.done(v.tensor_tensor(bn_w[:, 2:3], bn_w[:, 0:1], ac[:, 0:1], ALU.mult))
            me.settle()
            me.done(v.tensor_tensor(ac[:, 1:2], cols[:, beta:beta + 1], bn_w[:, 2:3], ALU.subtract))
            me.settle()

        def affine_rows(pe, p, ac, done):
            for j in range(2):
                last = pe.matmul(p[:, j * D:(j + 1) * D], ac[:, j:j + 1].to_broadcast([D, NP]), ident[0:D, 0:D], start=True, stop=True)
            last.then_inc(done, 1)

        with ExitStack() as c:
            pA = pb("bn_pa", [NP, 512], c)
            pB = pb("bn_pb", [D, 512], c)
            s_vs, s_var, s_root, s_ac, s_mm = (sem(f"bn_{n}") for n in ("steps", "var_ready", "root_ready", "folded", "multiplied"))
            with nc.Block() as block:
                @block.scalar
                def _(act):
                    for n in range(2):
                        act.wait_ge(s_var, n + 1)
                        act.activation(bn_w[:, 3:4], bn_w[:, 2:3], ACT.Sqrt).then_inc(s_root, 1)

                @block.vector
                def _(v):
                    me = Steps(v, s_vs)
                    fold(v, me, f_stats[:, :, :].rearrange("p a s -> p (a s)"), G_NODE, BETA_NODE, node_ac, s_var, s_root, 1)
                    fold(v, me, e_stats[:, :, :].rearrange("p a s -> p (a s)"), G_EDGE, BETA_EDGE, edge_ac, s_var, s_root, 2)
                    me.done(v.tensor_scalar(Wc[:, :], Wmsg[:, 2, :], edge_ac[:, 0:1], None, ALU.mult))
                    me.settle()
                    v.sem_inc(s_ac, 1)
                    v.wait_ge(s_mm, 2)
                    me.done(v.tensor_copy(affine[:, 0:2, :], pA[:, 0:2 * D].rearrange("p (a f) -> p a f", a=2)))
                    me.done(v.tensor_tensor(msg_bias[:, :], pB[:, 0:1], cols[:, B_MSG:B_MSG + 1], ALU.add))
                    me.settle()

                @block.tensor
                def _(pe):
                    pe.wait_ge(s_ac, 1)
                    affine_rows(pe, pA, node_ac, s_mm)
                    pe.matmul(pB[:, 0:1], Wmsg[:, 2, :], edge_ac[:, 1:2], start=True, stop=True).then_inc(s_mm, 1)
            end_phase()

        with ExitStack() as c:
            X = [sb(f"n2_x{k}", [NP, NG, D], c=c) for k in range(R)]
            XC = [sb(f"n2_xc{k}", [NP, NG, D], c=c) for k in range(R)]
            CN = [sb(f"n2_cn{k}", [NP, NG, D], c=c) for k in range(2)]
            C2 = [sb(f"n2_c{k}", [NP, NG, D], c=c) for k in range(2)]
            Y = [sb(f"n2_y{k}", [NP, NG, D], c=c) for k in range(2)]
            O = [sb(f"n2_o{k}", [NP, NG, D], c=c) for k in range(R)]
            H2 = [sb(f"n2_h{k}", [D + 1, NG, NP], c=c) for k in range(2)]
            pT = [pb(f"n2_pt{k}", [D, 2, 512], c) for k in range(2)]
            pZ = [pb(f"n2_pz{k}", [NP, 2, 512], c) for k in range(2)]
            s_one, s_x, s_st = sem("n2_ones"), ring_sems("n2_x_loaded"), ring_sems("n2_stored")
            s_cn, s_c, s_t, s_h, s_z, s_y, s_xc, s_o = (sem(f"n2_{n}") for n in ("centred", "c_ready", "c_turned", "h_ready", "z_made", "y_ready", "xc_ready", "o_ready"))

            def kept(what, at, P, G):
                return what[0:P, bass.ds(at.n, 1), 0:G].rearrange("p a g -> p g a").to_broadcast([P, G, D])

            with nc.Block() as block:
                @block.sync
                def _(sp):
                    def step(at):
                        if is_item(at, NB):
                            P, G = shape(at)
                            free(sp, s_xc, at, R)
                            sp_seen(sp)
                            sp.dma_start(X[at.slot][0:P, 0:G, :].rearrange("p g f -> p (g f)"), one_block(x2, at)).then_inc(s_x[at.slot], 16)
                    pipeline(sp, NB, 0, step)

                @block.gpsimd
                def _(pool):
                    def step(at):
                        if is_item(at, NB):
                            P, G = shape(at)
                            landed(pool, s_x, at)
                            seen(pool)
                            if not (at.fixed and at.n < 2):
                                free(pool, s_c, at, 2)
                                seen(pool)
                            pool.tensor_tensor(CN[at.pair()][0:P, 0:G, :], X[at.slot][0:P, 0:G, :], kept(mean_n, at, P, G), ALU.subtract).then_inc(s_cn, 1)
                            if not (at.fixed and at.n < R):
                                free(pool, s_o, at, R)
                                seen(pool)
                            pool.tensor_tensor(XC[at.slot][0:P, 0:G, :], X[at.slot][0:P, 0:G, :],
                                               affine[0:P, 1:2, :].to_broadcast([P, G, D]), ALU.add).then_inc(s_xc, 1)
                    pipeline(pool, NB, 0, step)

                @block.scalar
                def _(act):
                    def step(at):
                        o = at.back(1)
                        if is_item(o, NB):
                            P, G = shape(o)
                            ready(act, s_t, o)
                            free(act, s_z, o, 2)
                            for h, (g0, n) in enumerate(halves(G)):
                                last = act.activation(H2[o.pair()][0:D, g0:g0 + n, 0:P], pT[o.pair()][:, h, 0:n * P].rearrange("p (g n) -> p g n", g=n), ACT.Relu)
                            last.then_inc(s_h, 1)
                        o = at.back(3)
                        if is_item(o, NB):
                            P, G = shape(o)
                            ready(act, s_o, o)
                            act.dma_start(one_block(out, o), O[o.slot][0:P, 0:G, :].rearrange("p g f -> p (g f)")).then_inc(s_st[o.slot], 16)
                    pipeline(act, NB, 3, step)
                    for k in range(R):
                        act.wait_ge(s_st[k], 16 * ((NB - 1 - k) // R + 1))

                @block.tensor
                def _(pe):
                    pe.wait_ge(s_one, 2)

                    def step(at):
                        if is_item(at, NB):
                            P, G = shape(at)
                            ready(pe, s_c, at)
                            free(pe, s_h, at, 2)
                            for g in range(G):
                                last = pe.transpose(pT[at.pair()][:, g // 4, (g % 4) * P:(g % 4 + 1) * P], C2[at.pair()][0:P, g, :], ident[0:P, 0:P])
                            last.then_inc(s_t, 1)
                        o = at.back(1)
                        if is_item(o, NB):
                            P, G = shape(o)
                            ready(pe, s_h, o)
                            free(pe, s_y, o, 2)
                            for g in range(G):
                                last = pe.matmul(pZ[o.pair()][0:P, g // 4, (g % 4) * D:(g % 4 + 1) * D], H2[o.pair()][:, g, 0:P], Wnode[:, :], start=True, stop=True)
                            last.then_inc(s_z, 1)
                    pipeline(pe, NB, 1, step)

                @block.vector
                def _(v):
                    for k in range(2):
                        v.memset(H2[k][D:D + 1, :, :], 1.0).then_inc(s_one, 1)

                    def step(at):
                        if is_item(at, NB):
                            P, G = shape(at)
                            k = at.pair()
                            ready(v, s_cn, at)
                            free(v, s_t, at, 2)
                            v.tensor_tensor(C2[k][0:P, 0:G, :], CN[k][0:P, 0:G, :], kept(rstd_n, at, P, G), ALU.mult).then_inc(s_c, 1)
                        o = at.back(2)
                        if is_item(o, NB):
                            P, G = shape(o)
                            k = o.pair()
                            ready(v, s_z, o)
                            for h, (g0, n) in enumerate(halves(G)):
                                last = v.scalar_tensor_tensor(Y[k][0:P, g0:g0 + n, :], pZ[k][0:P, h, 0:n * D].rearrange("p (g f) -> p g f", g=n), 0.0,
                                                              affine[0:P, 0:1, :].to_broadcast([P, n, D]), ALU.max, ALU.mult)
                            last.then_inc(s_y, 1)
                            ready(v, s_y, o)
                            ready(v, s_xc, o)
                            left(v, s_st, o)
                            v.tensor_tensor(O[o.slot][0:P, 0:G, :], Y[k][0:P, 0:G, :], XC[o.slot][0:P, 0:G, :], ALU.add).then_inc(s_o, 1)
                    pipeline(v, NB, 2, step)

        def stage_both(v, idx, at, s_staged):
            v.tensor_copy(idx[at.slot][:, 0, :], src_i[:, bass.ds(GT * at.n, GT)])
            v.tensor_copy(idx[at.slot][:, 1, :], dst_i[:, bass.ds(GT * at.n, GT)]).then_inc(s_staged, 1)

        def gather_both(pool, X, table, idx, s_staged, s_done, s_gat):
            def step(at):
                if is_item(at, GR):
                    ready(pool, s_staged, at)
                    seen(pool)
                    if not (at.fixed and at.n < R):
                        free(pool, s_done, at, R)
                        seen(pool)
                    for h in range(2):
                        for u in range(GT):
                            pool.indirect_dma_start(X[at.slot][:, h * GT + u, :], None, table,
                                                    bass.IndirectOffsetOnAxis(ap=idx[at.slot][:, h, u:u + 1], axis=0)).then_inc(s_gat[at.slot], 16)
            pipeline(pool, GR, 0, step)

        def load_kept(sp, KP, s_used, s_kp):
            def step(at):
                if is_item(at, GR):
                    free(sp, s_used, at, R)
                    sp_seen(sp)
                    sp.dma_start(KP[at.slot][:, :, :], one_group(keep_groups, at.n)).then_inc(s_kp[at.slot], 16)
            pipeline(sp, GR, 0, step)

        hi = ExitStack()
        U = sb("l2_U", [EP, ET, WU], c=hi)
        with ExitStack() as c:
            X = [sb(f"l2_x{k}", [EP, 2 * GT, D], c=c) for k in range(R)]
            C = [sb(f"l2_c{k}", [EP, 2 * GT, D], c=c) for k in range(2)]
            HT = [sb(f"l2_ht{k}", [D + 1, 2, GE], c=c) for k in range(2)]
            E4 = [sb(f"l2_e4{k}", [EP, GT, 5], c=c) for k in range(R)]
            E4T = sb("l2_e4t", [5, GE], c=c)
            EF = [sb(f"l2_ef{k}", [D, GE], c=c) for k in range(2)]
            RT = [sb(f"l2_rt{k}", [D, GE], c=c) for k in range(2)]
            RN = sb("l2_rn", [EP, GT, D + 1], c=c)
            B = [sb(f"l2_base{k}", [EP, GT, D], c=c) for k in range(R)]
            S = [sb(f"l2_same{k}", [EP, GT, EP], c=c) for k in range(R)]
            ROW = [sb(f"l2_row{k}", [EP, GE], I32, c) for k in range(R)]
            idx = [sb(f"l2_idx{k}", [EP, 2, GT], I32, c) for k in range(R)]
            norm = [Norm(f"l2{k}", c, EP, 2 * GT) for k in range(2)]
            pT = pb("l2_pt", [D, 2, 512], c)
            pE = pb("l2_pe", [D, 512], c)
            pR = pb("l2_pr", [D, 512], c)
            pN = pb("l2_pn", [EP, 512], c)
            pF = pb("l2_pf", [EP, 512], c)
            pU = pb("l2_pu", [EP, 512], c)
            s_one, s_vs = sem("l2_ones"), sem("l2_steps")
            s_row, s_e4, s_gat, s_keep = ring_sems("l2_row_loaded"), ring_sems("l2_attr_loaded"), ring_sems("l2_gathered"), ring_sems("l2_base_stored")
            s_staged, s_same, s_c, s_b = (sem(f"l2_{n}") for n in ("staged", "same_ready", "normed", "base_ready"))
            s_t, s_h, s_et, s_etc, s_ef, s_efc = (sem(f"l2_{n}") for n in ("turned", "h_ready", "attr_turned", "attr_copied", "ef_made", "ef_relu"))
            s_r, s_rr, s_rs, s_n, s_nc, s_f, s_u, s_uc = (sem(f"l2_{n}") for n in ("r_made", "r_relu", "r_counted", "r_turned", "rn_ready", "f_made", "summed", "sums_kept"))

            with nc.Block() as block:
                @block.sync
                def _(sp):
                    sp.wait_ge(s_one, R + 3)

                    def step(at):
                        if is_item(at, GR):
                            free(sp, s_same, at, R)
                            sp_seen(sp)
                            sp.dma_start(ROW[at.slot][:, :], edge_row(A["dst"], at.n)).then_inc(s_row[at.slot], 16)
                            free(sp, s_et, at, R)
                            sp_seen(sp)
                            sp.dma_start(E4[at.slot][:, :, 0:4], one_group(e4_groups, at.n)).then_inc(s_e4[at.slot], 16)
                        o = at.back(R)
                        if is_item(o, GR):
                            ready(sp, s_b, o)
                            sp_seen(sp)
                            sp.dma_start(one_group(keep_groups, o.n), B[o.slot][:, :, :]).then_inc(s_keep[o.slot], 16)
                    pipeline(sp, GR, R, step)
                    for k in range(R):
                        sp.wait_ge(s_keep[k], 16 * ((GR - 1 - k) // R + 1))

                @block.gpsimd
                def _(pool):
                    gather_both(pool, X, x2, idx, s_staged, s_b, s_gat)

                @block.scalar
                def _(act):
                    def step(at):
                        o = at.back(1)
                        if is_item(o, GR):
                            ready(act, s_t, o)
                            free(act, s_r, o, 2)
                            act.activation(HT[o.pair()][0:D, :, :], pT[:, :, 0:GE], ACT.Relu).then_inc(s_h, 1)
                        if is_item(at, GR):
                            ready(act, s_et, at)
                            free(act, s_ef, at, 1)
                            act.activation(E4T[:, :], pE[0:5, 0:GE], ACT.Copy).then_inc(s_etc, 1)
                            norm[at.pair()].root(act, half_count(at), EP, 2 * GT)
                        o = at.back(2)
                        if is_item(o, GR):
                            ready(act, s_r, o)
                            free(act, s_rs, o, 2)
                            free(act, s_n, o, 2)
                            act.activation(RT[o.pair()][:, :], pR[:, 0:GE], ACT.Relu, bias=msg_bias[:, :]).then_inc(s_rr, 1)
                        o = at.back(3)
                        if is_item(o, GR):
                            ready(act, s_n, o)
                            free(act, s_u, o, 1)
                            act.activation(RN[:, :, 0:D], by_tile(pN), ACT.Copy).then_inc(s_nc, 1)
                        if is_item(at, GR):
                            ready(act, s_ef, at)
                            free(act, s_r, at, 2)
                            act.activation(EF[at.pair()][:, :], pE[:, 0:GE], ACT.Relu).then_inc(s_efc, 1)
                        if is_item(o, GR):
                            ready(act, s_u, o)
                            act.activation(U[:, bass.ds(GT * o.n, GT), 0:D + 1], by_tile(pU, D + 1), ACT.Copy).then_inc(s_uc, 1)
                    pipeline(act, GR, 3, step)

                @block.tensor
                def _(pe):
                    pe.wait_ge(s_one, R + 3)

                    def step(at):
                        o = at.back(1)
                        if is_item(o, GR):
                            ready(pe, s_c, o)
                            free(pe, s_h, o, 1)
                            for h in range(2):
                                for u in range(GT):
                                    last = pe.transpose(pT[:, h, u * EP:(u + 1) * EP], C[o.pair()][:, h * GT + u, :], ident[0:EP, 0:EP])
                            last.then_inc(s_t, 1)
                        if is_item(at, GR):
                            landed(pe, s_e4, at)
                            free(pe, s_efc, at, 1)
                            for u in range(GT):
                                last = pe.transpose(pE[0:5, u * EP:(u + 1) * EP], E4[at.slot][:, u, :], ident[0:EP, 0:EP])
                            last.then_inc(s_et, 1)
                        o = at.back(2)
                        if is_item(o, GR):
                            k = o.pair()
                            ready(pe, s_h, o)
                            free(pe, s_b, o, 1)
                            for u in range(GT):
                                last = pe.matmul(pF[:, u * D:(u + 1) * D], HT[k][:, 1, u * EP:(u + 1) * EP], Wnode[:, :], start=True, stop=True)
                            last.then_inc(s_f, 1)
                            ready(pe, s_efc, o)
                            free(pe, s_rr, o, 1)
                            pe.matmul(pR[:, 0:GE], Wmsg[:, 0, :], HT[k][0:D, 0, :], start=True, stop=False)
                            pe.matmul(pR[:, 0:GE], Wmsg[:, 1, :], HT[k][0:D, 1, :], start=False, stop=False)
                            pe.matmul(pR[:, 0:GE], Wc[:, :], EF[k][:, :], start=False, stop=True).then_inc(s_r, 1)
                        o = at.back(3)
                        if is_item(o, GR):
                            ready(pe, s_rr, o)
                            free(pe, s_nc, o, 1)
                            for u in range(GT):
                                last = pe.transpose(pN[:, u * D:(u + 1) * D], RT[o.pair()][:, u * EP:(u + 1) * EP], ident[0:D, 0:D])
                            last.then_inc(s_n, 1)
                        if is_item(at, GR):
                            ready(pe, s_etc, at)
                            pe.matmul(pE[:, 0:GE], Wedge[:, :], E4T[:, :], start=True, stop=True).then_inc(s_ef, 1)
                        if is_item(o, GR):
                            ready(pe, s_nc, o)
                            ready(pe, s_same, o)
                            free(pe, s_uc, o, 1)
                            for u in range(GT):
                                last = pe.matmul(pU[:, u * (D + 1):(u + 1) * (D + 1)], S[o.slot][:, u, :], RN[:, u, :], start=True, stop=True)
                            last.then_inc(s_u, 1)
                    pipeline(pe, GR, 3, step)

                @block.vector
                def _(v):
                    me = Steps(v, s_vs)
                    for k in range(R):
                        v.memset(E4[k][:, :, 4:5], 1.0).then_inc(s_one, 1)
                    for k in range(2):
                        v.memset(HT[k][D:D + 1, :, :], 1.0).then_inc(s_one, 1)
                    v.memset(RN[:, :, D:D + 1], 1.0).then_inc(s_one, 1)
                    for n in range(AHEAD):
                        stage_both(v, idx, At(0, n), s_staged)

                    def step(at):
                        if is_item(at, GR):
                            stage_both(v, idx, at.back(-AHEAD), s_staged)
                            landed(v, s_row, at)
                            free(v, s_u, at, R)
                            same_target(v, S[at.slot], ROW[at.slot], at.n).then_inc(s_same, 1)
                            landed(v, s_gat, at, 32 * GT)
                            norm[at.pair()].stats(v, me, X[at.slot], EP, 2 * GT)
                        o = at.back(3)
                        if is_item(o, GR):
                            ready(v, s_rr, o)
                            v.bn_stats(r_stats[:, bass.ds(o.n, 1), :].rearrange("p a s -> p (a s)"), RT[o.pair()][:, :]).then_inc(s_rs, 1)
                        if is_item(at, GR):
                            norm[at.pair()].invert(v, me, half_count(at), EP, 2 * GT)
                            free(v, s_t, at, 2)
                            norm[at.pair()].apply(v, me, X[at.slot], C[at.pair()], EP, 2 * GT).then_inc(s_c, 1)
                            ready(v, s_c, at)
                        o = at.back(2)
                        if is_item(o, GR):
                            ready(v, s_f, o)
                            left(v, s_keep, o)
                            to = B[o.slot][:, :, :]
                            row = lambda j: affine[0:EP, j:j + 1, :].to_broadcast([EP, GT, D])
                            me.done(v.scalar_tensor_tensor(to, by_tile(pF), 0.0, row(0), ALU.max, ALU.mult))
                            me.settle()
                            me.done(v.tensor_tensor(to, to, row(1), ALU.add))
                            me.settle()
                            v.tensor_tensor(to, to, X[o.slot][:, GT:2 * GT, :], ALU.add).then_inc(s_b, 1)
                    pipeline(v, GR, 3, step, me)

        carry_block(U, D + 1, "l2")

        with ExitStack() as c:
            pA = pb("bm_pa", [NP, 512], c)
            s_vs, s_var, s_root, s_ac, s_mm = (sem(f"bm_{n}") for n in ("steps", "var_ready", "root_ready", "folded", "multiplied"))
            with nc.Block() as block:
                @block.scalar
                def _(act):
                    act.wait_ge(s_var, 1)
                    act.activation(bn_w[:, 3:4], bn_w[:, 2:3], ACT.Sqrt).then_inc(s_root, 1)

                @block.vector
                def _(v):
                    me = Steps(v, s_vs)
                    fold(v, me, r_stats[:, :, :].rearrange("p a s -> p (a s)"), G_MSG, BETA_MSG, msg_ac, s_var, s_root, 1)
                    v.sem_inc(s_ac, 1)
                    v.wait_ge(s_mm, 1)
                    me.done(v.tensor_copy(affine[:, 2:4, :], pA[:, 0:2 * D].rearrange("p (a f) -> p a f", a=2)))
                    me.settle()

                @block.tensor
                def _(pe):
                    pe.wait_ge(s_ac, 1)
                    affine_rows(pe, pA, msg_ac, s_mm)
            end_phase()

        with ExitStack() as c:
            tot = Totals("l2b", c, D + 1)
            T = [sb(f"l2b_t{k}", [EP, GT, D + 1], c=c) for k in range(2)]
            KP = [sb(f"l2b_keep{k}", [EP, GT, D], c=c) for k in range(R)]
            W = [sb(f"l2b_w{k}", [EP, GT, D], c=c) for k in range(2)]
            X3 = [sb(f"l2b_x3{k}", [EP, GT, D], c=c) for k in range(R)]
            idx = [sb(f"l2b_idx{k}", [EP, GT], I32, c) for k in range(R)]
            s_vs, s_kp, s_put, s_x3 = sem("l2b_steps"), ring_sems("l2b_keep_loaded"), ring_sems("l2b_stored"), sem("l2b_x3_ready")
            with nc.Block() as block:
                @block.sync
                def _(sp):
                    load_kept(sp, KP, s_x3, s_kp)

                @block.gpsimd
                def _(pool):
                    send(pool, out, X3, idx, s_x3, s_put, pool.to_reg(N - 1))

                @block.tensor
                def _(pe):
                    def step(at):
                        if is_item(at, GR):
                            tot.place(pe, at)
                    pipeline(pe, GR, 0, step)

                @block.vector
                def _(v):
                    me = Steps(v, s_vs)

                    def step(at):
                        if is_item(at, GR):
                            tot.pick_first(v, at)
                        o = at.back(1)
                        if is_item(o, GR):
                            k = o.pair()
                            tot.add(v, o, U, T[k][:, :, :])
                            left(v, s_put, o, 16 * GT)
                            v.tensor_copy(idx[o.slot][:, :], end_i[:, bass.ds(GT * o.n, GT)])
                            ready(v, tot.s_used, o)
                            me.done(v.tensor_tensor(W[k][:, :, :], T[k][:, :, 0:D], affine[0:EP, 2:3, :].to_broadcast([EP, GT, D]), ALU.mult))
                            landed(v, s_kp, o)
                            for u in range(GT):
                                me.done(v.scalar_tensor_tensor(X3[o.slot][:, u, :], affine[0:EP, 3, :], T[k][:, u, D:D + 1], KP[o.slot][:, u, :], ALU.mult, ALU.add))
                            me.settle()
                            v.tensor_tensor(X3[o.slot][:, :, :], X3[o.slot][:, :, :], W[k][:, :, :], ALU.add).then_inc(s_x3, 1)
                    pipeline(v, GR, 1, step, me)

        with ExitStack() as c:
            X = [sb(f"l3_x{k}", [EP, 2 * GT, D], c=c) for k in range(R)]
            C = [sb(f"l3_c{k}", [EP, 2 * GT, D], c=c) for k in range(2)]
            HT = [sb(f"l3_ht{k}", [D + 1, 3, GE], c=c) for k in range(2)]
            EA = [sb(f"l3_ea{k}", [EP, GT, D], c=c) for k in range(R)]
            QE = sb("l3_qe", [EP, 2, GT, D], c=c)
            KQ = sb("l3_kq", [EP, GT, D], c=c)
            SC = sb("l3_sc", [EP, 2, GT, HEADS], c=c)
            M = [sb(f"l3_m{k}", [EP, GT, WU], c=c) for k in range(2)]
            S = [sb(f"l3_same{k}", [EP, GT, EP], c=c) for k in range(R)]
            ROW = [sb(f"l3_row{k}", [EP, GE], I32, c) for k in range(R)]
            idx = [sb(f"l3_idx{k}", [EP, 2, GT], I32, c) for k in range(R)]
            norm = [Norm(f"l3{k}", c, EP, 2 * GT) for k in range(2)]
            pT = pb("l3_pt", [D, 3, 512], c)
            pKQEV = pb("l3_pk", [EP, 4, 512], c)
            pU = pb("l3_pu", [EP, 512], c)
            s_one, s_vs = sem("l3_ones"), sem("l3_steps")
            s_row, s_ea, s_gat, s_keep = ring_sems("l3_row_loaded"), ring_sems("l3_attr_loaded"), ring_sems("l3_gathered"), ring_sems("l3_kept")
            s_staged, s_same, s_c, s_sc, s_m, s_x, s_v = (sem(f"l3_{n}") for n in ("staged", "same_ready", "normed", "scores_ready", "messages_ready", "x_used", "values_made"))
            s_t, s_at, s_h, s_ah, s_p, s_qe, s_ex, s_u, s_uc = (sem(f"l3_{n}") for n in ("turned", "attr_turned", "h_ready", "attr_copied", "projected", "qe_copied", "exp_ready", "summed", "sums_kept"))
            ea_groups = A["edge_attr_96"].rearrange("(g u p) k -> p g u k", u=GT, p=EP)

            with nc.Block() as block:
                @block.sync
                def _(sp):
                    def step(at):
                        if is_item(at, GR):
                            free(sp, s_same, at, R)
                            sp_seen(sp)
                            sp.dma_start(ROW[at.slot][:, :], edge_row(A["dst"], at.n)).then_inc(s_row[at.slot], 16)
                            free(sp, s_at, at, R)
                            sp_seen(sp)
                            sp.dma_start(EA[at.slot][:, :, :], one_group(ea_groups, at.n)).then_inc(s_ea[at.slot], 16)
                        o = at.back(2)
                        if is_item(o, GR):
                            landed(sp, s_gat, o, 32 * GT)
                            sp_seen(sp)
                            sp.dma_start(one_group(keep_groups, o.n), X[o.slot][:, GT:2 * GT, :]).then_inc(s_keep[o.slot], 16)
                        o = at.back(3)
                        if is_item(o, GR):
                            landed(sp, s_keep, o)
                            sp_seen(sp)
                            ready(sp, s_c, o)
                            sp_seen(sp)
                            sp.sem_inc(s_x, 1)
                    pipeline(sp, GR, 3, step)

                @block.gpsimd
                def _(pool):
                    gather_both(pool, X, out, idx, s_staged, s_x, s_gat)

                @block.scalar
                def _(act):
                    def step(at):
                        o = at.back(1)
                        if is_item(o, GR):
                            ready(act, s_t, o)
                            free(act, s_v, o, 2)
                            act.activation(HT[o.pair()][0:D, 0:2, :], pT[:, 0:2, 0:GE], ACT.Relu).then_inc(s_h, 1)
                            ready(act, s_at, o)
                            act.activation(HT[o.pair()][0:D, 2, :], pT[:, 2, 0:GE], ACT.Copy).then_inc(s_ah, 1)
                        if is_item(at, GR):
                            norm[at.pair()].root(act, half_count(at), EP, 2 * GT)
                        o = at.back(3)
                        if is_item(o, GR):
                            ready(act, s_u, o)
                            act.activation(U[:, bass.ds(GT * o.n, GT), :], by_tile(pU, WU), ACT.Copy).then_inc(s_uc, 1)
                        o = at.back(2)
                        if is_item(o, GR):
                            ready(act, s_p, o)
                            free(act, s_sc, o, 1)
                            act.activation(QE[:, :, :, :].rearrange("p a u d -> p a (u d)"), pKQEV[:, 1:3, 0:GT * D], ACT.Copy).then_inc(s_qe, 1)
                            ready(act, s_sc, o)
                            free(act, s_u, o, 2)
                            act.activation(M[o.pair()][:, :, D:WU], SC[:, 0, :, :], ACT.Exp).then_inc(s_ex, 1)
                    pipeline(act, GR, 3, step)

                @block.tensor
                def _(pe):
                    pe.wait_ge(s_one, 2)

                    def step(at):
                        o = at.back(1)
                        if is_item(o, GR):
                            ready(pe, s_c, o)
                            free(pe, s_h, o, 1)
                            for h in range(2):
                                for u in range(GT):
                                    last = pe.transpose(pT[:, h, u * EP:(u + 1) * EP], C[o.pair()][:, h * GT + u, :], ident[0:EP, 0:EP])
                            last.then_inc(s_t, 1)
                            landed(pe, s_ea, o)
                            free(pe, s_ah, o, 1)
                            for u in range(GT):
                                last = pe.transpose(pT[:, 2, u * EP:(u + 1) * EP], EA[o.slot][:, u, :], ident[0:EP, 0:EP])
                            last.then_inc(s_at, 1)
                        o = at.back(2)
                        if is_item(o, GR):
                            H = HT[o.pair()]
                            ready(pe, s_h, o)
                            ready(pe, s_ah, o)
                            free(pe, s_sc, o, 1)
                            for u in range(GT):
                                cols_u = slice(u * EP, (u + 1) * EP)
                                to = slice(u * D, (u + 1) * D)
                                pe.matmul(pKQEV[:, 0, to], H[:, 0, cols_u], WkV[:, 0:D], start=True, stop=True)
                                pe.matmul(pKQEV[:, 1, to], H[:, 1, cols_u], Wq[:, :], start=True, stop=True)
                                last = pe.matmul(pKQEV[:, 2, to], H[:, 2, cols_u], We[:, :], start=True, stop=True)
                            last.then_inc(s_p, 1)
                        o = at.back(3)
                        if is_item(o, GR):
                            ready(pe, s_m, o)
                            ready(pe, s_same, o)
                            free(pe, s_uc, o, 1)
                            for u in range(GT):
                                last = pe.matmul(pU[:, u * WU:(u + 1) * WU], S[o.slot][:, u, :], M[o.pair()][:, u, :], start=True, stop=True)
                            last.then_inc(s_u, 1)
                        o = at.back(2)
                        if is_item(o, GR):
                            free(pe, s_m, o, 1)
                            for u in range(GT):
                                last = pe.matmul(pKQEV[:, 3, u * D:(u + 1) * D], HT[o.pair()][:, 0, u * EP:(u + 1) * EP], WkV[:, D:2 * D], start=True, stop=True)
                            last.then_inc(s_v, 1)
                    pipeline(pe, GR, 3, step)

                @block.vector
                def _(v):
                    me = Steps(v, s_vs)
                    for k in range(2):
                        v.memset(HT[k][D:D + 1, :, :], 1.0).then_inc(s_one, 1)
                    for n in range(AHEAD):
                        stage_both(v, idx, At(0, n), s_staged)

                    def bank(j):
                        return by_tile(pKQEV[:, j, :])

                    def step(at):
                        o = at.back(3)
                        if is_item(o, GR):
                            ready(v, s_ex, o)
                            ready(v, s_v, o)
                            Mo = M[o.pair()]
                            by_head = lambda x: x.rearrange("p u (h d) -> p u h d", d=HD)
                            v.tensor_tensor(by_head(Mo[:, :, 0:D]), by_head(bank(3)),
                                            Mo[:, :, D:WU].rearrange("p u (h a) -> p u h a", a=1).to_broadcast([EP, GT, HEADS, HD]), ALU.mult).then_inc(s_m, 1)
                        if is_item(at, GR):
                            stage_both(v, idx, at.back(-AHEAD), s_staged)
                            landed(v, s_row, at)
                            free(v, s_u, at, R)
                            same_target(v, S[at.slot], ROW[at.slot], at.n).then_inc(s_same, 1)
                            landed(v, s_gat, at, 32 * GT)
                            norm[at.pair()].stats(v, me, X[at.slot], EP, 2 * GT)
                            norm[at.pair()].invert(v, me, half_count(at), EP, 2 * GT)
                            free(v, s_t, at, 2)
                            norm[at.pair()].apply(v, me, X[at.slot], C[at.pair()], EP, 2 * GT).then_inc(s_c, 1)
                            ready(v, s_c, at)
                        o = at.back(2)
                        if is_item(o, GR):
                            ready(v, s_qe, o)
                            me.done(v.tensor_tensor(KQ[:, :, :], bank(0), QE[:, 0, :, :], ALU.mult))
                            me.settle()
                            me.done(v.tensor_tensor(KQ[:, :, :], KQ[:, :, :], QE[:, 1, :, :], ALU.mult))
                            me.settle()
                            me.done(v.tensor_reduce(SC[:, 1, :, :].rearrange("p u h -> p (u h)"), KQ[:, :, :].rearrange("p u (h d) -> p (u h) d", d=HD),
                                                    mybir.AxisListType.X, ALU.add))
                            me.settle()
                            me.done(v.tensor_scalar(SC[:, 1, :, :], SC[:, 1, :, :], SCORE, 5.0, ALU.mult, ALU.min))
                            me.settle()
                            v.tensor_scalar(SC[:, 0, :, :], SC[:, 1, :, :], -5.0, None, ALU.max).then_inc(s_sc, 1)
                    pipeline(v, GR, 3, step, me)

        carry_block(U, WU, "l3")

        with ExitStack() as c:
            tot = Totals("l3b", c, WU)
            T = [sb(f"l3b_t{k}", [EP, GT, WU], c=c) for k in range(2)]
            Z = [sb(f"l3b_z{k}", [EP, 2, GT, HEADS], c=c) for k in range(2)]
            KP = [sb(f"l3b_keep{k}", [EP, GT, D], c=c) for k in range(R)]
            O = [sb(f"l3b_o{k}", [EP, GT, D], c=c) for k in range(R)]
            idx = [sb(f"l3b_idx{k}", [EP, GT], I32, c) for k in range(R)]
            s_vs, s_kp, s_put, s_o = sem("l3b_steps"), ring_sems("l3b_keep_loaded"), ring_sems("l3b_stored"), sem("l3b_out_ready")
            with nc.Block() as block:
                @block.sync
                def _(sp):
                    load_kept(sp, KP, s_o, s_kp)

                @block.gpsimd
                def _(pool):
                    send(pool, out, O, idx, s_o, s_put, pool.to_reg(N - 1))

                @block.tensor
                def _(pe):
                    def step(at):
                        if is_item(at, GR):
                            tot.place(pe, at)
                    pipeline(pe, GR, 0, step)

                @block.vector
                def _(v):
                    me = Steps(v, s_vs)
                    by_head = lambda x: x.rearrange("p u (h d) -> p u h d", d=HD)

                    def step(at):
                        if is_item(at, GR):
                            tot.pick_first(v, at)
                        o = at.back(1)
                        if is_item(o, GR):
                            k = o.pair()
                            tot.add(v, o, U, T[k][:, :, :])
                            left(v, s_put, o, 16 * GT)
                            v.tensor_copy(idx[o.slot][:, :], end_i[:, bass.ds(GT * o.n, GT)])
                            ready(v, tot.s_used, o)
                            me.done(v.tensor_scalar(Z[k][:, 0, :, :], T[k][:, :, D:WU], Z_EPS, None, ALU.add))
                            me.settle()
                            me.done(v.reciprocal(Z[k][:, 1, :, :], Z[k][:, 0, :, :]))
                            me.settle()
                            me.done(v.tensor_tensor(by_head(O[o.slot][:, :, :]), by_head(T[k][:, :, 0:D]),
                                                    Z[k][:, 1, :, :].rearrange("p u (h a) -> p u h a", a=1).to_broadcast([EP, GT, HEADS, HD]), ALU.mult))
                            me.settle()
                            landed(v, s_kp, o)
                            v.tensor_tensor(O[o.slot][:, :, :], O[o.slot][:, :, :], KP[o.slot][:, :, :], ALU.add).then_inc(s_o, 1)
                    pipeline(v, GR, 1, step, me)
        hi.close()


_INS = ['x', 'src', 'dst', 'edge_attr_17', 'edge_attr_4', 'edge_attr_96', 'L1_gnn_W1', 'L1_gnn_b1', 'L1_gnn_W2',
        'L1_gnn_b2', 'L1_gnn_Ws', 'L1_gnn_bs', 'L1_gnn_Wn', 'L1_gnn_bn', 'L2_gnn_W_node', 'L2_gnn_b_node',
        'L2_gnn_g_node', 'L2_gnn_beta_node', 'L2_gnn_W_edge', 'L2_gnn_b_edge', 'L2_gnn_g_edge', 'L2_gnn_beta_edge',
        'L2_gnn_W_msg', 'L2_gnn_b_msg', 'L2_gnn_g_msg', 'L2_gnn_beta_msg', 'L3_gnn_Wq', 'L3_gnn_bq', 'L3_gnn_Wk',
        'L3_gnn_bk', 'L3_gnn_We', 'L3_gnn_be', 'L3_gnn_Wv', 'L3_gnn_bv']
_OUTS = [((100000, 96), 'float32')]


def kernel(**inputs):
    import numpy as _np
    import concourse.bacc as _bacc
    from concourse import mybir as _mybir
    from concourse.bass_utils import run_bass_kernel_spmd as _run

    nc = _bacc.Bacc("TRN2", target_bir_lowering=False, num_devices=1)
    arrays, args = {}, {}
    for name in _INS:
        a = _np.ascontiguousarray(inputs[name])
        arrays[f"in_{name}_dram"] = a
        args[name] = nc.dram_tensor(f"in_{name}_dram", a.shape, _mybir.dt.from_np(a.dtype), kind="ExternalInput").ap()
    shape, dtype = _OUTS[0]
    out = nc.dram_tensor("out_0_dram", shape, _mybir.dt.from_np(_np.dtype(dtype)), kind="ExternalOutput").ap()
    build(nc, args, out)
    r = _run(nc, [arrays], core_ids=[0])
    return r.results[0]["out_0_dram"]
```
